# Optimizing a Trainium2 kernel written in Bass

```python
import numpy as np
import jax
import jax.numpy as jnp

def _softmax(x, axis=-1):
    return jax.nn.softmax(x, axis=axis)

def _gelu(x):
    return jax.nn.gelu(x, approximate=True)

def _silu(x):
    return jax.nn.silu(x)

def _sigmoid(x):
    return jax.nn.sigmoid(x)

def _layernorm(x, axis=-1, eps=1e-05):
    m = jnp.mean(x, axis=axis, keepdims=True)
    v = jnp.var(x, axis=axis, keepdims=True)
    return (x - m) / jnp.sqrt(v + eps)

def _scatter_add(tgt, idx, src, axis=0):
    return tgt.at[idx].add(src)

def _segment_sum(src, seg, n):
    return jax.ops.segment_sum(src, seg, n)
kernel_name = 'mk_adaln_d2_jaxref_r8_e361ca'

def setup_inputs(seed: int=0):
    np.random.seed(seed)
    _w = jnp.asarray

    def _L0_attn_setup():
        import jax, jax.numpy as jnp
        import numpy as np
        import math
        B, L, D = (2, 512, 128)
        H, DK, DV = (4, 32, 32)
        CHUNK = 32
        PROB_FLOOR = 0.02

        def _l2norm(x, eps=1e-06):
            return x * jax.lax.rsqrt(jnp.sum(x * x, -1, keepdims=True) + eps)

        def _silu(x):
            return x * jax.nn.sigmoid(x)

        def _short_conv(x, w):
            K = w.shape[-1]
            xp = jnp.pad(x, ((0, 0), (K - 1, 0), (0, 0)))
            y = sum((xp[:, j:j + x.shape[1], :] * w[:, j] for j in range(K)))
            return _silu(y)

        def _fir_conv(x, filt):
            b, l, h, d = x.shape
            K = filt.shape[-1]
            xf = jnp.pad(x.reshape(b, l, h * d).transpose(0, 2, 1), ((0, 0), (0, 0), (K - 1, 0)))
            w = filt.reshape(h * d, 1, K)
            y = jax.lax.conv_general_dilated(xf, w, (1,), 'VALID', dimension_numbers=('NCH', 'OIH', 'NCH'), feature_group_count=h * d)
            return y.transpose(0, 2, 1).reshape(b, l, h, d)

        def _delta_rule_chunkwise(q, k, v, beta, chunk=CHUNK):
            b, h, Lq, dk = q.shape
            dv = v.shape[-1]
            n = Lq // chunk
            q = _l2norm(q)
            k = _l2norm(k)
            v = v * beta[..., None]
            kb = k * beta[..., None]
            rs = lambda t: t.reshape(b, h, n, chunk, t.shape[-1])
            qc, kc, vc, kbc = (rs(q), rs(k), rs(v), rs(kb))
            strict_lower = jnp.tril(jnp.ones((chunk, chunk), bool), -1)
            M = jnp.where(strict_lower, jnp.einsum('bhncd,bhnmd->bhncm', kbc, kc), 0.0)
            eye = jnp.eye(chunk, dtype=q.dtype)
            T = jax.scipy.linalg.solve_triangular(eye + M, jnp.broadcast_to(eye, M.shape), lower=True, unit_diagonal=True)
            u = T @ vc
            w = T @ kbc
            incl_lower = jnp.tril(jnp.ones((chunk, chunk), bool), 0)

            def step(S, xs):
                q_i, k_i, u_i, w_i = xs
                attn = jnp.where(incl_lower, q_i @ k_i.swapaxes(-1, -2), 0.0)
                u_adj = u_i - w_i @ S
                out_i = q_i @ S + attn @ u_adj
                S = S + k_i.swapaxes(-1, -2) @ u_adj
                return (S, out_i)
            S0 = jnp.zeros((b, h, dk, dv), q.dtype)
            xs = tuple((jnp.moveaxis(t, 2, 0) for t in (qc, kc, u, w)))
            S, out = jax.lax.scan(step, S0, xs)
            out = jnp.moveaxis(out, 0, 2).reshape(b, h, Lq, dv)
            return (out, S)

        def _rmsnorm(x, w, eps=1e-05):
            return x * jax.lax.rsqrt(jnp.mean(x * x, -1, keepdims=True) + eps) * w

        def _per_head_stats(x):
            mean = jnp.mean(x, -1, keepdims=True)
            var = jnp.var(x, -1, keepdims=True)
            am = jnp.mean(jnp.abs(x), -1, keepdims=True)
            l2 = jnp.sqrt(jnp.sum(x * x, -1, keepdims=True))
            return jnp.concatenate([mean, var, am, l2], -1)

        def _forward(hidden_states, q_w, k_w, v_w, b_w, q_cw, k_cw, v_cw, fir_short_w, fir_long_w, mlp1_w, mlp1_b, mlp2_w, mlp2_b, logit_temp, conv_res_logit, norm_w, o_w):
            b, l, _ = hidden_states.shape
            q_in = _short_conv(hidden_states @ q_w.T, q_cw)
            k_in = _short_conv(hidden_states @ k_w.T, k_cw)
            v_in = _short_conv(hidden_states @ v_w.T, v_cw)
            q = q_in.reshape(b, l, H, DK)
            k = k_in.reshape(b, l, H, DK)
            v_direct = v_in.reshape(b, l, H, DV)
            beta = jnp.maximum(jax.nn.sigmoid(hidden_states @ b_w.T), 1e-06)
            delta_out, _S = _delta_rule_chunkwise(q.transpose(0, 2, 1, 3), k.transpose(0, 2, 1, 3), v_direct.transpose(0, 2, 1, 3), beta.transpose(0, 2, 1))
            delta_out = delta_out.transpose(0, 2, 1, 3)
            local_short = _fir_conv(v_direct, fir_short_w)
            local_long = _fir_conv(v_direct, fir_long_w)
            stats = jnp.concatenate([_per_head_stats(local_short), _per_head_stats(local_long), _per_head_stats(delta_out), _per_head_stats(v_direct)], -1)
            hs_exp = jnp.broadcast_to(hidden_states[:, :, None, :], (b, l, H, hidden_states.shape[-1]))
            gate_in = jnp.concatenate([hs_exp, stats], -1)
            h1 = jax.nn.gelu(gate_in @ mlp1_w.T + mlp1_b)
            logits = h1 @ mlp2_w.T + mlp2_b
            temp = jax.nn.softplus(logit_temp)
            p = jax.nn.softmax(logits / temp, -1)
            p = jnp.maximum(p, PROB_FLOOR)
            p = p / jnp.sum(p, -1, keepdims=True)
            o = p[..., 0:1] * local_short + p[..., 1:2] * local_long + p[..., 2:3] * delta_out + p[..., 3:4] * v_direct
            o = o + jax.nn.sigmoid(conv_res_logit)[None, None, :, None] * local_short
            o = _rmsnorm(o, norm_w)
            o = o.reshape(b, l, H * DV) @ o_w.T
            return o
        key = jax.random.key(seed)
        ks = jax.random.split(key, 16)
        s = 0.02
        hidden_gate = D * 2 // 2
        gate_in_dim = D + 16
        inp = {'hidden_states': jax.random.normal(ks[0], (B, L, D), jnp.float32), 'q_w': jax.random.normal(ks[1], (D, D), jnp.float32) * s, 'k_w': jax.random.normal(ks[2], (D, D), jnp.float32) * s, 'v_w': jax.random.normal(ks[3], (D, D), jnp.float32) * s, 'b_w': jax.random.normal(ks[4], (H, D), jnp.float32) * s, 'q_cw': jax.random.normal(ks[5], (D, 4), jnp.float32) * s, 'k_cw': jax.random.normal(ks[6], (D, 4), jnp.float32) * s, 'v_cw': jax.random.normal(ks[7], (D, 4), jnp.float32) * s, 'fir_short_w': jax.random.normal(ks[8], (H, DV, 5), jnp.float32) * s, 'fir_long_w': jax.random.normal(ks[9], (H, DV, 64), jnp.float32) * s, 'mlp1_w': jax.random.normal(ks[10], (hidden_gate, gate_in_dim), jnp.float32) * s, 'mlp1_b': jnp.zeros((hidden_gate,), jnp.float32), 'mlp2_w': jax.random.normal(ks[11], (4, hidden_gate), jnp.float32) * s, 'mlp2_b': jnp.array([-0.5, -0.5, 1.0, 3.0], jnp.float32), 'logit_temp': jnp.full((1,), math.log(math.expm1(0.7)), jnp.float32), 'conv_res_logit': jnp.full((H,), -2.0, jnp.float32), 'norm_w': jnp.ones((DV,), jnp.float32), 'o_w': jax.random.normal(ks[12], (D, D), jnp.float32) * s}
        return inp
    _L0_attn_in = _L0_attn_setup()

    def _L0_ffn_setup():
        import jax, jax.numpy as jnp
        import numpy as np
        E = 8
        K = 2
        D = 128
        H = 128
        B, T = (2, 128)
        key = jax.random.key(seed)
        ks = jax.random.split(key, 6)
        s = 0.02
        return {'x': jax.random.normal(ks[0], (B, T, D), dtype=jnp.float32), 'gate_w': jax.random.normal(ks[1], (E, D), dtype=jnp.float32) * s, 'lb_bias': jnp.zeros((E,), dtype=jnp.float32), 'w1': jax.random.normal(ks[2], (E, H, D), dtype=jnp.float32) * s, 'w2': jax.random.normal(ks[3], (E, D, H), dtype=jnp.float32) * s, 'cfc': jax.random.normal(ks[4], (H, D), dtype=jnp.float32) * s, 'cproj': jax.random.normal(ks[5], (D, H), dtype=jnp.float32) * s}
    _L0_ffn_in = _L0_ffn_setup()
    _L0_c = _w((lambda *s: np.random.randn(*s).astype(np.float32) * 0.05)(8, 128))
    _L0_wmod = _w((lambda *s: np.random.randn(*s).astype(np.float32) * 0.05)(128, 6 * 128) * 128 ** (-0.5))

    def _L1_attn_setup():
        import jax, jax.numpy as jnp
        import numpy as np
        D_MODEL = 128
        N_HEADS = 16
        D_HEAD = D_MODEL // N_HEADS
        BATCH = 2
        SEQ = 256

        def _evolved_attention(x, Wq, bq, Wk, bk, Wv, bv, Wo, bo, Wt, bt, Wg, bg):
            B, S, D = x.shape
            H, dh = (N_HEADS, D_HEAD)

            def heads(y):
                return y.reshape(B, S, H, dh).transpose(0, 2, 1, 3)
            q = heads(x @ Wq + bq)
            k = heads(x @ Wk + bk)
            v = heads(x @ Wv + bv)
            qn = q / jnp.maximum(jnp.linalg.norm(q, axis=-1, keepdims=True), 1e-12)
            kn = k / jnp.maximum(jnp.linalg.norm(k, axis=-1, keepdims=True), 1e-12)
            scores = jnp.einsum('bhqd,bhkd->bhqk', qn, kn)
            temp = jax.nn.sigmoid(x.mean(axis=1) @ Wt + bt) + 0.5
            scores = scores / temp[:, None, None, :]
            kk = max(1, S // 4)
            vals, idx = jax.lax.top_k(scores, kk)
            w = jax.nn.softmax(vals, axis=-1)
            rows = jnp.arange(B * H * S)[:, None]
            attn = jnp.zeros((B * H * S, S), scores.dtype).at[rows, idx.reshape(-1, kk)].set(w.reshape(-1, kk)).reshape(B, H, S, S)
            out = jnp.einsum('bhqk,bhkd->bhqd', attn, v)
            out = out.transpose(0, 2, 1, 3).reshape(B, S, D)
            out = out @ Wo + bo
            gate = jax.nn.sigmoid(x @ Wg + bg)
            return gate * out + (1.0 - gate) * x
        key = jax.random.key(seed)
        ks = jax.random.split(key, 16)
        s = 0.02
        d = D_MODEL
        return {'x': jax.random.normal(ks[0], (BATCH, SEQ, d), jnp.float32), 'Wq': jax.random.normal(ks[1], (d, d), jnp.float32) * s, 'bq': jnp.zeros((d,), jnp.float32), 'Wk': jax.random.normal(ks[2], (d, d), jnp.float32) * s, 'bk': jnp.zeros((d,), jnp.float32), 'Wv': jax.random.normal(ks[3], (d, d), jnp.float32) * s, 'bv': jnp.zeros((d,), jnp.float32), 'Wo': jax.random.normal(ks[4], (d, d), jnp.float32) * s, 'bo': jnp.zeros((d,), jnp.float32), 'Wt': jax.random.normal(ks[5], (d, 1), jnp.float32) * s, 'bt': jnp.zeros((1,), jnp.float32), 'Wg': jax.random.normal(ks[6], (d, d), jnp.float32) * s, 'bg': jnp.zeros((d,), jnp.float32)}
    _L1_attn_in = _L1_attn_setup()

    def _L1_ffn_setup():
        import jax, jax.numpy as jnp
        import numpy as np
        DIM = 128
        DEPTH = 6
        HEADS = 16
        DIM_HEAD = 64
        WINDOW = 32
        INNER = HEADS * DIM_HEAD
        DIM_INNER = int(DIM * 4 * 2 / 3)
        QK_SCALE = 8.0

        def shift_tokens(t):
            a, s = jnp.split(t, 2, -1)
            s = jnp.pad(s, ((0, 0), (1, 0), (0, 0)))[:, :-1]
            return jnp.concatenate([a, s], -1)

        def l2norm(t):
            return t / jnp.maximum(jnp.linalg.norm(t, axis=-1, keepdims=True), 1e-12)

        def rotate_half(x):
            x1, x2 = jnp.split(x, 2, -1)
            return jnp.concatenate([-x2, x1], -1)

        def rotary_tables(n):
            half = jnp.arange(0, DIM_HEAD, 2, dtype=jnp.float32)
            inv_freq = 1.0 / 10000.0 ** (half / DIM_HEAD)
            t = jnp.arange(n, dtype=jnp.float32)
            freqs = t[:, None] * inv_freq[None, :]
            freqs = jnp.concatenate([freqs, freqs], -1)
            base_scale = (half + 0.4 * DIM_HEAD) / (1.4 * DIM_HEAD)
            power = (t - n // 2) / (WINDOW // 2)
            scale = base_scale[None, :] ** power[:, None]
            scale = jnp.concatenate([scale, scale], -1)
            return (freqs, scale)

        def local_attention(q, k, v):
            b, h, n, d = q.shape
            w = WINDOW
            nw = n // w
            bq = q.reshape(b, h, nw, w, d)
            bk = k.reshape(b, h, nw, w, d)
            bv = v.reshape(b, h, nw, w, d)

            def look(t):
                p = jnp.pad(t, ((0, 0), (0, 0), (1, 0), (0, 0), (0, 0)))
                return jnp.concatenate([p[:, :, :nw], p[:, :, 1:]], axis=3)
            bk2, bv2 = (look(bk), look(bv))
            seq = jnp.arange(n).reshape(nw, w)
            seq_p = jnp.pad(seq, ((1, 0), (0, 0)), constant_values=-1)
            jt = jnp.concatenate([seq_p[:nw], seq_p[1:]], axis=1)
            it = seq[:, :, None]
            jb = jt[:, None, :]
            mask = (it < jb) | (it > jb + w) | (jb == -1)
            sim = jnp.einsum('bhwie,bhwje->bhwij', bq, bk2) * QK_SCALE
            sim = jnp.where(mask, -jnp.finfo(sim.dtype).max, sim)
            attn = jax.nn.softmax(sim, -1)
            out = jnp.einsum('bhwij,bhwje->bhwie', attn, bv2)
            return out.reshape(b, h, n, d)

        def attn_layer(x, Wqkv, qs, ksc, Wo):
            b, n, _ = x.shape
            qkv = x @ Wqkv
            q, k, v = jnp.split(qkv, 3, -1)
            sh = lambda t: t.reshape(b, n, HEADS, DIM_HEAD).transpose(0, 2, 1, 3)
            q, k, v = (sh(q), sh(k), sh(v))
            q = l2norm(q) * qs
            k = l2norm(k) * ksc
            freqs, scale = rotary_tables(n)
            cos, sin = (jnp.cos(freqs), jnp.sin(freqs))
            q = q * cos * scale + rotate_half(q) * sin * scale
            inv = 1.0 / scale
            k = k * cos * inv + rotate_half(k) * sin * inv
            out = local_attention(q, k, v)
            out = out.transpose(0, 2, 1, 3).reshape(b, n, INNER)
            return out @ Wo

        def ffn_layer(x, g, bln, W1, b1, W2, b2):
            mu = x.mean(-1, keepdims=True)
            var = ((x - mu) ** 2).mean(-1, keepdims=True)
            xn = (x - mu) / jnp.sqrt(var + 1e-05) * g + bln
            hg = xn @ W1 + b1
            a, gate = jnp.split(hg, 2, -1)
            return a * jax.nn.gelu(gate, approximate=False) @ W2 + b2
        key = jax.random.key(seed)
        ks = jax.random.split(key, 8)
        B, N = (2, 256)
        init = lambda k, shape: jax.random.normal(k, shape, jnp.float32) * 0.02
        return {'x': jax.random.normal(ks[0], (B, N, DIM), jnp.float32), 'Wqkv': init(ks[1], (DEPTH, DIM, 3 * INNER)), 'q_scale': jnp.ones((DEPTH, DIM_HEAD), jnp.float32), 'k_scale': jnp.ones((DEPTH, DIM_HEAD), jnp.float32), 'Wo': init(ks[2], (DEPTH, INNER, DIM)), 'ln_g': jnp.ones((DEPTH, DIM), jnp.float32), 'ln_b': jnp.zeros((DEPTH, DIM), jnp.float32), 'W1': init(ks[3], (DEPTH, DIM, 2 * DIM_INNER)), 'b1': jnp.zeros((DEPTH, 2 * DIM_INNER), jnp.float32), 'W2': init(ks[4], (DEPTH, DIM_INNER, DIM)), 'b2': jnp.zeros((DEPTH, DIM), jnp.float32)}
    _L1_ffn_in = _L1_ffn_setup()
    _L1_c = _w((lambda *s: np.random.randn(*s).astype(np.float32) * 0.05)(8, 128))
    _L1_wmod = _w((lambda *s: np.random.randn(*s).astype(np.float32) * 0.05)(128, 6 * 128) * 128 ** (-0.5))
    _d = {'L0_attn_hidden_states': _L0_attn_in['hidden_states'], 'L0_attn_q_w': _L0_attn_in['q_w'], 'L0_attn_k_w': _L0_attn_in['k_w'], 'L0_attn_v_w': _L0_attn_in['v_w'], 'L0_attn_b_w': _L0_attn_in['b_w'], 'L0_attn_q_cw': _L0_attn_in['q_cw'], 'L0_attn_k_cw': _L0_attn_in['k_cw'], 'L0_attn_v_cw': _L0_attn_in['v_cw'], 'L0_attn_fir_short_w': _L0_attn_in['fir_short_w'], 'L0_attn_fir_long_w': _L0_attn_in['fir_long_w'], 'L0_attn_mlp1_w': _L0_attn_in['mlp1_w'], 'L0_attn_mlp1_b': _L0_attn_in['mlp1_b'], 'L0_attn_mlp2_w': _L0_attn_in['mlp2_w'], 'L0_attn_mlp2_b': _L0_attn_in['mlp2_b'], 'L0_attn_logit_temp': _L0_attn_in['logit_temp'], 'L0_attn_conv_res_logit': _L0_attn_in['conv_res_logit'], 'L0_attn_norm_w': _L0_attn_in['norm_w'], 'L0_attn_o_w': _L0_attn_in['o_w'], 'L0_ffn_gate_w': _L0_ffn_in['gate_w'], 'L0_ffn_lb_bias': _L0_ffn_in['lb_bias'], 'L0_ffn_w1': _L0_ffn_in['w1'], 'L0_ffn_w2': _L0_ffn_in['w2'], 'L0_ffn_cfc': _L0_ffn_in['cfc'], 'L0_ffn_cproj': _L0_ffn_in['cproj'], 'L0_c': _L0_c, 'L0_wmod': _L0_wmod, 'L1_attn_Wq': _L1_attn_in['Wq'], 'L1_attn_bq': _L1_attn_in['bq'], 'L1_attn_Wk': _L1_attn_in['Wk'], 'L1_attn_bk': _L1_attn_in['bk'], 'L1_attn_Wv': _L1_attn_in['Wv'], 'L1_attn_bv': _L1_attn_in['bv'], 'L1_attn_Wo': _L1_attn_in['Wo'], 'L1_attn_bo': _L1_attn_in['bo'], 'L1_attn_Wt': _L1_attn_in['Wt'], 'L1_attn_bt': _L1_attn_in['bt'], 'L1_attn_Wg': _L1_attn_in['Wg'], 'L1_attn_bg': _L1_attn_in['bg'], 'L1_ffn_Wqkv': _L1_ffn_in['Wqkv'], 'L1_ffn_q_scale': _L1_ffn_in['q_scale'], 'L1_ffn_k_scale': _L1_ffn_in['k_scale'], 'L1_ffn_Wo': _L1_ffn_in['Wo'], 'L1_ffn_ln_g': _L1_ffn_in['ln_g'], 'L1_ffn_ln_b': _L1_ffn_in['ln_b'], 'L1_ffn_W1': _L1_ffn_in['W1'], 'L1_ffn_b1': _L1_ffn_in['b1'], 'L1_ffn_W2': _L1_ffn_in['W2'], 'L1_ffn_b2': _L1_ffn_in['b2'], 'L1_c': _L1_c, 'L1_wmod': _L1_wmod}
    _x0 = _d['L0_attn_hidden_states']
    _d['L0_attn_hidden_states'] = jax.random.normal(jax.random.fold_in(jax.random.key(seed), 1), (8, 512, 128), dtype=_x0.dtype)
    del _x0
    return _d

def reference(L0_attn_hidden_states, L0_attn_q_w, L0_attn_k_w, L0_attn_v_w, L0_attn_b_w, L0_attn_q_cw, L0_attn_k_cw, L0_attn_v_cw, L0_attn_fir_short_w, L0_attn_fir_long_w, L0_attn_mlp1_w, L0_attn_mlp1_b, L0_attn_mlp2_w, L0_attn_mlp2_b, L0_attn_logit_temp, L0_attn_conv_res_logit, L0_attn_norm_w, L0_attn_o_w, L0_ffn_gate_w, L0_ffn_lb_bias, L0_ffn_w1, L0_ffn_w2, L0_ffn_cfc, L0_ffn_cproj, L0_c, L0_wmod, L1_attn_Wq, L1_attn_bq, L1_attn_Wk, L1_attn_bk, L1_attn_Wv, L1_attn_bv, L1_attn_Wo, L1_attn_bo, L1_attn_Wt, L1_attn_bt, L1_attn_Wg, L1_attn_bg, L1_ffn_Wqkv, L1_ffn_q_scale, L1_ffn_k_scale, L1_ffn_Wo, L1_ffn_ln_g, L1_ffn_ln_b, L1_ffn_W1, L1_ffn_b1, L1_ffn_W2, L1_ffn_b2, L1_c, L1_wmod):

    def _L0_attn_ref(hidden_states, q_w, k_w, v_w, b_w, q_cw, k_cw, v_cw, fir_short_w, fir_long_w, mlp1_w, mlp1_b, mlp2_w, mlp2_b, logit_temp, conv_res_logit, norm_w, o_w):
        import jax, jax.numpy as jnp
        import numpy as np
        import math
        B, L, D = (2, 512, 128)
        H, DK, DV = (4, 32, 32)
        CHUNK = 32
        PROB_FLOOR = 0.02

        def _l2norm(x, eps=1e-06):
            return x * jax.lax.rsqrt(jnp.sum(x * x, -1, keepdims=True) + eps)

        def _silu(x):
            return x * jax.nn.sigmoid(x)

        def _short_conv(x, w):
            K = w.shape[-1]
            xp = jnp.pad(x, ((0, 0), (K - 1, 0), (0, 0)))
            y = sum((xp[:, j:j + x.shape[1], :] * w[:, j] for j in range(K)))
            return _silu(y)

        def _fir_conv(x, filt):
            b, l, h, d = x.shape
            K = filt.shape[-1]
            xf = jnp.pad(x.reshape(b, l, h * d).transpose(0, 2, 1), ((0, 0), (0, 0), (K - 1, 0)))
            w = filt.reshape(h * d, 1, K)
            y = jax.lax.conv_general_dilated(xf, w, (1,), 'VALID', dimension_numbers=('NCH', 'OIH', 'NCH'), feature_group_count=h * d)
            return y.transpose(0, 2, 1).reshape(b, l, h, d)

        def _delta_rule_chunkwise(q, k, v, beta, chunk=CHUNK):
            b, h, Lq, dk = q.shape
            dv = v.shape[-1]
            n = Lq // chunk
            q = _l2norm(q)
            k = _l2norm(k)
            v = v * beta[..., None]
            kb = k * beta[..., None]
            rs = lambda t: t.reshape(b, h, n, chunk, t.shape[-1])
            qc, kc, vc, kbc = (rs(q), rs(k), rs(v), rs(kb))
            strict_lower = jnp.tril(jnp.ones((chunk, chunk), bool), -1)
            M = jnp.where(strict_lower, jnp.einsum('bhncd,bhnmd->bhncm', kbc, kc), 0.0)
            eye = jnp.eye(chunk, dtype=q.dtype)
            T = jax.scipy.linalg.solve_triangular(eye + M, jnp.broadcast_to(eye, M.shape), lower=True, unit_diagonal=True)
            u = T @ vc
            w = T @ kbc
            incl_lower = jnp.tril(jnp.ones((chunk, chunk), bool), 0)

            def step(S, xs):
                q_i, k_i, u_i, w_i = xs
                attn = jnp.where(incl_lower, q_i @ k_i.swapaxes(-1, -2), 0.0)
                u_adj = u_i - w_i @ S
                out_i = q_i @ S + attn @ u_adj
                S = S + k_i.swapaxes(-1, -2) @ u_adj
                return (S, out_i)
            S0 = jnp.zeros((b, h, dk, dv), q.dtype)
            xs = tuple((jnp.moveaxis(t, 2, 0) for t in (qc, kc, u, w)))
            S, out = jax.lax.scan(step, S0, xs)
            out = jnp.moveaxis(out, 0, 2).reshape(b, h, Lq, dv)
            return (out, S)

        def _rmsnorm(x, w, eps=1e-05):
            return x * jax.lax.rsqrt(jnp.mean(x * x, -1, keepdims=True) + eps) * w

        def _per_head_stats(x):
            mean = jnp.mean(x, -1, keepdims=True)
            var = jnp.var(x, -1, keepdims=True)
            am = jnp.mean(jnp.abs(x), -1, keepdims=True)
            l2 = jnp.sqrt(jnp.sum(x * x, -1, keepdims=True))
            return jnp.concatenate([mean, var, am, l2], -1)

        def _forward(hidden_states, q_w, k_w, v_w, b_w, q_cw, k_cw, v_cw, fir_short_w, fir_long_w, mlp1_w, mlp1_b, mlp2_w, mlp2_b, logit_temp, conv_res_logit, norm_w, o_w):
            b, l, _ = hidden_states.shape
            q_in = _short_conv(hidden_states @ q_w.T, q_cw)
            k_in = _short_conv(hidden_states @ k_w.T, k_cw)
            v_in = _short_conv(hidden_states @ v_w.T, v_cw)
            q = q_in.reshape(b, l, H, DK)
            k = k_in.reshape(b, l, H, DK)
            v_direct = v_in.reshape(b, l, H, DV)
            beta = jnp.maximum(jax.nn.sigmoid(hidden_states @ b_w.T), 1e-06)
            delta_out, _S = _delta_rule_chunkwise(q.transpose(0, 2, 1, 3), k.transpose(0, 2, 1, 3), v_direct.transpose(0, 2, 1, 3), beta.transpose(0, 2, 1))
            delta_out = delta_out.transpose(0, 2, 1, 3)
            local_short = _fir_conv(v_direct, fir_short_w)
            local_long = _fir_conv(v_direct, fir_long_w)
            stats = jnp.concatenate([_per_head_stats(local_short), _per_head_stats(local_long), _per_head_stats(delta_out), _per_head_stats(v_direct)], -1)
            hs_exp = jnp.broadcast_to(hidden_states[:, :, None, :], (b, l, H, hidden_states.shape[-1]))
            gate_in = jnp.concatenate([hs_exp, stats], -1)
            h1 = jax.nn.gelu(gate_in @ mlp1_w.T + mlp1_b)
            logits = h1 @ mlp2_w.T + mlp2_b
            temp = jax.nn.softplus(logit_temp)
            p = jax.nn.softmax(logits / temp, -1)
            p = jnp.maximum(p, PROB_FLOOR)
            p = p / jnp.sum(p, -1, keepdims=True)
            o = p[..., 0:1] * local_short + p[..., 1:2] * local_long + p[..., 2:3] * delta_out + p[..., 3:4] * v_direct
            o = o + jax.nn.sigmoid(conv_res_logit)[None, None, :, None] * local_short
            o = _rmsnorm(o, norm_w)
            o = o.reshape(b, l, H * DV) @ o_w.T
            return o
        return _forward(hidden_states, q_w, k_w, v_w, b_w, q_cw, k_cw, v_cw, fir_short_w, fir_long_w, mlp1_w, mlp1_b, mlp2_w, mlp2_b, logit_temp, conv_res_logit, norm_w, o_w)

    def _L0_ffn_ref(x, gate_w, lb_bias, w1, w2, cfc, cproj):
        import jax, jax.numpy as jnp
        import numpy as np
        E = 8
        K = 2
        D = 128
        H = 128
        B, T = (2, 128)
        Bx, Tx, Dx = x.shape
        logits = jnp.einsum('btd,ed->bte', x, gate_w)
        _, idx = jax.lax.top_k(logits + lb_bias, K)
        sel_logits = jnp.take_along_axis(logits, idx, axis=-1)
        w = jax.nn.sigmoid(sel_logits)
        w = w / (jnp.sum(w, axis=-1, keepdims=True) + 1e-06)
        xf = x.reshape(-1, Dx)
        idxf = idx.reshape(-1, K)
        wf = w.reshape(-1, K)
        onehot = jax.nn.one_hot(idxf, E, dtype=wf.dtype)
        we = jnp.einsum('nke,nk->ne', onehot, wf)
        hidden = jnp.square(jax.nn.relu(jnp.einsum('nd,ehd->neh', xf, w1)))
        expert_out = jnp.einsum('neh,edh->ned', hidden, w2)
        moe_out = jnp.einsum('ned,ne->nd', expert_out, we).reshape(Bx, Tx, Dx)
        sh = jnp.square(jax.nn.relu(jnp.einsum('btd,hd->bth', x, cfc)))
        shared = jnp.einsum('bth,dh->btd', sh, cproj)
        return moe_out + shared

    def _L1_attn_ref(x, Wq, bq, Wk, bk, Wv, bv, Wo, bo, Wt, bt, Wg, bg):
        import jax, jax.numpy as jnp
        import numpy as np
        D_MODEL = 128
        N_HEADS = 16
        D_HEAD = D_MODEL // N_HEADS
        BATCH = 2
        SEQ = 256

        def _evolved_attention(x, Wq, bq, Wk, bk, Wv, bv, Wo, bo, Wt, bt, Wg, bg):
            B, S, D = x.shape
            H, dh = (N_HEADS, D_HEAD)

            def heads(y):
                return y.reshape(B, S, H, dh).transpose(0, 2, 1, 3)
            q = heads(x @ Wq + bq)
            k = heads(x @ Wk + bk)
            v = heads(x @ Wv + bv)
            qn = q / jnp.maximum(jnp.linalg.norm(q, axis=-1, keepdims=True), 1e-12)
            kn = k / jnp.maximum(jnp.linalg.norm(k, axis=-1, keepdims=True), 1e-12)
            scores = jnp.einsum('bhqd,bhkd->bhqk', qn, kn)
            temp = jax.nn.sigmoid(x.mean(axis=1) @ Wt + bt) + 0.5
            scores = scores / temp[:, None, None, :]
            kk = max(1, S // 4)
            vals, idx = jax.lax.top_k(scores, kk)
            w = jax.nn.softmax(vals, axis=-1)
            rows = jnp.arange(B * H * S)[:, None]
            attn = jnp.zeros((B * H * S, S), scores.dtype).at[rows, idx.reshape(-1, kk)].set(w.reshape(-1, kk)).reshape(B, H, S, S)
            out = jnp.einsum('bhqk,bhkd->bhqd', attn, v)
            out = out.transpose(0, 2, 1, 3).reshape(B, S, D)
            out = out @ Wo + bo
            gate = jax.nn.sigmoid(x @ Wg + bg)
            return gate * out + (1.0 - gate) * x
        return _evolved_attention(x, Wq, bq, Wk, bk, Wv, bv, Wo, bo, Wt, bt, Wg, bg)

    def _L1_ffn_ref(x, Wqkv, q_scale, k_scale, Wo, ln_g, ln_b, W1, b1, W2, b2):
        import jax, jax.numpy as jnp
        import numpy as np
        DIM = 128
        DEPTH = 6
        HEADS = 16
        DIM_HEAD = 64
        WINDOW = 32
        INNER = HEADS * DIM_HEAD
        DIM_INNER = int(DIM * 4 * 2 / 3)
        QK_SCALE = 8.0

        def shift_tokens(t):
            a, s = jnp.split(t, 2, -1)
            s = jnp.pad(s, ((0, 0), (1, 0), (0, 0)))[:, :-1]
            return jnp.concatenate([a, s], -1)

        def l2norm(t):
            return t / jnp.maximum(jnp.linalg.norm(t, axis=-1, keepdims=True), 1e-12)

        def rotate_half(x):
            x1, x2 = jnp.split(x, 2, -1)
            return jnp.concatenate([-x2, x1], -1)

        def rotary_tables(n):
            half = jnp.arange(0, DIM_HEAD, 2, dtype=jnp.float32)
            inv_freq = 1.0 / 10000.0 ** (half / DIM_HEAD)
            t = jnp.arange(n, dtype=jnp.float32)
            freqs = t[:, None] * inv_freq[None, :]
            freqs = jnp.concatenate([freqs, freqs], -1)
            base_scale = (half + 0.4 * DIM_HEAD) / (1.4 * DIM_HEAD)
            power = (t - n // 2) / (WINDOW // 2)
            scale = base_scale[None, :] ** power[:, None]
            scale = jnp.concatenate([scale, scale], -1)
            return (freqs, scale)

        def local_attention(q, k, v):
            b, h, n, d = q.shape
            w = WINDOW
            nw = n // w
            bq = q.reshape(b, h, nw, w, d)
            bk = k.reshape(b, h, nw, w, d)
            bv = v.reshape(b, h, nw, w, d)

            def look(t):
                p = jnp.pad(t, ((0, 0), (0, 0), (1, 0), (0, 0), (0, 0)))
                return jnp.concatenate([p[:, :, :nw], p[:, :, 1:]], axis=3)
            bk2, bv2 = (look(bk), look(bv))
            seq = jnp.arange(n).reshape(nw, w)
            seq_p = jnp.pad(seq, ((1, 0), (0, 0)), constant_values=-1)
            jt = jnp.concatenate([seq_p[:nw], seq_p[1:]], axis=1)
            it = seq[:, :, None]
            jb = jt[:, None, :]
            mask = (it < jb) | (it > jb + w) | (jb == -1)
            sim = jnp.einsum('bhwie,bhwje->bhwij', bq, bk2) * QK_SCALE
            sim = jnp.where(mask, -jnp.finfo(sim.dtype).max, sim)
            attn = jax.nn.softmax(sim, -1)
            out = jnp.einsum('bhwij,bhwje->bhwie', attn, bv2)
            return out.reshape(b, h, n, d)

        def attn_layer(x, Wqkv, qs, ksc, Wo):
            b, n, _ = x.shape
            qkv = x @ Wqkv
            q, k, v = jnp.split(qkv, 3, -1)
            sh = lambda t: t.reshape(b, n, HEADS, DIM_HEAD).transpose(0, 2, 1, 3)
            q, k, v = (sh(q), sh(k), sh(v))
            q = l2norm(q) * qs
            k = l2norm(k) * ksc
            freqs, scale = rotary_tables(n)
            cos, sin = (jnp.cos(freqs), jnp.sin(freqs))
            q = q * cos * scale + rotate_half(q) * sin * scale
            inv = 1.0 / scale
            k = k * cos * inv + rotate_half(k) * sin * inv
            out = local_attention(q, k, v)
            out = out.transpose(0, 2, 1, 3).reshape(b, n, INNER)
            return out @ Wo

        def ffn_layer(x, g, bln, W1, b1, W2, b2):
            mu = x.mean(-1, keepdims=True)
            var = ((x - mu) ** 2).mean(-1, keepdims=True)
            xn = (x - mu) / jnp.sqrt(var + 1e-05) * g + bln
            hg = xn @ W1 + b1
            a, gate = jnp.split(hg, 2, -1)
            return a * jax.nn.gelu(gate, approximate=False) @ W2 + b2
        for i in range(DEPTH):
            x = attn_layer(shift_tokens(x), Wqkv[i], q_scale[i], k_scale[i], Wo[i]) + x
            x = ffn_layer(shift_tokens(x), ln_g[i], ln_b[i], W1[i], b1[i], W2[i], b2[i]) + x
        return x
    x = L0_attn_hidden_states
    mod = (_silu(L0_c) @ L0_wmod).reshape(L0_c.shape[0], 6, 1, -1)
    sa, ca, ga, sb, cb, gb = (mod[:, 0], mod[:, 1], mod[:, 2], mod[:, 3], mod[:, 4], mod[:, 5])
    ga = (2 * (ga >= 0) - 1) * jnp.maximum(jnp.abs(ga), 0.25)
    gb = (2 * (gb >= 0) - 1) * jnp.maximum(jnp.abs(gb), 0.25)
    h = _layernorm(x, axis=-1) * (1 + ca) + sa
    x = x + ga * _L0_attn_ref(h, L0_attn_q_w, L0_attn_k_w, L0_attn_v_w, L0_attn_b_w, L0_attn_q_cw, L0_attn_k_cw, L0_attn_v_cw, L0_attn_fir_short_w, L0_attn_fir_long_w, L0_attn_mlp1_w, L0_attn_mlp1_b, L0_attn_mlp2_w, L0_attn_mlp2_b, L0_attn_logit_temp, L0_attn_conv_res_logit, L0_attn_norm_w, L0_attn_o_w)
    h = _layernorm(x, axis=-1) * (1 + cb) + sb
    x = x + gb * _L0_ffn_ref(h, L0_ffn_gate_w, L0_ffn_lb_bias, L0_ffn_w1, L0_ffn_w2, L0_ffn_cfc, L0_ffn_cproj)
    mod = (_silu(L1_c) @ L1_wmod).reshape(L1_c.shape[0], 6, 1, -1)
    sa, ca, ga, sb, cb, gb = (mod[:, 0], mod[:, 1], mod[:, 2], mod[:, 3], mod[:, 4], mod[:, 5])
    ga = (2 * (ga >= 0) - 1) * jnp.maximum(jnp.abs(ga), 0.25)
    gb = (2 * (gb >= 0) - 1) * jnp.maximum(jnp.abs(gb), 0.25)
    h = _layernorm(x, axis=-1) * (1 + ca) + sa
    x = x + ga * _L1_attn_ref(h, L1_attn_Wq, L1_attn_bq, L1_attn_Wk, L1_attn_bk, L1_attn_Wv, L1_attn_bv, L1_attn_Wo, L1_attn_bo, L1_attn_Wt, L1_attn_bt, L1_attn_Wg, L1_attn_bg)
    h = _layernorm(x, axis=-1) * (1 + cb) + sb
    x = x + gb * _L1_ffn_ref(h, L1_ffn_Wqkv, L1_ffn_q_scale, L1_ffn_k_scale, L1_ffn_Wo, L1_ffn_ln_g, L1_ffn_ln_b, L1_ffn_W1, L1_ffn_b1, L1_ffn_W2, L1_ffn_b2)
    return x

_drawn_inputs = setup_inputs


def setup_inputs(seed=0):
    import zlib

    import numpy as np

    out = dict(_drawn_inputs(seed))
    spreads = {'L0_attn_mlp1_b': (0.0, 0.8),
     'L0_attn_conv_res_logit': (-2.0, 0.6),
     'L0_attn_norm_w': (1.0, 0.6),
     'L0_ffn_lb_bias': (0.0, 0.8),
     'L1_attn_bq': (0.0, 2.0),
     'L1_attn_bk': (0.0, 2.0),
     'L1_attn_bv': (0.0, 0.8),
     'L1_attn_bo': (0.0, 0.675),
     'L1_attn_bg': (0.0, 0.8),
     'L1_ffn_q_scale': (1.0, 0.6),
     'L1_ffn_k_scale': (1.0, 0.6),
     'L1_ffn_ln_g': (1.0, 0.6),
     'L1_ffn_ln_b': (0.0, 0.8),
     'L1_ffn_b1': (0.0, 0.8),
     'L1_ffn_b2': (0.0, 0.654)}
    factors = {'L0_attn_q_w': 8.0,
     'L0_attn_k_w': 8.0,
     'L0_attn_b_w': 8.0,
     'L0_attn_q_cw': 8.0,
     'L0_attn_k_cw': 8.0,
     'L0_attn_fir_short_w': 8.0,
     'L0_attn_fir_long_w': 8.0,
     'L0_attn_mlp1_w': 8.0,
     'L0_attn_mlp2_w': 8.0,
     'L0_ffn_gate_w': 8.0,
     'L0_ffn_w1': 8.0,
     'L0_ffn_w2': 8.0,
     'L0_ffn_cfc': 8.0,
     'L0_ffn_cproj': 8.0,
     'L1_attn_Wq': 8.0,
     'L1_attn_Wk': 8.0,
     'L1_attn_Wv': 8.0,
     'L1_attn_Wo': 8.0,
     'L1_attn_Wt': 64.0,
     'L1_attn_Wg': 4.079,
     'L1_ffn_W1': 7.587,
     'L1_ffn_W2': 7.454}
    for name, (base, spread) in spreads.items():
        noise = np.random.default_rng([zlib.crc32(name.encode()), seed]).standard_normal(out[name].shape)
        drawn = base * np.exp(spread * noise) if base else spread * noise
        out[name] = jnp.asarray(drawn.astype(out[name].dtype))
    for name, factor in factors.items():
        out[name] = (out[name] * factor).astype(out[name].dtype)
    return out
```

```python
from contextlib import ExitStack

import concourse.bass as bass
from concourse import mybir
from concourse.alu_op_type import AluOpType as ALU

F32 = mybir.dt.float32
ACT = mybir.ActivationFunctionType
AX = mybir.AxisListType.X
ds = bass.ds

P = 128
NB = 8
T = 512
LN_EPS = 1e-5
H0, D0 = 4, 32
CH = 32
NCH = T // CH
FIR_S, FIR_L = 5, 64
PROB_FLOOR = 0.02


def semaphores(nc, ctx, names):
    return {n: ctx.enter_context(nc.semaphore(n)) for n in names.split()}


def end_of_body(nc, s):
    for h in s.values():
        nc.gpsimd.sem_clear(h)
    nc.all_engine_barrier()


def stage(nc, names, count, body):
    with ExitStack() as ctx:
        s = semaphores(nc, ctx, names)

        def once(i):
            with nc.Block() as block:
                body(block, i, s)
            end_of_body(nc, s)

        if count == 1:
            once(0)
        else:
            with nc.Fori(0, count) as i:
                once(i)


LN_SEMS = "ln_mean ln_xc ln_sq ln_var ln_log ln_rstd ln_norm ln_out "


def ln_tensor(pe, s, x, mean_w, sq, ps_mean, ps_var):
    pe.matmul(ps_mean, mean_w, x, start=True, stop=True).then_inc(s["ln_mean"], 1)
    pe.wait_ge(s["ln_sq"], 1)
    pe.matmul(ps_var, mean_w, sq, start=True, stop=True).then_inc(s["ln_var"], 1)


def ln_scalar(act, s, xc, sq, ps_var, rstd, eps):
    act.wait_ge(s["ln_xc"], 1)
    act.activation(sq, xc, ACT.Square).then_inc(s["ln_sq"], 1)
    act.wait_ge(s["ln_var"], 1)
    act.activation(rstd, ps_var, ACT.Ln, bias=eps).then_inc(s["ln_log"], 1)
    act.wait_ge(s["ln_log"], 1)
    act.activation(rstd, rstd, ACT.Exp, scale=-0.5).then_inc(s["ln_rstd"], 1)


def ln_vector(dve, s, x, xc, ps_mean, rstd, gain, shift, out):
    dve.wait_ge(s["ln_mean"], 1)
    dve.tensor_tensor(xc, x, ps_mean, ALU.subtract).then_inc(s["ln_xc"], 1)
    dve.wait_ge(s["ln_rstd"], 1)
    dve.wait_ge(s["ln_xc"], 1)
    dve.tensor_tensor(xc, xc, rstd, ALU.mult).then_inc(s["ln_norm"], 1)
    dve.wait_ge(s["ln_norm"], 1)
    dve.tensor_scalar(out, xc, gain, shift, ALU.mult, ALU.add).then_inc(s["ln_out"], 1)


def nested(nc, names, i, body):
    with ExitStack() as ctx:
        s = semaphores(nc, ctx, names)
        with nc.Block() as block:
            body(block, i, s)
        end_of_body(nc, s)


class Chain:

    def __init__(self, eng, sem):
        self.eng, self.sem, self.n = eng, sem, 0

    def __call__(self, ins):
        self.n += 1
        ins.then_inc(self.sem, 1)
        self.eng.wait_ge(self.sem, self.n)


def modulation_stage(nc, dram, consts, PS, MOD):
    with ExitStack() as ctx:
        def sb(n, shape):
            return ctx.enter_context(nc.sbuf_tensor("mod_" + n, shape, F32))
        cT = [sb(f"cT{l}", [P, NB]) for l in range(2)]
        wm = [sb(f"wm{l}", [P, 6 * P]) for l in range(2)]
        sgn = sb("sgn", [P, NB])

        def body(block, i, s):
            @block.sync
            def _(sp):
                for l in range(2):
                    sp.dma_start(cT[l][:, :], dram[f"cT{l}"]).then_inc(s["c_in"], 16)
                    sp.dma_start(wm[l][:, :], dram[f"wmod{l}"]).then_inc(s["c_in"], 16)
                for tile, src in consts:
                    sp.dma_start(tile, src).then_inc(s["const_in"], 16)
                sp.wait_ge(s["const_in"], 16 * len(consts))

            @block.scalar
            def _(act):
                act.wait_ge(s["c_in"], 64)
                for l in range(2):
                    act.activation(cT[l][:, :], cT[l][:, :], ACT.Silu).then_inc(s["c_silu"], 1)

            @block.tensor
            def _(pe):
                pe.wait_ge(s["c_silu"], 2)
                for l in range(2):
                    for j in range(6):
                        mm = pe.matmul(PS[:, l, j * NB:(j + 1) * NB], wm[l][:, j * P:(j + 1) * P],
                                       cT[l][:, :], start=True, stop=True)
                    mm.then_inc(s["mod_ps"], 1)

            @block.vector
            def _(dve):
                step = Chain(dve, s["dve_step"])
                for l in range(2):
                    dve.wait_ge(s["mod_ps"], l + 1)
                    m = MOD[l]
                    step(dve.tensor_copy(m[:, :, :].rearrange("p b j -> p j b"),
                                         PS[:, l, 0:6 * NB].rearrange("p (j b) -> p j b", j=6)))
                    for j in (1, 4):
                        step(dve.tensor_scalar(m[:, :, j], m[:, :, j], 1.0, None, ALU.add))
                    for j in (2, 5):
                        step(dve.tensor_scalar(sgn[:, :], m[:, :, j], 0.0, 2.0, ALU.is_ge, ALU.mult))
                        step(dve.tensor_scalar(sgn[:, :], sgn[:, :], 1.0, None, ALU.subtract))
                        step(dve.tensor_tensor(m[:, :, j], m[:, :, j], sgn[:, :], ALU.mult))
                        step(dve.scalar_tensor_tensor(m[:, :, j], m[:, :, j], 0.25, sgn[:, :], ALU.max, ALU.mult))

        stage(nc, "c_in const_in c_silu mod_ps dve_step", 1, body)


def delta_attention_stage(nc, dram, g, PS):
    X, MOD, eps, mean_w, ident = g.X, g.MOD0, g.eps, g.mean_w, g.ident
    with ExitStack() as ctx:
        def sb(n, shape):
            return ctx.enter_context(nc.sbuf_tensor("delta_" + n, shape, F32))
        w = {n: sb("a_" + n, [P, P]) for n in ("qwT", "kwT", "vwT", "bwT", "mlp1h", "mlp1s", "owT")}
        cw = sb("a_cw", [P, 3, 4])
        firs, firl = sb("a_firs", [P, FIR_S]), sb("a_firl", [P, FIR_L])
        mlp1b, mlp2T, mlp2b = sb("a_mlp1b", [P, 1]), sb("a_mlp2T", [P, 4]), sb("a_mlp2b", [P, 4])
        ltemp, cres, normw = sb("a_ltemp", [P, 1]), sb("a_cres", [P, 1]), sb("a_normw", [P, 1])
        itemp, tscr = sb("a_itemp", [P, 1]), sb("a_tscr", [P, 2])
        blk = sb("a_blk", [P, P])
        masks = sb("a_masks", [P, 8, CH])
        sel = sb("a_sel", [P, 4, 3, P])
        stm = sb("a_stm", [P, 3])
        psel = sb("a_psel", [16, 4, P])
        loads = [(w[n][:, :], dram[n]) for n in w] + [
            (cw[:, :, :], dram["cw"]), (firs[:, :], dram["firs"]), (firl[:, :], dram["firl"]),
            (mlp1b[:, :], dram["mlp1b"]), (mlp2T[:, :], dram["mlp2T"]), (mlp2b[:, :], dram["mlp2b"]),
            (ltemp[:, :], dram["ltemp"]), (cres[:, :], dram["cres"]), (normw[:, :], dram["normw"]),
            (blk[:, :], dram["blk32"]), (masks[:, :, :], dram["masks"]), (sel[:, :, :, :], dram["sel"]),
            (stm[:, :], dram["stm"]), (psel[:, :, :], dram["psel"])]
        xc, sq, rstd, hn = sb("xc", [P, T]), sb("sq", [P, T]), sb("rstd", [P, T]), sb("hn", [P, T])
        pad = [sb(f"pad{j}", [P, 3 + T]) for j in range(3)]
        acc = [sb(f"acc{j}", [P, T]) for j in range(3)]
        vpad = sb("vpad", [P, FIR_L - 1 + T])
        V = vpad[:, FIR_L - 1:]
        qn, kn, beta, kb, vb = (sb(n, [P, T]) for n in ("qn", "kn", "beta", "kb", "vb"))
        kR, kbR, vbR = (sb(n, [P, T]) for n in ("kR", "kbR", "vbR"))
        M, MT, LT, AT, Xi, Zi, Y = (sb(n, [P, T]) for n in ("M", "MT", "LT", "AT", "Xi", "Zi", "Y"))
        U, WT, UA, S = sb("U", [P, T]), sb("WT", [P, T]), sb("UA", [P, CH]), sb("S", [P, D0])
        SH, LO, DE = sb("SH", [P, T]), sb("LO", [P, T]), sb("DE", [P, T])
        ab, sqr = sb("ab", [P, 4, T]), sb("sqr", [P, 4, T])
        st, h1 = sb("st", [P, T]), sb("h1", [P, 4, T])
        lg, pr, r16, m16 = sb("lg", [P, 64]), sb("pr", [P, 64]), sb("r16", [P, 16]), sb("m16", [P, 16])
        pT = sb("pT", [16, T])
        o = sb("o", [P, T])
        mod = sb("mod", [P, 6])

        def c3(a):
            return a.rearrange("p (n c) -> p n c", c=CH)

        def mask(j):
            return masks[:, j:j + 1, :].broadcast_to([P, NCH, CH])

        def setup(block, i, s):
            @block.sync
            def _(sp):
                for tile, src in loads:
                    sp.dma_start(tile, src).then_inc(s["w_in"], 16)

            @block.gpsimd
            def _(pool):
                pool.memset(vpad[:, 0:FIR_L - 1], 0.0).then_inc(s["pool_done"], 1)
                for j in range(3):
                    pool.memset(pad[j][:, 0:3], 0.0).then_inc(s["pool_done"], 1)
                pool.wait_ge(s["pool_done"], 4)

            @block.scalar
            def _(act):
                act.wait_ge(s["w_in"], 16 * len(loads))
                step = Chain(act, s["act_step"])
                step(act.activation(cres[:, :], cres[:, :], ACT.Sigmoid))
                step(act.activation(tscr[:, 0:1], ltemp[:, :], ACT.Abs))
                step(act.activation(tscr[:, 0:1], tscr[:, 0:1], ACT.Exp, scale=-1.0))
                step(act.activation(tscr[:, 0:1], tscr[:, 0:1], ACT.Ln, bias=1.0))

            @block.vector
            def _(dve):
                dve.wait_ge(s["act_step"], 4)
                step = Chain(dve, s["dve_step"])
                step(dve.scalar_tensor_tensor(tscr[:, 1:2], ltemp[:, :], 0.0, tscr[:, 0:1], ALU.max, ALU.add))
                step(dve.reciprocal(itemp[:, :], tscr[:, 1:2]))

        stage(nc, "w_in pool_done act_step dve_step", 1, setup)

        def body(block, b, s):
            xb = X[:, ds(b, 1), :].rearrange("p a t -> p (a t)")

            @block.tensor
            def _(pe):
                ln_tensor(pe, s, xb, mean_w[:, :], sq[:, :], PS[:, 0, :], PS[:, 1, :])
                pe.wait_ge(s["ln_out"], 1)
                for j, n in enumerate(("qwT", "kwT", "vwT", "bwT")):
                    pe.matmul(PS[:, 2 + j, :], w[n][:, :], hn[:, :], start=True, stop=True).then_inc(s["proj"], 1)
                for j in range(2):
                    pe.wait_ge(s["qk_sq"], j + 1)
                    pe.matmul(PS[:, j, :], blk[:, :], sqr[:, j, :], start=True, stop=True).then_inc(s["qk_ss"], 1)

                def blocks(bank, a, c, done):
                    for n in range(NCH):
                        for h in range(H0):
                            r, f = slice(32 * h, 32 * h + 32), slice(CH * n, CH * n + CH)
                            mm = pe.matmul(PS[r, bank, f], a[r, f], c[r, f], start=True, stop=True,
                                           tile_position=(32 * h, 32 * h))
                    mm.then_inc(done, 1)

                pe.wait_ge(s["kb_ready"], 3)
                blocks(2, kb, kn, s["mm_M"])
                blocks(3, kn, qn, s["mm_AT"])
                for lev in range(4):
                    pe.wait_ge(s["inv_in"], lev + 1)
                    blocks(4, LT, Xi, s["mm_Y"])
                    pe.wait_ge(s["y_ready"], lev + 1)
                    if lev < 3:
                        blocks(5, Zi, Y, s["mm_XY"])
                    else:
                        blocks(5, Y, Zi, s["mm_XY"])
                pe.wait_ge(s["inv_out"], 1)
                blocks(6, Zi, vbR, s["mm_u"])
                blocks(7, kbR, Zi, s["mm_w"])
                pe.wait_ge(s["uw_ready"], 2)
                for n in range(NCH):
                    f = slice(CH * n, CH * n + CH)
                    pe.wait_ge(s["state"], n + 1)
                    for h in range(H0):
                        r = slice(32 * h, 32 * h + 32)
                        mm = pe.matmul(PS[r, 2, 0:D0], WT[r, f], S[r, :], start=True, stop=True,
                                       tile_position=(32 * h, 32 * h))
                    mm.then_inc(s["mm_ws"], 1)
                    for h in range(H0):
                        r = slice(32 * h, 32 * h + 32)
                        mm = pe.matmul(PS[r, 3, f], qn[r, f], S[r, :], start=True, stop=False,
                                       tile_position=(32 * h, 32 * h))
                    pe.wait_ge(s["ua_ready"], n + 1)
                    for h in range(H0):
                        r = slice(32 * h, 32 * h + 32)
                        mm = pe.matmul(PS[r, 4, 0:D0], kR[r, f], UA[r, :], start=True, stop=True,
                                       tile_position=(32 * h, 32 * h))
                    mm.then_inc(s["mm_ds"], 1)
                    for h in range(H0):
                        r = slice(32 * h, 32 * h + 32)
                        mm = pe.matmul(PS[r, 3, f], AT[r, f], UA[r, :], start=False, stop=True,
                                       tile_position=(32 * h, 32 * h))
                    mm.then_inc(s["mm_out"], 1)
                pe.wait_ge(s["src_ready"], 4)
                src = (SH, LO, DE, V)
                for k in range(4):
                    pe.wait_ge(s["src_abs"], k + 1)
                    pe.matmul(PS[:, 0, :], sel[:, k, 0, :], src[k][:, :], start=(k == 0), stop=False)
                    mm = pe.matmul(PS[:, 0, :], sel[:, k, 1, :], ab[:, k, :], start=False, stop=(k == 3))
                mm.then_inc(s["mm_stat"], 1)
                for k in range(4):
                    pe.wait_ge(s["src_sq"], k + 1)
                    mm = pe.matmul(PS[:, 1, :], sel[:, k, 2, :], sqr[:, k, :], start=(k == 0), stop=(k == 3))
                mm.then_inc(s["mm_stat"], 1)
                pe.wait_ge(s["stat_ready"], 1)
                for h in range(H0):
                    r = slice(32 * h, 32 * h + 32)
                    pe.matmul(PS[:, 4 + h, :], w["mlp1h"][:, :], hn[:, :], start=True, stop=False)
                    pe.matmul(PS[:, 4 + h, :], w["mlp1s"][r, :], st[r, :], start=False, stop=True,
                              tile_position=(32 * h, 0)).then_inc(s["mm_h1"], 1)
                for h in range(H0):
                    pe.wait_ge(s["h1_ready"], h + 1)
                    for t in range(4):
                        mm = pe.matmul(PS[:, 2, t * 16 + h * 4:t * 16 + h * 4 + 4],
                                       h1[:, h, t * P:(t + 1) * P], mlp2T[:, :], start=True, stop=True)
                mm.then_inc(s["mm_lg"], 1)
                pe.wait_ge(s["p_ready"], 1)
                for t in range(4):
                    mm = pe.transpose(PS[0:16, 3, t * P:(t + 1) * P], pr[:, t * 16:(t + 1) * 16], ident[:, :])
                mm.then_inc(s["mm_pT"], 1)
                pe.wait_ge(s["pT_ready"], 1)
                for k in range(4):
                    pe.matmul(PS[:, 4 + k, :], psel[:, k, :], pT[:, :], start=True, stop=True).then_inc(s["mm_P"], 1)
                pe.wait_ge(s["o_sq"], 1)
                pe.matmul(PS[:, 0, :], blk[:, :], sq[:, :], start=True, stop=True).then_inc(s["mm_oss"], 1)
                pe.wait_ge(s["o_ready"], 1)
                pe.matmul(PS[:, 1, :], w["owT"][:, :], o[:, :], start=True, stop=True).then_inc(s["mm_fin"], 1)

            @block.scalar
            def _(act):
                ln_scalar(act, s, xc[:, :], sq[:, :], PS[:, 1, :], rstd[:, :], eps[:, 0:1])
                for j in range(3):
                    act.wait_ge(s["proj"], j + 1)
                    act.activation(pad[j][:, 3:], PS[:, 2 + j, :], ACT.Copy).then_inc(s["pad_ready"], 1)
                act.wait_ge(s["proj"], 4)
                act.activation(beta[:, :], PS[:, 5, :], ACT.Sigmoid).then_inc(s["beta_raw"], 1)
                for j in range(3):
                    act.wait_ge(s["conv"], j + 1)
                    act.activation((qn[:, :], kn[:, :], V)[j], acc[j][:, :], ACT.Silu).then_inc(s["silu"], 1)
                for j in range(2):
                    act.wait_ge(s["silu"], j + 1)
                    act.activation(sqr[:, j, :], (qn, kn)[j][:, :], ACT.Square).then_inc(s["qk_sq"], 1)
                for j in range(2):
                    act.wait_ge(s["qk_ss"], j + 1)
                    act.activation(ab[:, j, :], PS[:, j, :], ACT.Ln, bias=eps[:, 1:2]).then_inc(s["rn_log"], 1)
                for j in range(2):
                    act.wait_ge(s["rn_log"], j + 1)
                    act.activation(ab[:, j, :], ab[:, j, :], ACT.Exp, scale=-0.5).then_inc(s["rn"], 1)
                act.wait_ge(s["mm_u"], 1)
                act.activation(U[:, :], PS[:, 6, :], ACT.Copy).then_inc(s["uw_ready"], 1)
                act.wait_ge(s["mm_w"], 1)
                act.activation(WT[:, :], PS[:, 7, :], ACT.Copy).then_inc(s["uw_ready"], 1)
                act.wait_ge(s["src_ready"], 4)
                for k, a in enumerate((SH[:, :], LO[:, :], DE[:, :], V)):
                    act.activation(ab[:, k, :], a, ACT.Abs).then_inc(s["src_abs"], 1)
                for k, a in enumerate((SH[:, :], LO[:, :], DE[:, :], V)):
                    act.activation(sqr[:, k, :], a, ACT.Square).then_inc(s["src_sq"], 1)
                act.wait_ge(s["mm_stat"], 2)
                act.activation(st[:, :], PS[:, 1, :], ACT.Sqrt, scale=stm[:, 2:3]).then_inc(s["stat_sqrt"], 1)
                for h in range(H0):
                    act.wait_ge(s["mm_h1"], h + 1)
                    act.activation(h1[:, h, :], PS[:, 4 + h, :], ACT.Gelu_apprx_tanh, bias=mlp1b[:, 0:1])\
                       .then_inc(s["h1_ready"], 1)
                act.wait_ge(s["lg_ready"], 1)
                act.activation(pr[:, :], lg[:, :], ACT.Exp, scale=itemp[:, 0:1]).then_inc(s["lg_exp"], 1)
                act.wait_ge(s["mm_pT"], 1)
                act.activation(pT[:, :], PS[0:16, 3, :], ACT.Copy).then_inc(s["pT_ready"], 1)
                act.wait_ge(s["o_mix"], 1)
                act.activation(sq[:, :], o[:, :], ACT.Square).then_inc(s["o_sq"], 1)
                act.wait_ge(s["mm_oss"], 1)
                act.activation(rstd[:, :], PS[:, 0, :], ACT.Ln, bias=eps[:, 0:1], scale=1.0 / D0).then_inc(s["o_log"], 1)
                act.wait_ge(s["o_log"], 1)
                act.activation(rstd[:, :], rstd[:, :], ACT.Exp, scale=-0.5).then_inc(s["o_rstd"], 1)

            @block.vector
            def _(dve):
                step = Chain(dve, s["dve_step"])
                step(dve.tensor_copy(mod[:, :], MOD[:, ds(b, 1), :].rearrange("p a j -> p (a j)")))
                ln_vector(dve, s, xb, xc[:, :], PS[:, 0, :], rstd[:, :], mod[:, 1:2], mod[:, 0:1], hn[:, :])
                for j in range(3):
                    dve.wait_ge(s["pad_ready"], j + 1)
                    step(dve.tensor_scalar(acc[j][:, :], pad[j][:, 3:3 + T], cw[:, j, 3:4], None, ALU.mult))
                    for k in range(3):
                        ins = dve.scalar_tensor_tensor(acc[j][:, :], pad[j][:, k:k + T], cw[:, j, k:k + 1],
                                                       acc[j][:, :], ALU.mult, ALU.add)
                        if k < 2:
                            step(ins)
                    ins.then_inc(s["conv"], 1)
                dve.wait_ge(s["beta_raw"], 1)
                step(dve.tensor_scalar(beta[:, :], beta[:, :], 1e-6, None, ALU.max))
                dve.wait_ge(s["silu"], 3)
                step(dve.tensor_tensor(vb[:, :], V, beta[:, :], ALU.mult))
                dve.wait_ge(s["rn"], 2)
                step(dve.tensor_tensor(kn[:, :], kn[:, :], ab[:, 1, :], ALU.mult))
                dve.tensor_tensor(qn[:, :], qn[:, :], ab[:, 0, :], ALU.mult).then_inc(s["kb_ready"], 1)
                dve.tensor_tensor(kb[:, :], kn[:, :], beta[:, :], ALU.mult).then_inc(s["kb_ready"], 1)
                dve.wait_ge(s["kb_ready"], 2)
                dve.transpose(kR[:, :], kn[:, :]).then_inc(s["kb_ready"], 1)
                step(dve.transpose(vbR[:, :], vb[:, :]))
                step(dve.transpose(kbR[:, :], kb[:, :]))
                dve.wait_ge(s["mm_M"], 1)
                step(dve.tensor_tensor(c3(M[:, :]), c3(PS[:, 2, :]), mask(0), ALU.mult))
                step(dve.transpose(MT[:, :], M[:, :]))
                dve.wait_ge(s["mm_AT"], 1)
                step(dve.tensor_tensor(c3(AT[:, :]), c3(PS[:, 3, :]), mask(1), ALU.mult))
                step(dve.tensor_tensor(c3(M[:, :]), c3(M[:, :]), mask(3), ALU.mult))
                step(dve.tensor_tensor(c3(Xi[:, :]), mask(2), c3(M[:, :]), ALU.subtract))
                for lev in range(4):
                    step(dve.transpose(Zi[:, :], Xi[:, :]))
                    dve.tensor_tensor(c3(LT[:, :]), c3(MT[:, :]), mask(4 + lev), ALU.mult).then_inc(s["inv_in"], 1)
                    dve.wait_ge(s["mm_Y"], lev + 1)
                    dve.tensor_copy(Y[:, :], PS[:, 4, :]).then_inc(s["y_ready"], 1)
                    dve.wait_ge(s["mm_XY"], lev + 1)
                    if lev < 3:
                        step(dve.tensor_tensor(Xi[:, :], Xi[:, :], PS[:, 5, :], ALU.subtract))
                    else:
                        dve.tensor_tensor(Zi[:, :], Zi[:, :], PS[:, 5, :], ALU.subtract).then_inc(s["inv_out"], 1)
                dve.memset(S[:, :], 0.0).then_inc(s["state"], 1)
                taps = [(SH, firs, FIR_S, k) for k in range(FIR_S)] + [(LO, firl, FIR_L, k) for k in range(FIR_L)]

                def tap():
                    if taps:
                        dst, f, K, k = taps.pop(0)
                        src = vpad[:, FIR_L - K + k:FIR_L - K + k + T]
                        if k == 0:
                            step(dve.tensor_scalar(dst[:, :], src, f[:, 0:1], None, ALU.mult))
                        else:
                            step(dve.scalar_tensor_tensor(dst[:, :], src, f[:, k:k + 1], dst[:, :],
                                                          ALU.mult, ALU.add))
                dve.wait_ge(s["uw_ready"], 2)
                for n in range(NCH):
                    f = slice(CH * n, CH * n + CH)
                    tap()
                    dve.wait_ge(s["mm_ws"], n + 1)
                    if n:
                        dve.wait_ge(s["mm_out"], n)
                    dve.tensor_tensor(UA[:, :], U[:, f], PS[:, 2, 0:D0], ALU.subtract).then_inc(s["ua_ready"], 1)
                    tap()
                    tap()
                    dve.wait_ge(s["mm_ds"], n + 1)
                    dve.wait_ge(s["state"], n + 1)
                    dve.tensor_tensor(S[:, :], S[:, :], PS[:, 4, 0:D0], ALU.add).then_inc(s["state"], 1)
                    tap()
                    tap()
                while taps:
                    tap()
                dve.wait_ge(s["mm_out"], NCH)
                dve.transpose(DE[:, :], PS[:, 3, :]).then_inc(s["src_ready"], 4)
                dve.wait_ge(s["mm_stat"], 2)
                step(dve.tensor_copy(o[:, :], PS[:, 0, :]))
                step(dve.scalar_tensor_tensor(sq[:, :], o[:, :], stm[:, 1:2], o[:, :], ALU.mult, ALU.mult))
                dve.wait_ge(s["stat_sqrt"], 1)
                step(dve.scalar_tensor_tensor(sq[:, :], PS[:, 1, :], stm[:, 1:2], sq[:, :], ALU.mult, ALU.subtract))
                step(dve.scalar_tensor_tensor(sq[:, :], o[:, :], stm[:, 0:1], sq[:, :], ALU.mult, ALU.add))
                dve.tensor_tensor(st[:, :], st[:, :], sq[:, :], ALU.add).then_inc(s["stat_ready"], 1)
                dve.wait_ge(s["mm_lg"], 1)

                def g4(a):
                    return a.rearrange("p (g k) -> p g k", k=4)

                def bc(a):
                    return a.rearrange("p (g k) -> p g k", k=1).broadcast_to([P, 16, 4])
                step(dve.tensor_tensor(g4(lg[:, :]), g4(PS[:, 2, 0:64]),
                                       mlp2b[:, :].rearrange("p (g k) -> p g k", g=1).broadcast_to([P, 16, 4]), ALU.add))
                step(dve.tensor_reduce(m16[:, :], g4(lg[:, :]), AX, ALU.max))
                dve.tensor_tensor(g4(lg[:, :]), g4(lg[:, :]), bc(m16[:, :]), ALU.subtract).then_inc(s["lg_ready"], 1)
                dve.wait_ge(s["lg_exp"], 1)
                step(dve.tensor_reduce(m16[:, :], g4(pr[:, :]), AX, ALU.add))
                step(dve.reciprocal(r16[:, :], m16[:, :]))
                step(dve.tensor_tensor(g4(pr[:, :]), g4(pr[:, :]), bc(r16[:, :]), ALU.mult))
                step(dve.tensor_scalar(pr[:, :], pr[:, :], PROB_FLOOR, None, ALU.max))
                step(dve.tensor_reduce(m16[:, :], g4(pr[:, :]), AX, ALU.add))
                step(dve.reciprocal(r16[:, :], m16[:, :]))
                dve.tensor_tensor(g4(pr[:, :]), g4(pr[:, :]), bc(r16[:, :]), ALU.mult).then_inc(s["p_ready"], 1)
                dve.wait_ge(s["mm_P"], 1)
                step(dve.scalar_tensor_tensor(o[:, :], PS[:, 4, :], cres[:, 0:1], SH[:, :], ALU.add, ALU.mult))
                for k, a in ((1, LO[:, :]), (2, DE[:, :]), (3, V)):
                    dve.wait_ge(s["mm_P"], k + 1)
                    step(dve.tensor_tensor(xc[:, :], a, PS[:, 4 + k, :], ALU.mult))
                    ins = dve.tensor_tensor(o[:, :], o[:, :], xc[:, :], ALU.add)
                    if k < 3:
                        step(ins)
                ins.then_inc(s["o_mix"], 1)
                dve.wait_ge(s["o_rstd"], 1)
                dve.scalar_tensor_tensor(o[:, :], o[:, :], normw[:, 0:1], rstd[:, :], ALU.mult, ALU.mult)\
                   .then_inc(s["o_ready"], 1)
                dve.wait_ge(s["mm_fin"], 1)
                dve.scalar_tensor_tensor(xb, PS[:, 1, :], mod[:, 2:3], xb, ALU.mult, ALU.add).then_inc(s["dve_step"], 1)

        stage(nc, LN_SEMS + "proj pad_ready beta_raw conv silu qk_sq qk_ss rn_log rn kb_ready mm_M mm_AT inv_in "
              "mm_Y y_ready mm_XY inv_out mm_u mm_w uw_ready state mm_ws ua_ready mm_ds mm_out src_ready src_abs "
              "src_sq mm_stat stat_sqrt stat_ready mm_h1 h1_ready mm_lg lg_ready lg_exp p_ready mm_pT pT_ready mm_P "
              "o_mix o_sq mm_oss o_log o_rstd o_ready mm_fin dve_step", NB, body)


def experts_stage(nc, dram, g, PS):
    X, MOD, eps, mean_w, ident = g.X, g.MOD0, g.eps, g.mean_w, g.ident
    NE = 8
    with ExitStack() as ctx:
        def sb(n, shape):
            return ctx.enter_context(nc.sbuf_tensor("moe_" + n, shape, F32))
        w1, w2 = sb("m_w1", [P, NE + 1, P]), sb("m_w2", [P, NE + 1, P])
        gw, lb, tri, esel = sb("m_gw", [P, NE]), sb("m_lb", [P, NE]), sb("m_tri", [P, NE, NE]), sb("m_esel", [NE, NE, P])
        xc, sq, rstd, hn = sb("xc", [P, T]), sb("sq", [P, T]), sb("rstd", [P, T]), sb("hn", [P, T])
        lgt, lgb, sg = sb("lgt", [P, 4, NE]), sb("lgb", [P, 4, NE]), sb("sg", [P, 4, NE])
        gt, eq = sb("gt", [P, 4, NE, NE]), sb("eq", [P, 4, NE, NE])
        cnt, ws, wr = sb("cnt", [P, 4, NE]), sb("ws", [P, 4]), sb("wr", [P, 4])
        weT = sb("weT", [NE, T])
        relu, act2, hid = sb("relu", [P, 2, T]), sb("act2", [P, 2, T]), sb("hid", [P, 2, T])
        mod = sb("mod", [P, 6])
        loads = [(w1[:, :, :], dram["w1"]), (w2[:, :, :], dram["w2"]), (gw[:, :], dram["gate_wT"]),
                 (lb[:, :], dram["lb_bias"]), (tri[:, :, :], dram["tri8"]), (esel[:, :, :], dram["esel"])]

        def setup(block, i, s):
            @block.sync
            def _(sp):
                for tile, src in loads:
                    sp.dma_start(tile, src).then_inc(s["w_in"], 16)
                sp.wait_ge(s["w_in"], 16 * len(loads))
        stage(nc, "w_in", 1, setup)

        def body(block, b, s):
            xb = X[:, ds(b, 1), :].rearrange("p a t -> p (a t)")

            @block.tensor
            def _(pe):
                ln_tensor(pe, s, xb, mean_w[:, :], sq[:, :], PS[:, 0, :], PS[:, 1, :])
                pe.wait_ge(s["ln_out"], 1)
                for t in range(4):
                    mm = pe.matmul(PS[:, 2, t * NE:(t + 1) * NE], hn[:, t * P:(t + 1) * P], gw[:, :],
                                   start=True, stop=True)
                mm.then_inc(s["mm_lg"], 1)

                def up(e):
                    if e >= 2:
                        pe.wait_ge(s["act_relu"], e - 1)
                    pe.matmul(PS[:, 4 + e % 2, :], w1[:, e, :], hn[:, :], start=True, stop=True).then_inc(s["mm_up"], 1)

                def spread(e):
                    if e >= 2:
                        pe.wait_ge(s["hid_ready"], e - 1)
                    pe.matmul(PS[:, 6 + e % 2, :], esel[:, e, :], weT[:, :], start=True, stop=True).then_inc(s["mm_we"], 1)

                def down(e):
                    if e < NE:
                        pe.wait_ge(s["hid_ready"], e + 1)
                    else:
                        pe.wait_ge(s["act_sq"], e + 1)
                    rhs = hid[:, e % 2, :] if e < NE else act2[:, e % 2, :]
                    pe.matmul(PS[:, 1, :], w2[:, e, :], rhs, start=(e == 0), stop=(e == NE)).then_inc(s["mm_down"], 1)
                up(0)
                up(1)
                pe.wait_ge(s["we_ready"], 1)
                for t in range(4):
                    mm = pe.transpose(PS[0:NE, 3, t * P:(t + 1) * P], cnt[:, t, :], ident[:, :])
                mm.then_inc(s["mm_weT"], 1)
                pe.wait_ge(s["weT_ready"], 1)
                spread(0)
                for e in range(NE + 1):
                    if e + 2 <= NE:
                        up(e + 2)
                    if e + 1 < NE:
                        spread(e + 1)
                    down(e)

            @block.scalar
            def _(act):
                ln_scalar(act, s, xc[:, :], sq[:, :], PS[:, 1, :], rstd[:, :], eps[:, 0:1])
                act.wait_ge(s["lg_ready"], 1)
                act.activation(sg[:, :, :], lgt[:, :, :], ACT.Sigmoid).then_inc(s["sig_ready"], 1)
                act.wait_ge(s["mm_weT"], 1)
                act.activation(weT[:, :], PS[0:NE, 3, :], ACT.Copy).then_inc(s["weT_ready"], 1)
                for e in range(NE + 1):
                    act.wait_ge(s["mm_up"], e + 1)
                    act.activation(relu[:, e % 2, :], PS[:, 4 + e % 2, :], ACT.Relu).then_inc(s["act_relu"], 1)
                    act.wait_ge(s["act_relu"], e + 1)
                    if e >= 2:
                        act.wait_ge(s["hid_ready"], e - 1)
                    act.activation(act2[:, e % 2, :], relu[:, e % 2, :], ACT.Square).then_inc(s["act_sq"], 1)

            @block.vector
            def _(dve):
                step = Chain(dve, s["dve_step"])
                step(dve.tensor_copy(mod[:, :], MOD[:, ds(b, 1), :].rearrange("p a j -> p (a j)")))
                ln_vector(dve, s, xb, xc[:, :], PS[:, 0, :], rstd[:, :], mod[:, 4:5], mod[:, 3:4], hn[:, :])
                dve.wait_ge(s["mm_lg"], 1)
                dve.tensor_copy(lgt[:, :, :], PS[:, 2, 0:4 * NE].rearrange("p (t e) -> p t e", e=NE)).then_inc(s["lg_ready"], 1)
                dve.wait_ge(s["lg_ready"], 1)
                bias = lb[:, :].rearrange("p (t e) -> p t e", t=1).broadcast_to([P, 4, NE])
                step(dve.tensor_tensor(lgb[:, :, :], lgt[:, :, :], bias, ALU.add))
                other = lgb[:, :, :].rearrange("p t (a e) -> p t a e", a=1).broadcast_to([P, 4, NE, NE])
                own = lgb[:, :, :].rearrange("p t (e a) -> p t e a", a=1).broadcast_to([P, 4, NE, NE])
                below = tri[:, :, :].rearrange("p (a e) f -> p a e f", a=1).broadcast_to([P, 4, NE, NE])
                step(dve.tensor_tensor(gt[:, :, :, :], other, own, ALU.is_gt))
                step(dve.tensor_tensor(eq[:, :, :, :], other, own, ALU.is_equal))
                step(dve.tensor_tensor(eq[:, :, :, :], eq[:, :, :, :], below, ALU.mult))
                step(dve.tensor_tensor(gt[:, :, :, :], gt[:, :, :, :], eq[:, :, :, :], ALU.add))
                step(dve.tensor_reduce(cnt[:, :, :], gt[:, :, :, :], AX, ALU.add))
                dve.wait_ge(s["sig_ready"], 1)
                step(dve.scalar_tensor_tensor(cnt[:, :, :], cnt[:, :, :], 1.5, sg[:, :, :], ALU.is_lt, ALU.mult))
                step(dve.tensor_reduce(ws[:, :], cnt[:, :, :], AX, ALU.add))
                step(dve.tensor_scalar(ws[:, :], ws[:, :], 1e-6, None, ALU.add))
                step(dve.reciprocal(wr[:, :], ws[:, :]))
                wrb = wr[:, :].rearrange("p (t a) -> p t a", a=1).broadcast_to([P, 4, NE])
                dve.tensor_tensor(cnt[:, :, :], cnt[:, :, :], wrb, ALU.mult).then_inc(s["we_ready"], 1)
                for e in range(NE):
                    dve.wait_ge(s["act_sq"], e + 1)
                    dve.wait_ge(s["mm_we"], e + 1)
                    if e >= 2:
                        dve.wait_ge(s["mm_down"], e - 1)
                    dve.tensor_tensor(hid[:, e % 2, :], act2[:, e % 2, :], PS[:, 6 + e % 2, :], ALU.mult)\
                       .then_inc(s["hid_ready"], 1)
                dve.wait_ge(s["mm_down"], NE + 1)
                dve.scalar_tensor_tensor(xb, PS[:, 1, :], mod[:, 5:6], xb, ALU.mult, ALU.add).then_inc(s["dve_step"], 1)

        stage(nc, LN_SEMS + "mm_lg mm_up mm_we mm_down mm_weT weT_ready we_ready act_relu act_sq hid_ready "
              "lg_ready sig_ready dve_step", NB, body)


H1, D1 = 16, 8
TOPK = T // 4
GONE = -1e30


def topk_attention_stage(nc, dram, g, PS):
    X, MOD, eps, mean_w, ident = g.X, g.MOD1, g.eps, g.mean_w, g.ident
    with ExitStack() as ctx:
        def sb(n, shape):
            return ctx.enter_context(nc.sbuf_tensor("topk_" + n, shape, F32))
        w = {n: sb("t_" + n, [P, P]) for n in ("Wq", "Wk", "Wv", "Wo", "Wg", "blk8", "bv")}
        col = {n: sb("t_" + n, [P, 1]) for n in ("bq", "bk", "bo", "bg", "bt", "Wt")}
        hm = sb("t_hm", [P, H1])
        loads = [(w[n][:, :], dram["t_" + n]) for n in w] + [(col[n][:, :], dram["t_" + n]) for n in col]
        loads += [(hm[:, :], dram["hm"])]
        xc, sq, rstd, hn = sb("xc", [P, T]), sb("sq", [P, T]), sb("rstd", [P, T]), sb("hn", [P, T])
        qk, qks, gate = sb("qk", [P, 2, T]), sb("qks", [P, 2, T]), sb("gate", [P, T])
        Vt, OUT, OT = sb("Vt", [P, 4, P]), sb("OUT", [P, 4, P]), sb("OT", [P, T])
        hsum, itemp = sb("hsum", [P, 1]), sb("itemp", [P, 2])
        qm, Vh = sb("qm", [P, T]), sb("Vh", [P, 4, D1])
        E, W, m8 = sb("E", [P, 4, T]), sb("W", [P, 4, T]), sb("m8", [P, 4, 8])
        psum, prec = sb("psum", [P, 4]), sb("prec", [P, 4])
        PT = sb("PT", [P, 2, T])
        mod = sb("mod", [P, 6])

        def setup(block, i, s):
            @block.sync
            def _(sp):
                for tile, src in loads:
                    sp.dma_start(tile, src).then_inc(s["w_in"], 16)
                sp.wait_ge(s["w_in"], 16 * len(loads))
        stage(nc, "w_in", 1, setup)

        def project(block, b, s):
            xb = X[:, ds(b, 1), :].rearrange("p a t -> p (a t)")

            @block.tensor
            def _(pe):
                ln_tensor(pe, s, xb, mean_w[:, :], sq[:, :], PS[:, 0, :], PS[:, 1, :])
                pe.wait_ge(s["ln_out"], 1)
                for j, n in enumerate(("Wq", "Wk", "Wg")):
                    pe.matmul(PS[:, 2 + j, :], w[n][:, :], hn[:, :], start=True, stop=True).then_inc(s["mm_proj"], 1)
                for t in range(4):
                    mm = pe.matmul(PS[:, 5, t * P:(t + 1) * P], hn[:, t * P:(t + 1) * P], w["Wv"][:, :],
                                   start=True, stop=True)
                mm.then_inc(s["mm_v"], 1)
                for j in range(2):
                    pe.wait_ge(s["qk_sq"], j + 1)
                    pe.matmul(PS[:, j, :], w["blk8"][:, :], qks[:, j, :], start=True, stop=True).then_inc(s["mm_ss"], 1)
                pe.wait_ge(s["mean_ready"], 1)
                pe.matmul(PS[:, 6, 0:1], hsum[:, 0:1].broadcast_to([P, P]), col["Wt"][:, :], start=True, stop=True)\
                  .then_inc(s["mm_temp"], 1)

            @block.scalar
            def _(act):
                ln_scalar(act, s, xc[:, :], sq[:, :], PS[:, 1, :], rstd[:, :], eps[:, 0:1])
                for j, n in enumerate(("bq", "bk")):
                    act.wait_ge(s["mm_proj"], j + 1)
                    act.activation(qk[:, j, :], PS[:, 2 + j, :], ACT.Identity, bias=col[n][:, 0:1]).then_inc(s["qk_ready"], 1)
                for j in range(2):
                    act.wait_ge(s["qk_ready"], j + 1)
                    act.activation(qks[:, j, :], qk[:, j, :], ACT.Square).then_inc(s["qk_sq"], 1)
                act.wait_ge(s["mm_proj"], 3)
                act.activation(gate[:, :], PS[:, 4, :], ACT.Sigmoid, bias=col["bg"][:, 0:1]).then_inc(s["gate_ready"], 1)
                act.wait_ge(s["mm_temp"], 1)
                act.activation(itemp[:, 0:1], PS[:, 6, 0:1], ACT.Sigmoid, bias=col["bt"][:, 0:1], scale=1.0 / T)\
                   .then_inc(s["temp_sig"], 1)
                for j in range(2):
                    act.wait_ge(s["mm_ss"], j + 1)
                    act.activation(qks[:, j, :], PS[:, j, :], ACT.Sqrt).then_inc(s["norm_ready"], 1)

            @block.vector
            def _(dve):
                step = Chain(dve, s["dve_step"])
                step(dve.tensor_copy(mod[:, :], MOD[:, ds(b, 1), :].rearrange("p a j -> p (a j)")))
                ln_vector(dve, s, xb, xc[:, :], PS[:, 0, :], rstd[:, :], mod[:, 1:2], mod[:, 0:1], hn[:, :])
                dve.wait_ge(s["ln_out"], 1)
                dve.tensor_reduce(hsum[:, :], hn[:, :], AX, ALU.add).then_inc(s["mean_ready"], 1)
                dve.wait_ge(s["mm_v"], 1)
                bv = w["bv"][:, :].rearrange("p (a c) -> p a c", a=1).broadcast_to([P, 4, P])
                step(dve.tensor_tensor(Vt[:, :, :], PS[:, 5, :].rearrange("p (t c) -> p t c", t=4), bv, ALU.add))
                dve.wait_ge(s["temp_sig"], 1)
                step(dve.tensor_scalar(itemp[:, 0:1], itemp[:, 0:1], 0.5, None, ALU.add))
                step(dve.reciprocal(itemp[:, 1:2], itemp[:, 0:1]))
                for j in range(2):
                    dve.wait_ge(s["norm_ready"], j + 1)
                    step(dve.tensor_scalar(qks[:, j, :], qks[:, j, :], 1e-12, None, ALU.max))
                    step(dve.reciprocal(qks[:, j, :], qks[:, j, :]))
                    if j == 0:
                        step(dve.scalar_tensor_tensor(qk[:, 0, :], qk[:, 0, :], itemp[:, 1:2], qks[:, 0, :],
                                                      ALU.mult, ALU.mult))
                    else:
                        step(dve.tensor_tensor(qk[:, 1, :], qk[:, 1, :], qks[:, 1, :], ALU.mult))

        def head(block, h, s):
            @block.tensor
            def _(pe):
                pe.wait_ge(s["q_ready"], 1)
                for t in range(4):
                    pe.matmul(PS[:, t, :], qm[:, t * P:(t + 1) * P], qk[:, 1, :], start=True, stop=True)\
                      .then_inc(s["mm_score"], 1)
                for t in range(4):
                    pe.wait_ge(s["p_ready"], t + 1)
                    if t >= 2:
                        pe.wait_ge(s["pT_ready"], t - 1)
                    for k in range(4):
                        mm = pe.transpose(PS[:, 4 + t % 2, k * P:(k + 1) * P], W[:, t, k * P:(k + 1) * P], ident[:, :])
                    mm.then_inc(s["mm_pT"], 1)
                    pe.wait_ge(s["pT_ready"], t + 1)
                    for k in range(4):
                        mm = pe.matmul(PS[:, 6, t * D1:(t + 1) * D1], PT[:, t % 2, k * P:(k + 1) * P], Vh[:, k, :],
                                       start=(k == 0), stop=(k == 3))
                    mm.then_inc(s["mm_pv"], 1)

            @block.scalar
            def _(act):
                act.activation(qm[:, :], qk[:, 0, :], ACT.Copy, scale=hm[:, ds(h, 1)]).then_inc(s["q_ready"], 1)
                act.activation(Vh[:, :, :], Vt[:, :, ds(h * D1, D1)], ACT.Copy).then_inc(s["vh_ready"], 1)
                for t in range(4):
                    act.wait_ge(s["mm_score"], t + 1)
                    act.wait_ge(s["first_round"], t + 1)
                    act.activation(E[:, t, :], PS[:, t, :], ACT.Exp).then_inc(s["exp_ready"], 1)
                for t in range(4):
                    act.wait_ge(s["mm_pT"], t + 1)
                    if t >= 2:
                        act.wait_ge(s["mm_pv"], t - 1)
                    act.activation(PT[:, t % 2, :], PS[:, 4 + t % 2, :], ACT.Copy).then_inc(s["pT_ready"], 1)

            @block.vector
            def _(dve):
                for r in range(TOPK // 8):
                    for t in range(4):
                        n = 4 * r + t
                        src = W[:, t, :] if r else PS[:, t, :]
                        if r == 0:
                            dve.wait_ge(s["mm_score"], t + 1)
                        else:
                            dve.wait_ge(s["taken"], n - 3)
                        dve.max(m8[:, t, :], src).then_inc(s["max8"], 1)
                    for t in range(4):
                        n = 4 * r + t
                        src = W[:, t, :] if r else PS[:, t, :]
                        dve.wait_ge(s["max8"], n + 1)
                        ins = dve.match_replace(W[:, t, :], m8[:, t, :], src, GONE)
                        ins.then_inc(s["taken"], 1)
                        if r == 0:
                            dve.wait_ge(s["taken"], n + 1)
                            dve.sem_inc(s["first_round"], 1)
                for t in range(4):
                    dve.wait_ge(s["exp_ready"], t + 1)
                    dve.wait_ge(s["taken"], 4 * (TOPK // 8) - 3 + t)
                    dve.scalar_tensor_tensor(W[:, t, :], W[:, t, :], GONE / 2, E[:, t, :], ALU.is_le, ALU.mult,
                                             accum_out=psum[:, t:t + 1]).then_inc(s["p_ready"], 1)
                dve.wait_ge(s["p_ready"], 4)
                dve.reciprocal(prec[:, :], psum[:, :]).then_inc(s["rec_ready"], 1)
                dve.wait_ge(s["rec_ready"], 1)
                dve.wait_ge(s["mm_pv"], 4)
                dve.tensor_tensor(OUT[:, :, ds(h * D1, D1)],
                                  PS[:, 6, 0:4 * D1].rearrange("p (t c) -> p t c", t=4),
                                  prec[:, :].rearrange("p (t a) -> p t a", a=1).broadcast_to([P, 4, D1]),
                                  ALU.mult).then_inc(s["rec_ready"], 1)

        def finish(block, b, s):
            xb = X[:, ds(b, 1), :].rearrange("p a t -> p (a t)")

            @block.tensor
            def _(pe):
                for t in range(4):
                    mm = pe.transpose(PS[:, 0, t * P:(t + 1) * P], OUT[:, t, :], ident[:, :])
                mm.then_inc(s["mm_oT"], 1)
                pe.wait_ge(s["oT_ready"], 1)
                pe.matmul(PS[:, 1, :], w["Wo"][:, :], OT[:, :], start=True, stop=True).then_inc(s["mm_o"], 1)

            @block.scalar
            def _(act):
                act.wait_ge(s["mm_oT"], 1)
                act.activation(OT[:, :], PS[:, 0, :], ACT.Copy).then_inc(s["oT_ready"], 1)

            @block.vector
            def _(dve):
                step = Chain(dve, s["dve_step"])
                dve.wait_ge(s["mm_o"], 1)
                step(dve.scalar_tensor_tensor(xc[:, :], PS[:, 1, :], col["bo"][:, 0:1], hn[:, :], ALU.add, ALU.subtract))
                step(dve.tensor_tensor(xc[:, :], xc[:, :], gate[:, :], ALU.mult))
                step(dve.tensor_tensor(xc[:, :], xc[:, :], hn[:, :], ALU.add))
                step(dve.scalar_tensor_tensor(xb, xc[:, :], mod[:, 2:3], xb, ALU.mult, ALU.add))

        with nc.Fori(0, NB) as b:
            nested(nc, LN_SEMS + "mm_proj mm_v mm_ss mm_temp mean_ready qk_ready qk_sq gate_ready temp_sig norm_ready dve_step",
                   b, project)
            stage(nc, "q_ready vh_ready mm_score first_round exp_ready mm_pT pT_ready mm_pv max8 taken p_ready rec_ready",
                  H1, head)
            nested(nc, "mm_oT oT_ready mm_o dve_step", b, finish)


DEPTH = 6
H2, D2 = 16, 64
WIN = 32
INNER = H2 * D2
NPAIR = H2 // 2
F_IN = P * 4 * 2 // 3
FC = -(-F_IN // P)
QK_SCALE = 8.0


def tower_stage(nc, dram, g, PS):
    X, XF, MOD, eps, mean_w, ident = g.X, g.XF, g.MOD1, g.eps, g.mean_w, g.ident
    with ExitStack() as ctx:
        def sb(n, shape):
            return ctx.enter_context(nc.sbuf_tensor("tower_" + n, shape, F32))
        wqkv, wrot = sb("wqkv", [P, 3 * INNER]), sb("wrot", [P, 2 * INNER])
        wo, w1, w2 = sb("wo", [P, NPAIR, P]), sb("w1", [P, 2 * FC, P]), sb("w2", [P, FC, P])
        b1, cols = sb("b1", [P, DEPTH, 2 * FC]), sb("cols", [P, DEPTH, 7])
        lb1, lcol = sb("lb1", [P, 2 * FC]), sb("lcol", [P, 7])
        tab = sb("tab", [P, 4, T])
        sel2, hsel = sb("sel2", [P, 2]), sb("hsel", [H2, NPAIR, P])
        bias = sb("bias", [P, 2, 2 * WIN])
        xs, xc, sq, rstd, xn = (sb(n, [P, T]) for n in ("xs", "xc", "sq", "rstd", "xn"))
        V, VP = sb("V", [P, 4, INNER]), sb("VP", [P, 4, INNER])
        QT, KT = sb("QT", [P, NPAIR, T]), sb("KT", [P, NPAIR, WIN + T])
        qc, qsq, t1, t2 = (sb(n, [P, 2, T]) for n in ("qc", "qsq", "t1", "t2"))
        rn, rkT = sb("rn", [P, 4, 2, H2]), sb("rkT", [H2, T])
        SC, PT, AO = sb("SC", [P, 2, INNER]), sb("PT", [P, 2, INNER]), sb("AO", [P, INNER])
        OT = sb("OT", [P, NPAIR, T])
        mx, ssum, rsum = sb("mx", [P, 2, H2]), sb("ssum", [P, 2, H2]), sb("rsum", [P, 2, H2])
        mod = sb("mod", [P, 6])
        flat = V[:, :, :].rearrange("p a c -> p (a c)")
        hg = [flat[:, j * T:(j + 1) * T] for j in range(2 * FC)]

        def setup(block, i, s):
            loads = [(b1[:, :, :], dram["f_b1"]), (cols[:, :, :], dram["f_cols"]), (sel2[:, :], dram["sel2"]),
                     (hsel[:, :, :], dram["hsel"]), (bias[:, :, :], dram["winmask"])]

            @block.sync
            def _(sp):
                for tile, src in loads:
                    sp.dma_start(tile, src).then_inc(s["w_in"], 16)
                sp.wait_ge(s["w_in"], 16 * len(loads))

            @block.gpsimd
            def _(pool):
                pool.memset(xs[64:128, 0:1], 0.0).then_inc(s["pool_done"], 1)
                pool.wait_ge(s["pool_done"], 1)
                pool.memset(VP[0:WIN, 0, :], 0.0).then_inc(s["pool_done"], 1)
                pool.wait_ge(s["pool_done"], 2)
                pool.memset(KT[:, :, 0:WIN], 0.0).then_inc(s["pool_done"], 1)
                pool.wait_ge(s["pool_done"], 3)
        stage(nc, "w_in pool_done", 1, setup)

        def enter(block, b, s):
            xb = X[:, ds(b, 1), :].rearrange("p a t -> p (a t)")
            xf = XF[:, ds(b, 1), :].rearrange("p a t -> p (a t)")

            @block.tensor
            def _(pe):
                ln_tensor(pe, s, xb, mean_w[:, :], sq[:, :], PS[:, 0, :], PS[:, 1, :])

            @block.scalar
            def _(act):
                ln_scalar(act, s, xc[:, :], sq[:, :], PS[:, 1, :], rstd[:, :], eps[:, 0:1])

            @block.vector
            def _(dve):
                step = Chain(dve, s["dve_step"])
                step(dve.tensor_copy(mod[:, :], MOD[:, ds(b, 1), :].rearrange("p a j -> p (a j)")))
                ln_vector(dve, s, xb, xc[:, :], PS[:, 0, :], rstd[:, :], mod[:, 4:5], mod[:, 3:4], xf)
        stage(nc, LN_SEMS + "dve_step", NB, enter)

        def load_layer(block, l, s):
            @block.sync
            def _(sp):
                def from_layer(name, tile):
                    src = dram[name][ds(l, 1)]
                    sp.dma_start(tile, src.rearrange("a p c -> p (a c)")).then_inc(s["layer_in"], 16)
                from_layer("f_Wqkv", wqkv[:, :])
                src = dram["f_Wqkv"][ds(l, 1), :, 0:2 * INNER].rearrange("a p (g z c) -> p (a g) z c", z=2, c=D2 // 2)
                dst = wrot[:, :].rearrange("p (g z c) -> p g z c", z=2, c=D2 // 2)
                for z in range(2):
                    sp.dma_start(dst[:, :, z, :], src[:, :, 1 - z, :]).then_inc(s["layer_in"], 16)
                from_layer("f_Wo", wo[:, :, :].rearrange("p a c -> p (a c)"))
                from_layer("f_W1", w1[:, :, :].rearrange("p a c -> p (a c)"))
                from_layer("f_W2", w2[:, :, :].rearrange("p a c -> p (a c)"))
                sp.dma_start(tab[:, :, :], dram["rotary"]).then_inc(s["tab_in"], 16)
                sp.wait_ge(s["layer_in"], 16 * 6)

            @block.vector
            def _(dve):
                dve.tensor_copy(lb1[:, :], b1[:, ds(l, 1), :].rearrange("p a j -> p (a j)")).then_inc(s["col_ready"], 1)
                dve.tensor_copy(lcol[:, :], cols[:, ds(l, 1), :].rearrange("p a j -> p (a j)")).then_inc(s["col_ready"], 1)
                dve.wait_ge(s["col_ready"], 2)
                dve.wait_ge(s["tab_in"], 16)
                for j in range(4):
                    dve.tensor_scalar(tab[:, j, :], tab[:, j, :], lcol[:, 3 + j:4 + j], None, ALU.mult)\
                       .then_inc(s["col_ready"], 1)

        def layer(block, b, s):
            xf = XF[:, ds(b, 1), :].rearrange("p a t -> p (a t)")
            xf_lo = XF[0:64, ds(b, 1), :].rearrange("p a t -> p (a t)")
            xf_hi = XF[64:128, ds(b, 1), 0:T - 1].rearrange("p a t -> p (a t)")

            @block.tensor
            def _(pe):
                pe.wait_ge(s["xs_ready"], 2)
                for t in range(4):
                    for j in range(2):
                        n = 2 * t + j
                        if n >= 2:
                            pe.wait_ge(s["v_ready"], n - 1)
                        pe.matmul(PS[:, n % 2, :], xs[:, t * P:(t + 1) * P],
                                  wqkv[:, 2 * INNER + j * 512:2 * INNER + (j + 1) * 512], start=True, stop=True)\
                          .then_inc(s["mm_v"], 1)
                for p in range(NPAIR):
                    for j in range(2):
                        c = slice(j * INNER + p * P, j * INNER + (p + 1) * P)
                        if p:
                            pe.wait_ge(s["qc_ready"], 2 * (p - 1) + j + 1)
                        pe.matmul(PS[:, 2 + j, :], wqkv[:, c], xs[:, :], start=True, stop=True).then_inc(s["mm_q"], 1)
                        if p:
                            pe.wait_ge(s["t2_ready"], 2 * (p - 1) + j + 1)
                        pe.matmul(PS[:, 4 + j, :], wrot[:, c], xs[:, :], start=True, stop=True).then_inc(s["mm_qr"], 1)
                    if p:
                        norms_of(pe, s, p - 1)
                norms_of(pe, s, NPAIR - 1)
                pe.wait_ge(s["rn_ready"], 1)
                for t in range(4):
                    mm = pe.transpose(PS[0:H2, 7, t * P:(t + 1) * P], rn[:, t, 1, :], ident[:, :])
                mm.then_inc(s["mm_rkT"], 1)
                pe.wait_ge(s["rkT_ready"], 1)
                for p in range(NPAIR):
                    if p >= 2:
                        pe.wait_ge(s["kt_ready"], p - 1)
                    pe.matmul(PS[:, p % 2, :], hsel[:, p, :], rkT[:, :], start=True, stop=True).then_inc(s["mm_rk"], 1)
                pe.wait_ge(s["kt_ready"], NPAIR)
                pe.wait_ge(s["qt_ready"], 2 * NPAIR)

                def scores(t):
                    if t:
                        pe.wait_ge(s["sc_scaled"], 2 * t)
                    for h in range(H2):
                        r = slice(64 * (h % 2), 64 * (h % 2) + 64)
                        for w in range(4):
                            c0 = t * P + w * WIN
                            mm = pe.matmul(PS[32 * w:32 * w + 32, h % 2, (h // 2) * 64:(h // 2) * 64 + 64],
                                           QT[r, h // 2, c0:c0 + WIN], KT[r, h // 2, c0:c0 + 2 * WIN],
                                           start=True, stop=True, tile_position=(64 * (h % 2), 32 * w))
                    mm.then_inc(s["mm_sc"], 1)

                def values(t):
                    pe.wait_ge(s["pt_ready"], t + 1)
                    if t == 0:
                        pe.wait_ge(s["vp_in"], 16 * 4)
                    else:
                        pe.wait_ge(s["ao_ready"], 2 * t)
                    for h in range(H2):
                        hc = (h % 2) * 512 + (h // 2) * 64
                        for w in range(4):
                            r = slice(32 * w, 32 * w + 32)
                            for kb, v in enumerate((VP, V)):
                                mm = pe.matmul(PS[r, 2 + h // 8, (h % 8) * 64:(h % 8) * 64 + 64],
                                               PT[r, t % 2, hc + 32 * kb:hc + 32 * kb + 32],
                                               v[r, t, h * D2:(h + 1) * D2], start=(kb == 0), stop=(kb == 1),
                                               tile_position=(32 * w, 32 * w))
                    mm.then_inc(s["mm_pv"], 1)

                def turn(t):
                    pe.wait_ge(s["ao_ready"], 2 * t + 2)
                    if t:
                        pe.wait_ge(s["ot_ready"], 2 * t)
                    for p in range(NPAIR):
                        mm = pe.transpose(PS[:, 4 + p // 4, (p % 4) * P:(p % 4 + 1) * P], AO[:, p * P:(p + 1) * P],
                                          ident[:, :])
                        if p % 4 == 3:
                            mm.then_inc(s["mm_ot"], 1)
                scores(0)
                for t in range(4):
                    if t < 3:
                        scores(t + 1)
                    values(t)
                    if t:
                        turn(t - 1)
                turn(3)
                pe.wait_ge(s["ot_ready"], 8)
                for p in range(NPAIR):
                    mm = pe.matmul(PS[:, 6, :], wo[:, p, :], OT[:, p, :], start=(p == 0), stop=(p == NPAIR - 1))
                mm.then_inc(s["mm_o"], 1)
                pe.wait_ge(s["xs_ready"], 4)
                ln_tensor(pe, s, xs[:, :], mean_w[:, :], sq[:, :], PS[:, 0, :], PS[:, 1, :])
                pe.wait_ge(s["ln_out"], 1)
                for j in range(FC):
                    pe.matmul(PS[:, 2 + j, :], w1[:, FC + j, :], xn[:, :], start=True, stop=True).then_inc(s["mm_gate"], 1)
                for j in range(FC):
                    if j == 2:
                        pe.wait_ge(s["x_mid"], 1)
                    pe.matmul(PS[:, (5, 7, 6)[j], :], w1[:, j, :], xn[:, :], start=True, stop=True).then_inc(s["mm_val"], 1)
                for j in range(FC):
                    pe.wait_ge(s["h_ready"], j + 1)
                    mm = pe.matmul(PS[:, 0, :], w2[:, j, :], hg[FC + j], start=(j == 0), stop=(j == FC - 1))
                mm.then_inc(s["mm_mlp"], 1)

            @block.scalar
            def _(act):
                for n in range(8):
                    act.wait_ge(s["mm_v"], n + 1)
                    act.activation(V[:, n // 2, (n % 2) * 512:(n % 2 + 1) * 512], PS[:, n % 2, :], ACT.Copy)\
                       .then_inc(s["v_ready"], 1)
                for p in range(NPAIR):
                    for j in range(2):
                        n = 2 * p + j
                        act.wait_ge(s["mm_q"], n + 1)
                        if p:
                            act.wait_ge(s["t1_ready"], n - 1)
                        act.activation(qc[:, j, :], PS[:, 2 + j, :], ACT.Copy).then_inc(s["qc_ready"], 1)
                        act.wait_ge(s["qc_ready"], n + 1)
                        if p:
                            act.wait_ge(s["mm_ss"], n - 1)
                        act.activation(qsq[:, j, :], qc[:, j, :], ACT.Square).then_inc(s["qsq_ready"], 1)
                act.wait_ge(s["mm_ss"], 2 * NPAIR)
                act.activation(rn[:, :, :, :].rearrange("p t z h -> p (t z h)"), PS[:, 6, 0:128], ACT.Sqrt)\
                   .then_inc(s["norm_ready"], 1)
                act.wait_ge(s["mm_rkT"], 1)
                act.activation(rkT[:, :], PS[0:H2, 7, :], ACT.Copy).then_inc(s["rkT_ready"], 1)

                def turned(t):
                    for j in range(2):
                        act.wait_ge(s["mm_ot"], 2 * t + j + 1)
                        act.activation(OT[:, 4 * j:4 * j + 4, t * P:(t + 1) * P],
                                       PS[:, 4 + j, :].rearrange("p (a c) -> p a c", a=4), ACT.Copy).then_inc(s["ot_ready"], 1)
                for t in range(4):
                    act.wait_ge(s["sc_ready"], t + 1)
                    act.activation(SC[:, t % 2, :], SC[:, t % 2, :], ACT.Exp).then_inc(s["exp_ready"], 1)
                    if t >= 2:
                        turned(t - 2)
                turned(2)
                turned(3)
                ln_scalar(act, s, xc[:, :], sq[:, :], PS[:, 1, :], rstd[:, :], eps[:, 0:1])
                for j in range(FC):
                    act.wait_ge(s["mm_gate"], j + 1)
                    act.activation(hg[j], PS[:, 2 + j, :], ACT.Gelu, bias=lb1[:, FC + j:FC + j + 1]).then_inc(s["gelu_ready"], 1)

            @block.gpsimd
            def _(pool):
                for p in range(NPAIR):
                    for j in range(2):
                        n = 2 * p + j
                        pool.wait_ge(s["t1_ready"], n + 1)
                        pool.wait_ge(s["t2_ready"], n + 1)
                        dst = QT[:, p, :] if j == 0 else KT[:, p, WIN:]
                        pool.tensor_tensor(dst, t1[:, j, :], t2[:, j, :], ALU.add).then_inc(s["qt_ready"], 1)

            @block.sync
            def _(sp):
                sp.wait_ge(s["v_ready"], 8)
                sp.dma_start(VP[WIN:P, :, :], V[0:P - WIN, :, :]).then_inc(s["vp_in"], 16)
                for t in range(3):
                    sp.dma_start(VP[0:WIN, t + 1, :], V[P - WIN:P, t, :]).then_inc(s["vp_in"], 16)
                sp.wait_ge(s["vp_in"], 16 * 4)

            @block.vector
            def _(dve):
                step = Chain(dve, s["dve_step"])
                dve.tensor_copy(xs[0:64, :], xf_lo).then_inc(s["xs_ready"], 1)
                dve.tensor_copy(xs[64:128, 1:T], xf_hi).then_inc(s["xs_ready"], 1)
                for p in range(NPAIR):
                    for j in range(2):
                        n = 2 * p + j
                        dve.wait_ge(s["qc_ready"], n + 1)
                        if p:
                            dve.wait_ge(s["qt_ready"], n - 1)
                        dve.tensor_tensor(t1[:, j, :], qc[:, j, :], tab[:, 2 * j, :], ALU.mult).then_inc(s["t1_ready"], 1)
                        dve.wait_ge(s["mm_qr"], n + 1)
                        dve.tensor_tensor(t2[:, j, :], PS[:, 4 + j, :], tab[:, 2 * j + 1, :], ALU.mult)\
                           .then_inc(s["t2_ready"], 1)
                dve.wait_ge(s["norm_ready"], 1)
                flat_rn = rn[:, :, :, :].rearrange("p t z h -> p (t z h)")
                step(dve.tensor_scalar(flat_rn, flat_rn, 1e-12, None, ALU.max))
                dve.reciprocal(flat_rn, flat_rn).then_inc(s["rn_ready"], 1)
                for p in range(NPAIR):
                    dve.wait_ge(s["mm_rk"], p + 1)
                    dve.wait_ge(s["qt_ready"], 2 * p + 2)
                    dve.tensor_tensor(KT[:, p, WIN:], KT[:, p, WIN:], PS[:, p % 2, :], ALU.mult).then_inc(s["kt_ready"], 1)

                def heads(a):
                    return a.rearrange("p (g k) -> p g k", k=2 * WIN)

                def spread(a):
                    return a.rearrange("p (g k) -> p g k", k=1)

                def front(t):
                    dve.wait_ge(s["mm_sc"], t + 1)
                    if t >= 2:
                        dve.wait_ge(s["pt_ready"], t - 1)
                    for j in range(2):
                        dve.tensor_tensor(heads(SC[:, t % 2, 512 * j:512 * j + 512]), heads(PS[:, j, :]),
                                          spread(rn[:, t, 0, 8 * j:8 * j + 8]).broadcast_to([P, 8, 2 * WIN]),
                                          ALU.mult).then_inc(s["sc_scaled"], 1)
                    dve.wait_ge(s["sc_scaled"], 2 * t + 2)
                    sc = heads(SC[:, t % 2, :])
                    mk = bias[:, min(t, 1):min(t, 1) + 1, :].broadcast_to([P, H2, 2 * WIN])
                    step(dve.scalar_tensor_tensor(sc, sc, QK_SCALE, mk, ALU.mult, ALU.add))
                    step(dve.tensor_reduce(mx[:, t % 2, :], sc, AX, ALU.max))
                    dve.tensor_tensor(sc, sc, spread(mx[:, t % 2, :]).broadcast_to([P, H2, 2 * WIN]), ALU.subtract)\
                       .then_inc(s["sc_ready"], 1)

                def back(t):
                    dve.wait_ge(s["exp_ready"], t + 1)
                    if t >= 2:
                        dve.wait_ge(s["mm_pv"], t - 1)
                    dve.transpose(PT[:, t % 2, :], SC[:, t % 2, :]).then_inc(s["pt_ready"], 1)
                    step(dve.tensor_reduce(ssum[:, t % 2, :].rearrange("p (g z) -> p z g", z=2),
                                           SC[:, t % 2, :].rearrange("p (z g k) -> p z g k", z=2, k=2 * WIN), AX, ALU.add))
                    step(dve.reciprocal(rsum[:, t % 2, :], ssum[:, t % 2, :]))

                def outs(t):
                    dve.wait_ge(s["mm_pv"], t + 1)
                    if t:
                        dve.wait_ge(s["mm_ot"], 2 * t)
                    for j in range(2):
                        dve.tensor_tensor(AO[:, 512 * j:512 * j + 512].rearrange("p (g k) -> p g k", k=D2),
                                          PS[:, 2 + j, :].rearrange("p (g k) -> p g k", k=D2),
                                          spread(rsum[:, t % 2, 8 * j:8 * j + 8]).broadcast_to([P, 8, D2]),
                                          ALU.mult).then_inc(s["ao_ready"], 1)
                front(0)
                for t in range(4):
                    if t < 3:
                        front(t + 1)
                    back(t)
                    outs(t)
                dve.wait_ge(s["mm_o"], 1)
                dve.tensor_tensor(xf, xf, PS[:, 6, :], ALU.add).then_inc(s["x_mid"], 1)
                dve.wait_ge(s["x_mid"], 1)
                dve.tensor_copy(xs[0:64, :], xf_lo).then_inc(s["xs_ready"], 1)
                dve.tensor_copy(xs[64:128, 1:T], xf_hi).then_inc(s["xs_ready"], 1)
                dve.wait_ge(s["xs_ready"], 4)
                ln_vector(dve, s, xs[:, :], xc[:, :], PS[:, 0, :], rstd[:, :], lcol[:, 0:1], lcol[:, 1:2], xn[:, :])
                for j in range(FC):
                    dve.wait_ge(s["gelu_ready"], j + 1)
                    dve.wait_ge(s["mm_val"], j + 1)
                    dve.scalar_tensor_tensor(hg[FC + j], PS[:, (5, 7, 6)[j], :], lb1[:, j:j + 1], hg[j], ALU.add, ALU.mult)\
                       .then_inc(s["h_ready"], 1)
                dve.wait_ge(s["mm_mlp"], 1)
                dve.scalar_tensor_tensor(xf, PS[:, 0, :], lcol[:, 2:3], xf, ALU.add, ALU.add).then_inc(s["dve_step"], 1)

        def norms_of(pe, s, p):
            cols6 = PS[:, 6, 0:128].rearrange("p (t z y g) -> p t z y g", t=4, z=2, y=2)
            for j in range(2):
                pe.wait_ge(s["qsq_ready"], 2 * p + j + 1)
                for t in range(4):
                    mm = pe.matmul(cols6[:, t, j, :, p], qsq[:, j, t * P:(t + 1) * P], sel2[:, :], start=True, stop=True)
                mm.then_inc(s["mm_ss"], 1)

        names = LN_SEMS + ("xs_ready mm_v v_ready mm_q mm_qr qc_ready qsq_ready mm_ss t1_ready t2_ready qt_ready "
                           "norm_ready rn_ready mm_rkT rkT_ready mm_rk kt_ready mm_sc sc_scaled sc_ready exp_ready "
                           "pt_ready vp_in mm_pv ao_ready mm_ot ot_ready mm_o x_mid mm_gate mm_val gelu_ready h_ready "
                           "mm_mlp dve_step")
        with nc.Fori(0, DEPTH) as l:
            nested(nc, "layer_in tab_in col_ready", l, load_layer)
            stage(nc, names, NB, layer)

        def leave(block, b, s):
            xb = X[:, ds(b, 1), :].rearrange("p a t -> p (a t)")
            xf = XF[:, ds(b, 1), :].rearrange("p a t -> p (a t)")

            @block.vector
            def _(dve):
                step = Chain(dve, s["dve_step"])
                step(dve.tensor_copy(mod[:, :], MOD[:, ds(b, 1), :].rearrange("p a j -> p (a j)")))
                step(dve.scalar_tensor_tensor(xb, xf, mod[:, 5:6], xb, ALU.mult, ALU.add))
        stage(nc, "dve_step", NB, leave)


class Globals:
    pass


def build(nc, dram, out):
    with ExitStack() as ctx:
        def sb(n, shape):
            return ctx.enter_context(nc.sbuf_tensor(n, shape, F32))
        g = Globals()
        g.X = sb("X", [P, NB, T])
        g.MOD0, g.MOD1 = sb("MOD0", [P, NB, 6]), sb("MOD1", [P, NB, 6])
        g.eps = sb("eps", [P, 4])
        g.mean_w, g.ident = sb("mean_w", [P, P]), sb("ident", [P, P])
        PS = ctx.enter_context(nc.psum_tensor("PS", [P, 8, 512], F32))
        consts = [(g.X[:, :, :], dram["x"]), (g.eps[:, :], dram["eps"]), (g.mean_w[:, :], dram["mean_w"]),
                  (g.ident[:, :], dram["ident"])]
        modulation_stage(nc, dram, consts, PS, (g.MOD0, g.MOD1))
        delta_attention_stage(nc, dram, g, PS)
        experts_stage(nc, dram, g, PS)
        topk_attention_stage(nc, dram, g, PS)
        g.XF = sb("XF", [P, NB, T])
        tower_stage(nc, dram, g, PS)

        def store(block, i, s):
            @block.sync
            def _(sp):
                sp.dma_start(out, g.X[:, :, :]).then_inc(s["out_done"], 16)
                sp.wait_ge(s["out_done"], 16)
        stage(nc, "out_done", 1, store)


def shape_constants(np):
    f = np.float32
    c = {"ident": np.eye(P, dtype=f), "mean_w": np.full((P, P), 1.0 / P, f)}
    c["eps"] = np.tile(np.array([LN_EPS, 1e-6, 0, 0], f), (P, 1))
    i = np.arange(P)
    c["blk32"] = (i[:, None] // D0 == i[None, :] // D0).astype(f)
    r, q = np.arange(CH)[:, None], np.arange(CH)[None, :]
    m = [q < r, r <= q, r == q, (r // 2 == q // 2) & (r % 2 == 1) & (q % 2 == 0)]
    for z in (2, 4, 8, 16):
        m.append((r // (2 * z) == q // (2 * z)) & (q // z % 2 == 1) & (r // z % 2 == 0))
    c["masks"] = np.tile(np.stack(m, 1), (H0, 1, 1)).astype(f)
    sel = np.zeros((P, 4, 3, P), f)
    for h in range(H0):
        ch = slice(32 * h, 32 * h + 32)
        for k in range(4):
            row = 32 * h + 4 * k
            sel[ch, k, 0, row] = sel[ch, k, 0, row + 1] = 1.0 / D0
            sel[ch, k, 1, row + 2] = 1.0 / D0
            sel[ch, k, 2, row + 1] = 1.0 / D0
            sel[ch, k, 2, row + 3] = 1.0
    c["sel"] = sel
    used = i % 32 < 16
    c["stm"] = np.stack([used & (i % 2 == 0), used & (i % 4 == 1), used & (i % 4 == 3)], 1).astype(f)
    ps = np.zeros((16, 4, P), f)
    for h in range(H0):
        for k in range(4):
            ps[4 * h + k, k, 32 * h:32 * h + 32] = 1
    c["psel"] = ps
    c["sel2"] = (i[:, None] // D2 == np.arange(2)[None, :]).astype(f)
    hs = np.zeros((H2, NPAIR, P), f)
    for par in range(2):
        for p in range(NPAIR):
            hs[par * NPAIR + p, p, 64 * par:64 * par + 64] = 1
    c["hsel"] = hs
    q, j = i % WIN, np.arange(2 * WIN)
    ok = (q[:, None] <= j[None, :]) & (j[None, :] <= q[:, None] + WIN)
    first = ok & ((i[:, None] >= WIN) | (j[None, :] >= WIN))
    c["winmask"] = np.where(np.stack([first, ok], 1), 0, -1e30).astype(f)
    half = np.arange(0, D2, 2, dtype=f)
    tt = np.arange(T, dtype=f)
    ang = tt[:, None] * (f(1.0) / f(10000.0) ** (half / f(D2)))[None, :]
    scl = ((half + f(0.4 * D2)) / f(1.4 * D2))[None, :] ** ((tt - T // 2) / f(WIN // 2))[:, None]
    ang, scl = (np.concatenate([z, z], -1) for z in (ang, scl))
    sgn = np.where(np.arange(D2) < D2 // 2, -1, 1).astype(f)
    tabs = [np.cos(ang) * scl, np.sin(ang) * sgn * scl, np.cos(ang) / scl, np.sin(ang) * sgn / scl]
    c["rotary"] = np.tile(np.stack([z.T for z in tabs], 1), (2, 1, 1)).astype(f)
    e = np.arange(8)
    c["tri8"] = np.tile((e[None, :] < e[:, None]).astype(f), (P, 1, 1))
    c["esel"] = np.tile(np.eye(8, dtype=f)[:, :, None], (1, 1, P))
    c["t_blk8"] = (i[:, None] // D1 == i[None, :] // D1).astype(f)
    c["hm"] = (i[:, None] // D1 == np.arange(H1)[None, :]).astype(f)
    return c


def kernel(**inputs):
    import numpy as np
    import concourse.bacc as bacc
    from concourse.bass_utils import run_bass_kernel_spmd as run

    def col(a, rep=1):
        return np.repeat(a.reshape(-1), rep).reshape(-1, 1)

    a = {n[8:]: v for n, v in inputs.items() if n.startswith("L0_attn_")}
    h = shape_constants(np)
    h["x"] = a["hidden_states"].transpose(2, 0, 1)
    for l in range(2):
        h[f"cT{l}"], h[f"wmod{l}"] = inputs[f"L{l}_c"].T, inputs[f"L{l}_wmod"]
    h["qwT"], h["kwT"], h["vwT"], h["owT"] = a["q_w"].T, a["k_w"].T, a["v_w"].T, a["o_w"].T
    h["bwT"] = np.repeat(a["b_w"].T, D0, axis=1)
    h["cw"] = np.stack([a["q_cw"], a["k_cw"], a["v_cw"]], 1)
    h["firs"], h["firl"] = a["fir_short_w"].reshape(P, FIR_S), a["fir_long_w"].reshape(P, FIR_L)
    h["mlp1h"] = a["mlp1_w"].T[:P]
    h["mlp1s"] = np.tile(np.concatenate([a["mlp1_w"].T[P:], np.zeros((16, P), np.float32)]), (4, 1))
    h["mlp1b"], h["mlp2T"] = col(a["mlp1_b"]), a["mlp2_w"].T
    h["mlp2b"] = np.tile(a["mlp2_b"], (P, 1))
    h["ltemp"], h["cres"] = col(a["logit_temp"], P), col(a["conv_res_logit"], D0)
    h["normw"] = np.tile(a["norm_w"], H0).reshape(P, 1)
    m = {n[7:]: v for n, v in inputs.items() if n.startswith("L0_ffn_")}
    h["w1"] = np.concatenate([m["w1"], m["cfc"][None]]).transpose(2, 0, 1)
    h["w2"] = np.concatenate([m["w2"], m["cproj"][None]]).transpose(2, 0, 1)
    h["gate_wT"], h["lb_bias"] = m["gate_w"].T, np.tile(m["lb_bias"], (P, 1))
    t = {n[8:]: v for n, v in inputs.items() if n.startswith("L1_attn_")}
    for n in ("Wq", "Wk", "Wv", "Wo", "Wg", "Wt"):
        h["t_" + n] = t[n]
    for n in ("bq", "bk", "bo", "bg"):
        h["t_" + n] = col(t[n])
    h["t_bt"], h["t_bv"] = col(t["bt"], P), np.tile(t["bv"], (P, 1))
    u = {n[7:]: v for n, v in inputs.items() if n.startswith("L1_ffn_")}
    h["f_Wqkv"] = u["Wqkv"]
    h["f_Wo"] = u["Wo"].reshape(DEPTH, NPAIR, P, P).transpose(0, 2, 1, 3).reshape(DEPTH, P, NPAIR * P)

    def chunked(v, axis):
        fill = [(0, 0)] * v.ndim
        fill[axis] = (0, FC * P - F_IN)
        return np.pad(v, fill)
    h["f_W1"] = np.concatenate([chunked(z, 2) for z in np.split(u["W1"], 2, 2)], 2)
    h["f_W2"] = chunked(u["W2"], 1).reshape(DEPTH, FC, P, P).transpose(0, 2, 1, 3).reshape(DEPTH, P, FC * P)
    h["f_b1"] = np.concatenate([chunked(z, 1) for z in np.split(u["b1"], 2, 1)], 1)\
        .reshape(DEPTH, 2 * FC, P).transpose(2, 0, 1)
    qs, ks = u["q_scale"], u["k_scale"]
    swap = (np.arange(D2) + D2 // 2) % D2
    h["f_cols"] = np.stack([u["ln_g"], u["ln_b"], u["b2"]] + [np.tile(z, (1, 2)) for z in
                           (qs, qs[:, swap], ks, ks[:, swap])], 1).transpose(2, 0, 1)

    nc = bacc.Bacc("TRN2", target_bir_lowering=False, num_devices=1)
    arrays, dram = {}, {}
    for n, v in h.items():
        arrays["in_" + n] = np.ascontiguousarray(v)
        dram[n] = nc.dram_tensor("in_" + n, v.shape, F32, kind="ExternalInput").ap()
    out = nc.dram_tensor("out", (P, NB, T), F32, kind="ExternalOutput").ap()
    build(nc, dram, out)
    r = run(nc, [arrays], core_ids=[0])
    return np.ascontiguousarray(r.results[0]["out"].transpose(1, 2, 0))
```

```python
from contextlib import ExitStack

import concourse.bass as bass
from concourse import mybir
from concourse.alu_op_type import AluOpType as ALU

F32 = mybir.dt.float32
ACT = mybir.ActivationFunctionType
AX = mybir.AxisListType.X
ds = bass.ds

P = 128
NB = 8
T = 512
LN_EPS = 1e-5
H0, D0 = 4, 32
CH = 32
NCH = T // CH
FIR_S, FIR_L = 5, 64
PROB_FLOOR = 0.02


def semaphores(nc, ctx, names):
    return {n: ctx.enter_context(nc.semaphore(n)) for n in names.split()}


def end_of_body(nc, s):
    for h in s.values():
        nc.gpsimd.sem_clear(h)
    nc.all_engine_barrier()


def stage(nc, names, count, body):
    with ExitStack() as ctx:
        s = semaphores(nc, ctx, names)

        def once(i):
            with nc.Block() as block:
                body(block, i, s)
            end_of_body(nc, s)

        if count == 1:
            once(0)
        else:
            with nc.Fori(0, count) as i:
                once(i)


LN_SEMS = "ln_mean ln_xc ln_sq ln_var ln_log ln_rstd ln_norm ln_out "


def ln_tensor(pe, s, x, mean_w, sq, ps_mean, ps_var):
    pe.matmul(ps_mean, mean_w, x, start=True, stop=True).then_inc(s["ln_mean"], 1)
    pe.wait_ge(s["ln_sq"], 1)
    pe.matmul(ps_var, mean_w, sq, start=True, stop=True).then_inc(s["ln_var"], 1)


def ln_scalar(act, s, xc, sq, ps_var, rstd, eps):
    act.wait_ge(s["ln_xc"], 1)
    act.activation(sq, xc, ACT.Square).then_inc(s["ln_sq"], 1)
    act.wait_ge(s["ln_var"], 1)
    act.activation(rstd, ps_var, ACT.Ln, bias=eps).then_inc(s["ln_log"], 1)
    act.wait_ge(s["ln_log"], 1)
    act.activation(rstd, rstd, ACT.Exp, scale=-0.5).then_inc(s["ln_rstd"], 1)


def ln_vector(dve, s, x, xc, ps_mean, rstd, gain, shift, out):
    dve.wait_ge(s["ln_mean"], 1)
    dve.tensor_tensor(xc, x, ps_mean, ALU.subtract).then_inc(s["ln_xc"], 1)
    dve.wait_ge(s["ln_rstd"], 1)
    dve.wait_ge(s["ln_xc"], 1)
    dve.tensor_tensor(xc, xc, rstd, ALU.mult).then_inc(s["ln_norm"], 1)
    dve.wait_ge(s["ln_norm"], 1)
    dve.tensor_scalar(out, xc, gain, shift, ALU.mult, ALU.add).then_inc(s["ln_out"], 1)


def nested(nc, names, i, body):
    with ExitStack() as ctx:
        s = semaphores(nc, ctx, names)
        with nc.Block() as block:
            body(block, i, s)
        end_of_body(nc, s)


class Chain:

    def __init__(self, eng, sem):
        self.eng, self.sem, self.n = eng, sem, 0

    def __call__(self, ins):
        self.n += 1
        ins.then_inc(self.sem, 1)
        self.eng.wait_ge(self.sem, self.n)


def modulation_stage(nc, dram, consts, PS, MOD):
    with ExitStack() as ctx:
        def sb(n, shape):
            return ctx.enter_context(nc.sbuf_tensor("mod_" + n, shape, F32))
        cT = [sb(f"cT{l}", [P, NB]) for l in range(2)]
        wm = [sb(f"wm{l}", [P, 6 * P]) for l in range(2)]
        sgn = sb("sgn", [P, NB])

        def body(block, i, s):
            @block.sync
            def _(sp):
                for l in range(2):
                    sp.dma_start(cT[l][:, :], dram[f"cT{l}"]).then_inc(s["c_in"], 16)
                    sp.dma_start(wm[l][:, :], dram[f"wmod{l}"]).then_inc(s["c_in"], 16)
                for tile, src in consts:
                    sp.dma_start(tile, src).then_inc(s["const_in"], 16)
                sp.wait_ge(s["const_in"], 16 * len(consts))

            @block.scalar
            def _(act):
                act.wait_ge(s["c_in"], 64)
                for l in range(2):
                    act.activation(cT[l][:, :], cT[l][:, :], ACT.Silu).then_inc(s["c_silu"], 1)

            @block.tensor
            def _(pe):
                pe.wait_ge(s["c_silu"], 2)
                for l in range(2):
                    for j in range(6):
                        mm = pe.matmul(PS[:, l, j * NB:(j + 1) * NB], wm[l][:, j * P:(j + 1) * P],
                                       cT[l][:, :], start=True, stop=True)
                    mm.then_inc(s["mod_ps"], 1)

            @block.vector
            def _(dve):
                step = Chain(dve, s["dve_step"])
                for l in range(2):
                    dve.wait_ge(s["mod_ps"], l + 1)
                    m = MOD[l]
                    step(dve.tensor_copy(m[:, :, :].rearrange("p b j -> p j b"),
                                         PS[:, l, 0:6 * NB].rearrange("p (j b) -> p j b", j=6)))
                    for j in (1, 4):
                        step(dve.tensor_scalar(m[:, :, j], m[:, :, j], 1.0, None, ALU.add))
                    for j in (2, 5):
                        step(dve.tensor_scalar(sgn[:, :], m[:, :, j], 0.0, 2.0, ALU.is_ge, ALU.mult))
                        step(dve.tensor_scalar(sgn[:, :], sgn[:, :], 1.0, None, ALU.subtract))
                        step(dve.tensor_tensor(m[:, :, j], m[:, :, j], sgn[:, :], ALU.mult))
                        step(dve.scalar_tensor_tensor(m[:, :, j], m[:, :, j], 0.25, sgn[:, :], ALU.max, ALU.mult))

        stage(nc, "c_in const_in c_silu mod_ps dve_step", 1, body)


def delta_attention_stage(nc, dram, g, PS):
    X, MOD, eps, mean_w, ident = g.X, g.MOD0, g.eps, g.mean_w, g.ident
    with ExitStack() as ctx:
        def sb(n, shape):
            return ctx.enter_context(nc.sbuf_tensor("delta_" + n, shape, F32))
        w = {n: sb("a_" + n, [P, P]) for n in ("qwT", "kwT", "vwT", "bwT", "mlp1h", "mlp1s", "owT")}
        cw = sb("a_cw", [P, 3, 4])
        firs, firl = sb("a_firs", [P, FIR_S]), sb("a_firl", [P, FIR_L])
        mlp1b, mlp2T, mlp2b = sb("a_mlp1b", [P, 1]), sb("a_mlp2T", [P, 4]), sb("a_mlp2b", [P, 4])
        ltemp, cres, normw = sb("a_ltemp", [P, 1]), sb("a_cres", [P, 1]), sb("a_normw", [P, 1])
        itemp, tscr = sb("a_itemp", [P, 1]), sb("a_tscr", [P, 2])
        blk = sb("a_blk", [P, P])
        masks = sb("a_masks", [P, 8, CH])
        sel = sb("a_sel", [P, 4, 3, P])
        stm = sb("a_stm", [P, 3])
        psel = sb("a_psel", [16, 4, P])
        loads = [(w[n][:, :], dram[n]) for n in w] + [
            (cw[:, :, :], dram["cw"]), (firs[:, :], dram["firs"]), (firl[:, :], dram["firl"]),
            (mlp1b[:, :], dram["mlp1b"]), (mlp2T[:, :], dram["mlp2T"]), (mlp2b[:, :], dram["mlp2b"]),
            (ltemp[:, :], dram["ltemp"]), (cres[:, :], dram["cres"]), (normw[:, :], dram["normw"]),
            (blk[:, :], dram["blk32"]), (masks[:, :, :], dram["masks"]), (sel[:, :, :, :], dram["sel"]),
            (stm[:, :], dram["stm"]), (psel[:, :, :], dram["psel"])]
        xc, sq, rstd, hn = sb("xc", [P, T]), sb("sq", [P, T]), sb("rstd", [P, T]), sb("hn", [P, T])
        pad = [sb(f"pad{j}", [P, 3 + T]) for j in range(3)]
        acc = [sb(f"acc{j}", [P, T]) for j in range(3)]
        vpad = sb("vpad", [P, FIR_L - 1 + T])
        V = vpad[:, FIR_L - 1:]
        qn, kn, beta, kb, vb = (sb(n, [P, T]) for n in ("qn", "kn", "beta", "kb", "vb"))
        kR, kbR, vbR = (sb(n, [P, T]) for n in ("kR", "kbR", "vbR"))
        M, MT, LT, AT, Xi, Zi, Y = (sb(n, [P, T]) for n in ("M", "MT", "LT", "AT", "Xi", "Zi", "Y"))
        U, WT, UA, S = sb("U", [P, T]), sb("WT", [P, T]), sb("UA", [P, CH]), sb("S", [P, D0])
        SH, LO, DE = sb("SH", [P, T]), sb("LO", [P, T]), sb("DE", [P, T])
        ab, sqr = sb("ab", [P, 4, T]), sb("sqr", [P, 4, T])
        st, h1 = sb("st", [P, T]), sb("h1", [P, 4, T])
        lg, pr, r16, m16 = sb("lg", [P, 64]), sb("pr", [P, 64]), sb("r16", [P, 16]), sb("m16", [P, 16])
        pT = sb("pT", [16, T])
        o = sb("o", [P, T])
        mod = sb("mod", [P, 6])

        def c3(a):
            return a.rearrange("p (n c) -> p n c", c=CH)

        def mask(j):
            return masks[:, j:j + 1, :].broadcast_to([P, NCH, CH])

        def setup(block, i, s):
            @block.sync
            def _(sp):
                for tile, src in loads:
                    sp.dma_start(tile, src).then_inc(s["w_in"], 16)

            @block.gpsimd
            def _(pool):
                pool.memset(vpad[:, 0:FIR_L - 1], 0.0).then_inc(s["pool_done"], 1)
                for j in range(3):
                    pool.memset(pad[j][:, 0:3], 0.0).then_inc(s["pool_done"], 1)
                pool.wait_ge(s["pool_done"], 4)

            @block.scalar
            def _(act):
                act.wait_ge(s["w_in"], 16 * len(loads))
                step = Chain(act, s["act_step"])
                step(act.activation(cres[:, :], cres[:, :], ACT.Sigmoid))
                step(act.activation(tscr[:, 0:1], ltemp[:, :], ACT.Abs))
                step(act.activation(tscr[:, 0:1], tscr[:, 0:1], ACT.Exp, scale=-1.0))
                step(act.activation(tscr[:, 0:1], tscr[:, 0:1], ACT.Ln, bias=1.0))

            @block.vector
            def _(dve):
                dve.wait_ge(s["act_step"], 4)
                step = Chain(dve, s["dve_step"])
                step(dve.scalar_tensor_tensor(tscr[:, 1:2], ltemp[:, :], 0.0, tscr[:, 0:1], ALU.max, ALU.add))
                step(dve.reciprocal(itemp[:, :], tscr[:, 1:2]))

        stage(nc, "w_in pool_done act_step dve_step", 1, setup)

        def body(block, b, s):
            xb = X[:, ds(b, 1), :].rearrange("p a t -> p (a t)")

            @block.tensor
            def _(pe):
                ln_tensor(pe, s, xb, mean_w[:, :], sq[:, :], PS[:, 0, :], PS[:, 1, :])
                pe.wait_ge(s["ln_out"], 1)
                for j, n in enumerate(("qwT", "kwT", "vwT", "bwT")):
                    pe.matmul(PS[:, 2 + j, :], w[n][:, :], hn[:, :], start=True, stop=True).then_inc(s["proj"], 1)
                for j in range(2):
                    pe.wait_ge(s["qk_sq"], j + 1)
                    pe.matmul(PS[:, j, :], blk[:, :], sqr[:, j, :], start=True, stop=True).then_inc(s["qk_ss"], 1)

                def blocks(bank, a, c, done):
                    for n in range(NCH):
                        for h in range(H0):
                            r, f = slice(32 * h, 32 * h + 32), slice(CH * n, CH * n + CH)
                            mm = pe.matmul(PS[r, bank, f], a[r, f], c[r, f], start=True, stop=True,
                                           tile_position=(32 * h, 32 * h))
                    mm.then_inc(done, 1)

                pe.wait_ge(s["kb_ready"], 3)
                blocks(2, kb, kn, s["mm_M"])
                blocks(3, kn, qn, s["mm_AT"])
                for lev in range(4):
                    pe.wait_ge(s["inv_in"], lev + 1)
                    blocks(4, LT, Xi, s["mm_Y"])
                    pe.wait_ge(s["y_ready"], lev + 1)
                    if lev < 3:
                        blocks(5, Zi, Y, s["mm_XY"])
                    else:
                        blocks(5, Y, Zi, s["mm_XY"])
                pe.wait_ge(s["inv_out"], 1)
                blocks(6, Zi, vbR, s["mm_u"])
                blocks(7, kbR, Zi, s["mm_w"])
                pe.wait_ge(s["uw_ready"], 2)
                for n in range(NCH):
                    f = slice(CH * n, CH * n + CH)
                    pe.wait_ge(s["state"], n + 1)
                    for h in range(H0):
                        r = slice(32 * h, 32 * h + 32)
                        mm = pe.matmul(PS[r, 2, 0:D0], WT[r, f], S[r, :], start=True, stop=True,
                                       tile_position=(32 * h, 32 * h))
                    mm.then_inc(s["mm_ws"], 1)
                    for h in range(H0):
                        r = slice(32 * h, 32 * h + 32)
                        mm = pe.matmul(PS[r, 3, f], qn[r, f], S[r, :], start=True, stop=False,
                                       tile_position=(32 * h, 32 * h))
                    pe.wait_ge(s["ua_ready"], n + 1)
                    for h in range(H0):
                        r = slice(32 * h, 32 * h + 32)
                        mm = pe.matmul(PS[r, 4, 0:D0], kR[r, f], UA[r, :], start=True, stop=True,
                                       tile_position=(32 * h, 32 * h))
                    mm.then_inc(s["mm_ds"], 1)
                    for h in range(H0):
                        r = slice(32 * h, 32 * h + 32)
                        mm = pe.matmul(PS[r, 3, f], AT[r, f], UA[r, :], start=False, stop=True,
                                       tile_position=(32 * h, 32 * h))
                    mm.then_inc(s["mm_out"], 1)
                pe.wait_ge(s["src_ready"], 4)
                src = (SH, LO, DE, V)
                for k in range(4):
                    pe.wait_ge(s["src_abs"], k + 1)
                    pe.matmul(PS[:, 0, :], sel[:, k, 0, :], src[k][:, :], start=(k == 0), stop=False)
                    mm = pe.matmul(PS[:, 0, :], sel[:, k, 1, :], ab[:, k, :], start=False, stop=(k == 3))
                mm.then_inc(s["mm_stat"], 1)
                for k in range(4):
                    pe.wait_ge(s["src_sq"], k + 1)
                    mm = pe.matmul(PS[:, 1, :], sel[:, k, 2, :], sqr[:, k, :], start=(k == 0), stop=(k == 3))
                mm.then_inc(s["mm_stat"], 1)
                pe.wait_ge(s["stat_ready"], 1)
                for h in range(H0):
                    r = slice(32 * h, 32 * h + 32)
                    pe.matmul(PS[:, 4 + h, :], w["mlp1h"][:, :], hn[:, :], start=True, stop=False)
                    pe.matmul(PS[:, 4 + h, :], w["mlp1s"][r, :], st[r, :], start=False, stop=True,
                              tile_position=(32 * h, 0)).then_inc(s["mm_h1"], 1)
                for h in range(H0):
                    pe.wait_ge(s["h1_ready"], h + 1)
                    for t in range(4):
                        mm = pe.matmul(PS[:, 2, t * 16 + h * 4:t * 16 + h * 4 + 4],
                                       h1[:, h, t * P:(t + 1) * P], mlp2T[:, :], start=True, stop=True)
                mm.then_inc(s["mm_lg"], 1)
                pe.wait_ge(s["p_ready"], 1)
                for t in range(4):
                    mm = pe.transpose(PS[0:16, 3, t * P:(t + 1) * P], pr[:, t * 16:(t + 1) * 16], ident[:, :])
                mm.then_inc(s["mm_pT"], 1)
                pe.wait_ge(s["pT_ready"], 1)
                for k in range(4):
                    pe.matmul(PS[:, 4 + k, :], psel[:, k, :], pT[:, :], start=True, stop=True).then_inc(s["mm_P"], 1)
                pe.wait_ge(s["o_sq"], 1)
                pe.matmul(PS[:, 0, :], blk[:, :], sq[:, :], start=True, stop=True).then_inc(s["mm_oss"], 1)
                pe.wait_ge(s["o_ready"], 1)
                pe.matmul(PS[:, 1, :], w["owT"][:, :], o[:, :], start=True, stop=True).then_inc(s["mm_fin"], 1)

            @block.scalar
            def _(act):
                ln_scalar(act, s, xc[:, :], sq[:, :], PS[:, 1, :], rstd[:, :], eps[:, 0:1])
                for j in range(3):
                    act.wait_ge(s["proj"], j + 1)
                    act.activation(pad[j][:, 3:], PS[:, 2 + j, :], ACT.Copy).then_inc(s["pad_ready"], 1)
                act.wait_ge(s["proj"], 4)
                act.activation(beta[:, :], PS[:, 5, :], ACT.Sigmoid).then_inc(s["beta_raw"], 1)
                for j in range(3):
                    act.wait_ge(s["conv"], j + 1)
                    act.activation((qn[:, :], kn[:, :], V)[j], acc[j][:, :], ACT.Silu).then_inc(s["silu"], 1)
                for j in range(2):
                    act.wait_ge(s["silu"], j + 1)
                    act.activation(sqr[:, j, :], (qn, kn)[j][:, :], ACT.Square).then_inc(s["qk_sq"], 1)
                for j in range(2):
                    act.wait_ge(s["qk_ss"], j + 1)
                    act.activation(ab[:, j, :], PS[:, j, :], ACT.Ln, bias=eps[:, 1:2]).then_inc(s["rn_log"], 1)
                for j in range(2):
                    act.wait_ge(s["rn_log"], j + 1)
                    act.activation(ab[:, j, :], ab[:, j, :], ACT.Exp, scale=-0.5).then_inc(s["rn"], 1)
                act.wait_ge(s["mm_u"], 1)
                act.activation(U[:, :], PS[:, 6, :], ACT.Copy).then_inc(s["uw_ready"], 1)
                act.wait_ge(s["mm_w"], 1)
                act.activation(WT[:, :], PS[:, 7, :], ACT.Copy).then_inc(s["uw_ready"], 1)
                act.wait_ge(s["src_ready"], 4)
                for k, a in enumerate((SH[:, :], LO[:, :], DE[:, :], V)):
                    act.activation(ab[:, k, :], a, ACT.Abs).then_inc(s["src_abs"], 1)
                for k, a in enumerate((SH[:, :], LO[:, :], DE[:, :], V)):
                    act.activation(sqr[:, k, :], a, ACT.Square).then_inc(s["src_sq"], 1)
                act.wait_ge(s["mm_stat"], 2)
                act.activation(st[:, :], PS[:, 1, :], ACT.Sqrt, scale=stm[:, 2:3]).then_inc(s["stat_sqrt"], 1)
                for h in range(H0):
                    act.wait_ge(s["mm_h1"], h + 1)
                    act.activation(h1[:, h, :], PS[:, 4 + h, :], ACT.Gelu_apprx_tanh, bias=mlp1b[:, 0:1])\
                       .then_inc(s["h1_ready"], 1)
                act.wait_ge(s["lg_ready"], 1)
                act.activation(pr[:, :], lg[:, :], ACT.Exp, scale=itemp[:, 0:1]).then_inc(s["lg_exp"], 1)
                act.wait_ge(s["mm_pT"], 1)
                act.activation(pT[:, :], PS[0:16, 3, :], ACT.Copy).then_inc(s["pT_ready"], 1)
                act.wait_ge(s["o_mix"], 1)
                act.activation(sq[:, :], o[:, :], ACT.Square).then_inc(s["o_sq"], 1)
                act.wait_ge(s["mm_oss"], 1)
                act.activation(rstd[:, :], PS[:, 0, :], ACT.Ln, bias=eps[:, 0:1], scale=1.0 / D0).then_inc(s["o_log"], 1)
                act.wait_ge(s["o_log"], 1)
                act.activation(rstd[:, :], rstd[:, :], ACT.Exp, scale=-0.5).then_inc(s["o_rstd"], 1)

            @block.vector
            def _(dve):
                step = Chain(dve, s["dve_step"])
                step(dve.tensor_copy(mod[:, :], MOD[:, ds(b, 1), :].rearrange("p a j -> p (a j)")))
                ln_vector(dve, s, xb, xc[:, :], PS[:, 0, :], rstd[:, :], mod[:, 1:2], mod[:, 0:1], hn[:, :])
                for j in range(3):
                    dve.wait_ge(s["pad_ready"], j + 1)
                    step(dve.tensor_scalar(acc[j][:, :], pad[j][:, 3:3 + T], cw[:, j, 3:4], None, ALU.mult))
                    for k in range(3):
                        ins = dve.scalar_tensor_tensor(acc[j][:, :], pad[j][:, k:k + T], cw[:, j, k:k + 1],
                                                       acc[j][:, :], ALU.mult, ALU.add)
                        if k < 2:
                            step(ins)
                    ins.then_inc(s["conv"], 1)
                dve.wait_ge(s["beta_raw"], 1)
                step(dve.tensor_scalar(beta[:, :], beta[:, :], 1e-6, None, ALU.max))
                dve.wait_ge(s["silu"], 3)
                step(dve.tensor_tensor(vb[:, :], V, beta[:, :], ALU.mult))
                dve.wait_ge(s["rn"], 2)
                step(dve.tensor_tensor(kn[:, :], kn[:, :], ab[:, 1, :], ALU.mult))
                dve.tensor_tensor(qn[:, :], qn[:, :], ab[:, 0, :], ALU.mult).then_inc(s["kb_ready"], 1)
                dve.tensor_tensor(kb[:, :], kn[:, :], beta[:, :], ALU.mult).then_inc(s["kb_ready"], 1)
                dve.wait_ge(s["kb_ready"], 2)
                dve.transpose(kR[:, :], kn[:, :]).then_inc(s["kb_ready"], 1)
                step(dve.transpose(vbR[:, :], vb[:, :]))
                step(dve.transpose(kbR[:, :], kb[:, :]))
                dve.wait_ge(s["mm_M"], 1)
                step(dve.tensor_tensor(c3(M[:, :]), c3(PS[:, 2, :]), mask(0), ALU.mult))
                step(dve.transpose(MT[:, :], M[:, :]))
                dve.wait_ge(s["mm_AT"], 1)
                step(dve.tensor_tensor(c3(AT[:, :]), c3(PS[:, 3, :]), mask(1), ALU.mult))
                step(dve.tensor_tensor(c3(M[:, :]), c3(M[:, :]), mask(3), ALU.mult))
                step(dve.tensor_tensor(c3(Xi[:, :]), mask(2), c3(M[:, :]), ALU.subtract))
                for lev in range(4):
                    step(dve.transpose(Zi[:, :], Xi[:, :]))
                    dve.tensor_tensor(c3(LT[:, :]), c3(MT[:, :]), mask(4 + lev), ALU.mult).then_inc(s["inv_in"], 1)
                    dve.wait_ge(s["mm_Y"], lev + 1)
                    dve.tensor_copy(Y[:, :], PS[:, 4, :]).then_inc(s["y_ready"], 1)
                    dve.wait_ge(s["mm_XY"], lev + 1)
                    if lev < 3:
                        step(dve.tensor_tensor(Xi[:, :], Xi[:, :], PS[:, 5, :], ALU.subtract))
                    else:
                        dve.tensor_tensor(Zi[:, :], Zi[:, :], PS[:, 5, :], ALU.subtract).then_inc(s["inv_out"], 1)
                dve.memset(S[:, :], 0.0).then_inc(s["state"], 1)
                taps = [(SH, firs, FIR_S, k) for k in range(FIR_S)] + [(LO, firl, FIR_L, k) for k in range(FIR_L)]

                def tap():
                    if taps:
                        dst, f, K, k = taps.pop(0)
                        src = vpad[:, FIR_L - K + k:FIR_L - K + k + T]
                        if k == 0:
                            step(dve.tensor_scalar(dst[:, :], src, f[:, 0:1], None, ALU.mult))
                        else:
                            step(dve.scalar_tensor_tensor(dst[:, :], src, f[:, k:k + 1], dst[:, :],
                                                          ALU.mult, ALU.add))
                dve.wait_ge(s["uw_ready"], 2)
                for n in range(NCH):
                    f = slice(CH * n, CH * n + CH)
                    tap()
                    dve.wait_ge(s["mm_ws"], n + 1)
                    if n:
                        dve.wait_ge(s["mm_out"], n)
                    dve.tensor_tensor(UA[:, :], U[:, f], PS[:, 2, 0:D0], ALU.subtract).then_inc(s["ua_ready"], 1)
                    tap()
                    tap()
                    dve.wait_ge(s["mm_ds"], n + 1)
                    dve.wait_ge(s["state"], n + 1)
                    dve.tensor_tensor(S[:, :], S[:, :], PS[:, 4, 0:D0], ALU.add).then_inc(s["state"], 1)
                    tap()
                    tap()
                while taps:
                    tap()
                dve.wait_ge(s["mm_out"], NCH)
                dve.transpose(DE[:, :], PS[:, 3, :]).then_inc(s["src_ready"], 4)
                dve.wait_ge(s["mm_stat"], 2)
                step(dve.tensor_copy(o[:, :], PS[:, 0, :]))
                step(dve.scalar_tensor_tensor(sq[:, :], o[:, :], stm[:, 1:2], o[:, :], ALU.mult, ALU.mult))
                dve.wait_ge(s["stat_sqrt"], 1)
                step(dve.scalar_tensor_tensor(sq[:, :], PS[:, 1, :], stm[:, 1:2], sq[:, :], ALU.mult, ALU.subtract))
                step(dve.scalar_tensor_tensor(sq[:, :], o[:, :], stm[:, 0:1], sq[:, :], ALU.mult, ALU.add))
                dve.tensor_tensor(st[:, :], st[:, :], sq[:, :], ALU.add).then_inc(s["stat_ready"], 1)
                dve.wait_ge(s["mm_lg"], 1)

                def g4(a):
                    return a.rearrange("p (g k) -> p g k", k=4)

                def bc(a):
                    return a.rearrange("p (g k) -> p g k", k=1).broadcast_to([P, 16, 4])
                step(dve.tensor_tensor(g4(lg[:, :]), g4(PS[:, 2, 0:64]),
                                       mlp2b[:, :].rearrange("p (g k) -> p g k", g=1).broadcast_to([P, 16, 4]), ALU.add))
                step(dve.tensor_reduce(m16[:, :], g4(lg[:, :]), AX, ALU.max))
                dve.tensor_tensor(g4(lg[:, :]), g4(lg[:, :]), bc(m16[:, :]), ALU.subtract).then_inc(s["lg_ready"], 1)
                dve.wait_ge(s["lg_exp"], 1)
                step(dve.tensor_reduce(m16[:, :], g4(pr[:, :]), AX, ALU.add))
                step(dve.reciprocal(r16[:, :], m16[:, :]))
                step(dve.tensor_tensor(g4(pr[:, :]), g4(pr[:, :]), bc(r16[:, :]), ALU.mult))
                step(dve.tensor_scalar(pr[:, :], pr[:, :], PROB_FLOOR, None, ALU.max))
                step(dve.tensor_reduce(m16[:, :], g4(pr[:, :]), AX, ALU.add))
                step(dve.reciprocal(r16[:, :], m16[:, :]))
                dve.tensor_tensor(g4(pr[:, :]), g4(pr[:, :]), bc(r16[:, :]), ALU.mult).then_inc(s["p_ready"], 1)
                dve.wait_ge(s["mm_P"], 1)
                step(dve.scalar_tensor_tensor(o[:, :], PS[:, 4, :], cres[:, 0:1], SH[:, :], ALU.add, ALU.mult))
                for k, a in ((1, LO[:, :]), (2, DE[:, :]), (3, V)):
                    dve.wait_ge(s["mm_P"], k + 1)
                    step(dve.tensor_tensor(xc[:, :], a, PS[:, 4 + k, :], ALU.mult))
                    ins = dve.tensor_tensor(o[:, :], o[:, :], xc[:, :], ALU.add)
                    if k < 3:
                        step(ins)
                ins.then_inc(s["o_mix"], 1)
                dve.wait_ge(s["o_rstd"], 1)
                dve.scalar_tensor_tensor(o[:, :], o[:, :], normw[:, 0:1], rstd[:, :], ALU.mult, ALU.mult)\
                   .then_inc(s["o_ready"], 1)
                dve.wait_ge(s["mm_fin"], 1)
                dve.scalar_tensor_tensor(xb, PS[:, 1, :], mod[:, 2:3], xb, ALU.mult, ALU.add).then_inc(s["dve_step"], 1)

        stage(nc, LN_SEMS + "proj pad_ready beta_raw conv silu qk_sq qk_ss rn_log rn kb_ready mm_M mm_AT inv_in "
              "mm_Y y_ready mm_XY inv_out mm_u mm_w uw_ready state mm_ws ua_ready mm_ds mm_out src_ready src_abs "
              "src_sq mm_stat stat_sqrt stat_ready mm_h1 h1_ready mm_lg lg_ready lg_exp p_ready mm_pT pT_ready mm_P "
              "o_mix o_sq mm_oss o_log o_rstd o_ready mm_fin dve_step", NB, body)


def experts_stage(nc, dram, g, PS):
    X, MOD, eps, mean_w, ident = g.X, g.MOD0, g.eps, g.mean_w, g.ident
    NE = 8
    with ExitStack() as ctx:
        def sb(n, shape):
            return ctx.enter_context(nc.sbuf_tensor("moe_" + n, shape, F32))
        w1, w2 = sb("m_w1", [P, NE + 1, P]), sb("m_w2", [P, NE + 1, P])
        gw, lb, tri, esel = sb("m_gw", [P, NE]), sb("m_lb", [P, NE]), sb("m_tri", [P, NE, NE]), sb("m_esel", [NE, NE, P])
        xc, sq, rstd, hn = sb("xc", [P, T]), sb("sq", [P, T]), sb("rstd", [P, T]), sb("hn", [P, T])
        lgt, lgb, sg = sb("lgt", [P, 4, NE]), sb("lgb", [P, 4, NE]), sb("sg", [P, 4, NE])
        gt, eq = sb("gt", [P, 4, NE, NE]), sb("eq", [P, 4, NE, NE])
        cnt, ws, wr = sb("cnt", [P, 4, NE]), sb("ws", [P, 4]), sb("wr", [P, 4])
        weT = sb("weT", [NE, T])
        relu, act2, hid = sb("relu", [P, 2, T]), sb("act2", [P, 2, T]), sb("hid", [P, 2, T])
        mod = sb("mod", [P, 6])
        loads = [(w1[:, :, :], dram["w1"]), (w2[:, :, :], dram["w2"]), (gw[:, :], dram["gate_wT"]),
                 (lb[:, :], dram["lb_bias"]), (tri[:, :, :], dram["tri8"]), (esel[:, :, :], dram["esel"])]

        def setup(block, i, s):
            @block.sync
            def _(sp):
                for tile, src in loads:
                    sp.dma_start(tile, src).then_inc(s["w_in"], 16)
                sp.wait_ge(s["w_in"], 16 * len(loads))
        stage(nc, "w_in", 1, setup)

        def body(block, b, s):
            xb = X[:, ds(b, 1), :].rearrange("p a t -> p (a t)")

            @block.tensor
            def _(pe):
                ln_tensor(pe, s, xb, mean_w[:, :], sq[:, :], PS[:, 0, :], PS[:, 1, :])
                pe.wait_ge(s["ln_out"], 1)
                for t in range(4):
                    mm = pe.matmul(PS[:, 2, t * NE:(t + 1) * NE], hn[:, t * P:(t + 1) * P], gw[:, :],
                                   start=True, stop=True)
                mm.then_inc(s["mm_lg"], 1)

                def up(e):
                    if e >= 2:
                        pe.wait_ge(s["act_relu"], e - 1)
                    pe.matmul(PS[:, 4 + e % 2, :], w1[:, e, :], hn[:, :], start=True, stop=True).then_inc(s["mm_up"], 1)

                def spread(e):
                    if e >= 2:
                        pe.wait_ge(s["hid_ready"], e - 1)
                    pe.matmul(PS[:, 6 + e % 2, :], esel[:, e, :], weT[:, :], start=True, stop=True).then_inc(s["mm_we"], 1)

                def down(e):
                    if e < NE:
                        pe.wait_ge(s["hid_ready"], e + 1)
                    else:
                        pe.wait_ge(s["act_sq"], e + 1)
                    rhs = hid[:, e % 2, :] if e < NE else act2[:, e % 2, :]
                    pe.matmul(PS[:, 1, :], w2[:, e, :], rhs, start=(e == 0), stop=(e == NE)).then_inc(s["mm_down"], 1)
                up(0)
                up(1)
                pe.wait_ge(s["we_ready"], 1)
                for t in range(4):
                    mm = pe.transpose(PS[0:NE, 3, t * P:(t + 1) * P], cnt[:, t, :], ident[:, :])
                mm.then_inc(s["mm_weT"], 1)
                pe.wait_ge(s["weT_ready"], 1)
                spread(0)
                for e in range(NE + 1):
                    if e + 2 <= NE:
                        up(e + 2)
                    if e + 1 < NE:
                        spread(e + 1)
                    down(e)

            @block.scalar
            def _(act):
                ln_scalar(act, s, xc[:, :], sq[:, :], PS[:, 1, :], rstd[:, :], eps[:, 0:1])
                act.wait_ge(s["lg_ready"], 1)
                act.activation(sg[:, :, :], lgt[:, :, :], ACT.Sigmoid).then_inc(s["sig_ready"], 1)
                act.wait_ge(s["mm_weT"], 1)
                act.activation(weT[:, :], PS[0:NE, 3, :], ACT.Copy).then_inc(s["weT_ready"], 1)
                for e in range(NE + 1):
                    act.wait_ge(s["mm_up"], e + 1)
                    act.activation(relu[:, e % 2, :], PS[:, 4 + e % 2, :], ACT.Relu).then_inc(s["act_relu"], 1)
                    act.wait_ge(s["act_relu"], e + 1)
                    if e >= 2:
                        act.wait_ge(s["hid_ready"], e - 1)
                    act.activation(act2[:, e % 2, :], relu[:, e % 2, :], ACT.Square).then_inc(s["act_sq"], 1)

            @block.vector
            def _(dve):
                step = Chain(dve, s["dve_step"])
                step(dve.tensor_copy(mod[:, :], MOD[:, ds(b, 1), :].rearrange("p a j -> p (a j)")))
                ln_vector(dve, s, xb, xc[:, :], PS[:, 0, :], rstd[:, :], mod[:, 4:5], mod[:, 3:4], hn[:, :])
                dve.wait_ge(s["mm_lg"], 1)
                dve.tensor_copy(lgt[:, :, :], PS[:, 2, 0:4 * NE].rearrange("p (t e) -> p t e", e=NE)).then_inc(s["lg_ready"], 1)
                dve.wait_ge(s["lg_ready"], 1)
                bias = lb[:, :].rearrange("p (t e) -> p t e", t=1).broadcast_to([P, 4, NE])
                step(dve.tensor_tensor(lgb[:, :, :], lgt[:, :, :], bias, ALU.add))
                other = lgb[:, :, :].rearrange("p t (a e) -> p t a e", a=1).broadcast_to([P, 4, NE, NE])
                own = lgb[:, :, :].rearrange("p t (e a) -> p t e a", a=1).broadcast_to([P, 4, NE, NE])
                below = tri[:, :, :].rearrange("p (a e) f -> p a e f", a=1).broadcast_to([P, 4, NE, NE])
                step(dve.tensor_tensor(gt[:, :, :, :], other, own, ALU.is_gt))
                step(dve.tensor_tensor(eq[:, :, :, :], other, own, ALU.is_equal))
                step(dve.tensor_tensor(eq[:, :, :, :], eq[:, :, :, :], below, ALU.mult))
                step(dve.tensor_tensor(gt[:, :, :, :], gt[:, :, :, :], eq[:, :, :, :], ALU.add))
                step(dve.tensor_reduce(cnt[:, :, :], gt[:, :, :, :], AX, ALU.add))
                dve.wait_ge(s["sig_ready"], 1)
                step(dve.scalar_tensor_tensor(cnt[:, :, :], cnt[:, :, :], 1.5, sg[:, :, :], ALU.is_lt, ALU.mult))
                step(dve.tensor_reduce(ws[:, :], cnt[:, :, :], AX, ALU.add))
                step(dve.tensor_scalar(ws[:, :], ws[:, :], 1e-6, None, ALU.add))
                step(dve.reciprocal(wr[:, :], ws[:, :]))
                wrb = wr[:, :].rearrange("p (t a) -> p t a", a=1).broadcast_to([P, 4, NE])
                dve.tensor_tensor(cnt[:, :, :], cnt[:, :, :], wrb, ALU.mult).then_inc(s["we_ready"], 1)
                for e in range(NE):
                    dve.wait_ge(s["act_sq"], e + 1)
                    dve.wait_ge(s["mm_we"], e + 1)
                    if e >= 2:
                        dve.wait_ge(s["mm_down"], e - 1)
                    dve.tensor_tensor(hid[:, e % 2, :], act2[:, e % 2, :], PS[:, 6 + e % 2, :], ALU.mult)\
                       .then_inc(s["hid_ready"], 1)
                dve.wait_ge(s["mm_down"], NE + 1)
                dve.scalar_tensor_tensor(xb, PS[:, 1, :], mod[:, 5:6], xb, ALU.mult, ALU.add).then_inc(s["dve_step"], 1)

        stage(nc, LN_SEMS + "mm_lg mm_up mm_we mm_down mm_weT weT_ready we_ready act_relu act_sq hid_ready "
              "lg_ready sig_ready dve_step", NB, body)


H1, D1 = 16, 8
TOPK = T // 4
TAKEN = -1e30
GH = 2
NT = 4 * GH
NG = H1 // GH
COUNTS = 5
ACT_COUNTS = 2
AIM = TOPK - 4.3
Z0, SLOPE, REACH = 0.697, 0.313 * T, 0.8


def topk_attention_stage(nc, dram, g, PS):
    X, MOD, eps, mean_w, ident = g.X, g.MOD1, g.eps, g.mean_w, g.ident
    with ExitStack() as ctx:
        def sb(n, shape, dt=F32):
            return ctx.enter_context(nc.sbuf_tensor("topk_" + n, shape, dt))
        w = {n: sb("t_" + n, [P, P]) for n in ("Wq", "Wk", "Wv", "Wo", "Wg", "blk8", "bv")}
        col = {n: sb("t_" + n, [P, 1]) for n in ("bq", "bk", "bo", "bg", "bt", "Wt")}
        hm, rank, ones = sb("hm", [P, H1]), sb("rank", [P, 8]), sb("ones", [P, 1])
        loads = [(w[n][:, :], dram["t_" + n]) for n in w] + [(col[n][:, :], dram["t_" + n]) for n in col]
        loads += [(hm[:, :], dram["hm"]), (rank[:, :], dram["rank"])]
        xc, sq, rstd, hn = sb("xc", [P, T]), sb("sq", [P, T]), sb("rstd", [P, T]), sb("hn", [P, T])
        qk, qks, gate = sb("qk", [P, 2, T]), sb("qks", [P, 2, T]), sb("gate", [P, T])
        Vt, OUT, OT = sb("Vt", [P, 4, H1, D1 + 1]), sb("OUT", [P, 4, H1, D1]), sb("OT", [P, T])
        hsum, itemp, kbm = sb("hsum", [P, 2]), sb("itemp", [P, 2]), sb("kbm", [P, H1])
        qm = sb("qm", [P, 2, T])
        NC_ = H1 * 4
        tc, lo, hi, dif = (sb(n, [P, 2, NC_]) for n in ("tc", "lo", "hi", "dif"))
        mean, sd, signs, rec = (sb(n, [P, NC_]) for n in ("mean", "sd", "signs", "rec"))
        up, dn = sb("up", [P, NC_], mybir.dt.int32), sb("dn", [P, NC_], mybir.dt.int32)
        S, E, W = sb("S", [P, 3 * NT, T]), sb("E", [P, 3 * NT, T]), sb("W", [P, 2 * NT, T])
        above, junk = sb("above", [P, 2, T], mybir.dt.bfloat16), sb("junk", [P, 4, T], mybir.dt.bfloat16)
        m8, keep, bad = sb("m8", [P, NT, 8]), sb("keep", [P, NT, 8]), sb("bad", [P, 2, NT])
        nbad = sb("nbad", [1, NT + 1], mybir.dt.int32)
        nbad_sum = sb("nbad_sum", [1, 1])
        prec = sb("prec", [P, NT])
        PT = sb("PT", [P, 2, T])
        mod = sb("mod", [P, 6])

        def setup(block, i, s):
            @block.sync
            def _(sp):
                for tile, src in loads:
                    sp.dma_start(tile, src).then_inc(s["w_in"], 16)
                sp.wait_ge(s["w_in"], 16 * len(loads))

            @block.gpsimd
            def _(pool):
                pool.memset(Vt[:, :, :, D1:], 1.0).then_inc(s["ones"], 1)
                pool.wait_ge(s["ones"], 1)
                pool.memset(ones[:, :], 1.0).then_inc(s["ones"], 1)
                pool.wait_ge(s["ones"], 2)
        stage(nc, "w_in ones", 1, setup)

        def project(block, b, s):
            xb = X[:, ds(b, 1), :].rearrange("p a t -> p (a t)")

            @block.tensor
            def _(pe):
                ln_tensor(pe, s, xb, mean_w[:, :], sq[:, :], PS[:, 0, :], PS[:, 1, :])
                pe.wait_ge(s["ln_out"], 1)
                for j, n in enumerate(("Wq", "Wk", "Wg")):
                    pe.matmul(PS[:, 2 + j, :], w[n][:, :], hn[:, :], start=True, stop=True).then_inc(s["mm_proj"], 1)
                for t in range(4):
                    mm = pe.matmul(PS[:, 5, t * P:(t + 1) * P], hn[:, t * P:(t + 1) * P], w["Wv"][:, :],
                                   start=True, stop=True)
                mm.then_inc(s["mm_v"], 1)
                for j in range(2):
                    pe.wait_ge(s["qk_sq"], j + 1)
                    pe.matmul(PS[:, j, :], w["blk8"][:, :], qks[:, j, :], start=True, stop=True).then_inc(s["mm_ss"], 1)
                pe.wait_ge(s["mean_ready"], 1)
                pe.matmul(PS[:, 6, 0:1], hsum[:, 0:1].broadcast_to([P, P]), col["Wt"][:, :], start=True, stop=True)\
                  .then_inc(s["mm_temp"], 1)
                pe.wait_ge(s["qk_norm"], 2)
                for t in range(4):
                    mm = pe.transpose(PS[:, 2, t * P:(t + 1) * P], qk[:, 1, t * P:(t + 1) * P], ident[:, :])
                mm.then_inc(s["mm_kT"], 1)
                pe.wait_ge(s["kT_ready"], 1)
                for t in range(4):
                    mm = pe.matmul(PS[:, 3, 0:P], sq[:, t * P:(t + 1) * P], sq[:, t * P:(t + 1) * P],
                                   start=(t == 0), stop=(t == 3))
                mm.then_inc(s["mm_C"], 1)
                pe.wait_ge(s["C_ready"], 1)
                pe.matmul(PS[:, 4, :], rstd[:, 0:P], qk[:, 0, :], start=True, stop=True).then_inc(s["mm_CQ"], 1)
                pe.wait_ge(s["qcq_ready"], 1)
                for t in range(4):
                    tt = slice(t * P, (t + 1) * P)
                    pe.matmul(PS[:, 7, t * H1:(t + 1) * H1], qk[:, 0, tt], kbm[:, :], start=True, stop=True)
                    mm = pe.matmul(PS[:, 7, (4 + t) * H1:(5 + t) * H1], xc[:, tt], hm[:, :], start=True, stop=True)
                mm.then_inc(s["mm_mom"], 1)

            @block.scalar
            def _(act):
                ln_scalar(act, s, xc[:, :], sq[:, :], PS[:, 1, :], rstd[:, :], eps[:, 0:1])
                for j, n in enumerate(("bq", "bk")):
                    act.wait_ge(s["mm_proj"], j + 1)
                    act.activation(qk[:, j, :], PS[:, 2 + j, :], ACT.Identity, bias=col[n][:, 0:1]).then_inc(s["qk_ready"], 1)
                for j in range(2):
                    act.wait_ge(s["qk_ready"], j + 1)
                    act.activation(qks[:, j, :], qk[:, j, :], ACT.Square).then_inc(s["qk_sq"], 1)
                act.wait_ge(s["mm_proj"], 3)
                act.activation(gate[:, :], PS[:, 4, :], ACT.Sigmoid, bias=col["bg"][:, 0:1]).then_inc(s["gate_ready"], 1)
                act.wait_ge(s["mm_temp"], 1)
                act.activation(itemp[:, 0:1], PS[:, 6, 0:1], ACT.Sigmoid, bias=col["bt"][:, 0:1], scale=1.0 / T)\
                   .then_inc(s["temp_sig"], 1)
                for j in range(2):
                    act.wait_ge(s["mm_ss"], j + 1)
                    act.activation(qks[:, j, :], PS[:, j, :], ACT.Sqrt).then_inc(s["norm_ready"], 1)
                act.wait_ge(s["mm_kT"], 1)
                act.activation(sq[:, :], PS[:, 2, :], ACT.Copy).then_inc(s["kT_ready"], 1)
                act.wait_ge(s["var_ready"], 1)
                act.activation(sd[:, :], sd[:, :], ACT.Sqrt).then_inc(s["sd_ready"], 1)

            @block.vector
            def _(dve):
                step = Chain(dve, s["dve_step"])
                step(dve.tensor_copy(mod[:, :], MOD[:, ds(b, 1), :].rearrange("p a j -> p (a j)")))
                ln_vector(dve, s, xb, xc[:, :], PS[:, 0, :], rstd[:, :], mod[:, 1:2], mod[:, 0:1], hn[:, :])
                dve.wait_ge(s["ln_out"], 1)
                dve.tensor_reduce(hsum[:, 0:1], hn[:, :], AX, ALU.add).then_inc(s["mean_ready"], 1)
                dve.wait_ge(s["mm_v"], 1)
                bv = w["bv"][:, :].rearrange("p (a h c) -> p a h c", a=1, c=D1).broadcast_to([P, 4, H1, D1])
                step(dve.tensor_tensor(Vt[:, :, :, 0:D1],
                                       PS[:, 5, :].rearrange("p (t h c) -> p t h c", t=4, c=D1), bv, ALU.add))
                dve.wait_ge(s["temp_sig"], 1)
                step(dve.tensor_scalar(itemp[:, 0:1], itemp[:, 0:1], 0.5, None, ALU.add))
                step(dve.reciprocal(itemp[:, 1:2], itemp[:, 0:1]))
                for j in range(2):
                    dve.wait_ge(s["norm_ready"], j + 1)
                    step(dve.tensor_scalar(qks[:, j, :], qks[:, j, :], 1e-12, None, ALU.max))
                    step(dve.reciprocal(qks[:, j, :], qks[:, j, :]))
                    sc = itemp[:, 1:2] if j == 0 else 1.0
                    dve.scalar_tensor_tensor(qk[:, j, :], qk[:, j, :], sc, qks[:, j, :], ALU.mult, ALU.mult)\
                       .then_inc(s["qk_norm"], 1)
                dve.wait_ge(s["qk_norm"], 2)
                step(dve.tensor_reduce(hsum[:, 1:2], qk[:, 1, :], AX, ALU.add))
                step(dve.tensor_scalar(kbm[:, :], hm[:, :], hsum[:, 1:2], 1.0 / T, ALU.mult, ALU.mult))
                dve.wait_ge(s["mm_C"], 1)
                dve.scalar_tensor_tensor(rstd[:, 0:P], PS[:, 3, 0:P], 1.0 / T, w["blk8"][:, :], ALU.mult, ALU.mult)\
                   .then_inc(s["C_ready"], 1)
                dve.wait_ge(s["mm_CQ"], 1)
                dve.tensor_tensor(xc[:, :], qk[:, 0, :], PS[:, 4, :], ALU.mult).then_inc(s["qcq_ready"], 1)
                dve.wait_ge(s["mm_mom"], 1)

                def by_head(bank_cols):
                    return bank_cols.rearrange("p (t h) -> p h t", t=4)
                h4 = "p (h t) -> p h t"
                step(dve.tensor_copy(mean[:, :].rearrange(h4, t=4), by_head(PS[:, 7, 0:4 * H1])))
                step(dve.tensor_tensor(rec[:, :], mean[:, :], mean[:, :], ALU.mult))
                step(dve.tensor_tensor(sd[:, :].rearrange(h4, t=4), by_head(PS[:, 7, 4 * H1:8 * H1]),
                                       rec[:, :].rearrange(h4, t=4), ALU.subtract))
                dve.tensor_scalar(sd[:, :], sd[:, :], 1e-12, None, ALU.max).then_inc(s["var_ready"], 1)
                dve.wait_ge(s["sd_ready"], 1)
                for tile, z, c in ((tc, Z0, 0.0), (lo, Z0 - REACH, AIM + REACH * SLOPE), (hi, Z0 + REACH, AIM - REACH * SLOPE)):
                    step(dve.scalar_tensor_tensor(tile[:, 0, :], sd[:, :], z, mean[:, :], ALU.mult, ALU.add))
                    step(dve.memset(tile[:, 1, :], c))

        def search(block, b, s):
            def S_(n):
                return S[:, n % (3 * NT), :]

            def E_(n):
                return E[:, n % (3 * NT), :]

            def W_(n):
                return W[:, n % (2 * NT), :]

            @block.tensor
            def _(pe):
                def score(n):
                    h, t = n // 4, n % 4
                    pe.wait_ge(s["q_ready"], h + 1)
                    if n >= 4:
                        pe.wait_ge(s["exp_ready"], n - 3)
                    pe.matmul(PS[:, n % 4, :], qm[:, h % 2, t * P:(t + 1) * P], qk[:, 1, :], start=True, stop=True)\
                      .then_inc(s["mm_score"], 1)

                def turn(n):
                    pe.wait_ge(s["p_ready"], n + 1)
                    if n >= 2:
                        pe.wait_ge(s["pT_ready"], n - 1)
                    for k in range(4):
                        mm = pe.transpose(PS[:, 4 + n % 2, k * P:(k + 1) * P], E_(n)[:, k * P:(k + 1) * P], ident[:, :])
                    mm.then_inc(s["mm_pT"], 1)

                def values(n):
                    gr, i = n // NT, n % NT
                    pe.wait_ge(s["pT_ready"], n + 1)
                    if i == 0 and gr >= 2:
                        pe.wait_ge(s["out_ready"], gr - 1)
                    for k in range(4):
                        mm = pe.matmul(PS[:, 6 + gr % 2, i * (D1 + 1):(i + 1) * (D1 + 1)],
                                       PT[:, n % 2, k * P:(k + 1) * P], Vt[:, k, n // 4, :],
                                       start=(k == 0), stop=(k == 3))
                    mm.then_inc(s["mm_pv"], 1)

                for n in range(2 * NT):
                    score(n)
                for gr in range(NG + 1):
                    if gr >= 1:
                        if gr >= 3:
                            pe.wait_ge(s["out_ready"], gr - 2)
                        pe.wait_ge(s["bad_ready"], gr)
                        pe.matmul(PS[0:1, 6 + (gr - 1) % 2, 128:128 + NT], ones[:, :],
                                  bad[:, (gr - 1) % 2, :],
                                  start=True, stop=True).then_inc(s["mm_bad"], 1)
                    for i in range(NT + 1):
                        if gr + 2 < NG and i < NT:
                            score((gr + 2) * NT + i)
                        if gr >= 1 and i < NT:
                            turn((gr - 1) * NT + i)
                        if gr >= 1 and i >= 1:
                            values((gr - 1) * NT + i - 1)

            @block.scalar
            def _(act):
                def load(n):
                    act.wait_ge(s["mm_score"], n + 1)
                    if n >= 3 * NT:
                        act.wait_ge(s["w_ready"], n // NT - 2)
                        act.wait_ge(s["mm_pT"], n - 3 * NT + 1)
                    act.activation(S_(n), PS[:, n % 4, :], ACT.Copy).then_inc(s["s_ready"], 1)
                    act.activation(E_(n), PS[:, n % 4, :], ACT.Exp).then_inc(s["exp_ready"], 1)

                def count(n, k):
                    if n % NT == 0 and k:
                        act.wait_ge(s["t_ready1"], n // NT + 1)
                    act.wait_ge(s["s_ready"], n + 1)
                    if n >= 2:
                        act.wait_ge(s["act_count%d" % k], n - 1)
                    act.activation(junk[:, 2 * k + n % 2, :], S_(n), ACT.Sign, bias=tc[:, 0, n:n + 1], scale=-1.0,
                                   accum_out=signs[:, n:n + 1]).then_inc(s["act_count%d" % k], 1)

                def rest(n):
                    act.wait_ge(s["w_ready"], n // NT + 1)
                    act.activation(W_(n), W_(n), ACT.Exp).then_inc(s["u_ready"], 1)

                def turned(n):
                    act.wait_ge(s["mm_pT"], n + 1)
                    if n >= 2:
                        act.wait_ge(s["mm_pv"], n - 1)
                    act.activation(PT[:, n % 2, :], PS[:, 4 + n % 2, :], ACT.Copy).then_inc(s["pT_ready"], 1)

                for n in range(NT):
                    load(n)
                    count(n, 0)
                for n in range(NT):
                    count(n, 1)
                for n in range(NT, 2 * NT):
                    load(n)
                    count(n, 0)
                for gr in range(NG + 1):
                    if gr + 1 < NG:
                        for n in range((gr + 1) * NT, (gr + 2) * NT):
                            count(n, 1)
                    for i in range(NT + 3):
                        if gr >= 1 and i < NT:
                            rest((gr - 1) * NT + i)
                        if gr >= 1 and 2 <= i < NT + 2:
                            turned((gr - 1) * NT + i - 2)
                        if gr + 2 < NG and i >= 3:
                            load((gr + 2) * NT + i - 3)
                            count((gr + 2) * NT + i - 3, 0)

            @block.gpsimd
            def _(pool):
                def mask_q(h):
                    if h >= 2:
                        pool.wait_ge(s["mm_score"], 4 * (h - 1))
                    pool.tensor_scalar(qm[:, h % 2, :], qk[:, 0, :], hm[:, h:h + 1], 1.0, ALU.mult, ALU.mult)\
                        .then_inc(s["q_ready"], 1)
                for h in range(3 * GH):
                    mask_q(h)
                for gr in range(1, NG + 1):
                    for h in range((gr + 2) * GH, min(H1, (gr + 3) * GH)):
                        mask_q(h)
                    for i in range(NT):
                        n = (gr - 1) * NT + i
                        pool.wait_ge(s["u_ready"], n + 1)
                        pool.tensor_tensor(E_(n), E_(n), W_(n), ALU.subtract).then_inc(s["p_ready"], 1)

            @block.vector
            def _(dve):
                step = Chain(dve, s["dve_step"])

                def gs(gr):
                    return slice(gr * NT, (gr + 1) * NT)

                def update(gr, k):
                    c = gs(gr)
                    if k <= ACT_COUNTS:
                        dve.wait_ge(s["act_count%d" % (k - 1)], NT * (gr + 1))
                        step(dve.tensor_scalar(tc[:, 1, c], signs[:, c], -0.5, T / 2.0, ALU.mult, ALU.add))
                    else:
                        dve.wait_ge(s["dve_count"], NT * ((COUNTS - ACT_COUNTS) * gr + k - ACT_COUNTS))
                    step(dve.tensor_scalar(up[:, c], tc[:, 1, c], AIM, None, ALU.is_ge))
                    step(dve.tensor_scalar(dn[:, c], tc[:, 1, c], AIM, None, ALU.is_lt))

                    def both(m):
                        return m[:, c].rearrange("p (a c) -> p a c", a=1).broadcast_to([P, 2, NT])
                    step(dve.copy_predicated(lo[:, :, c], both(up), tc[:, :, c]))
                    step(dve.copy_predicated(hi[:, :, c], both(dn), tc[:, :, c]))
                    step(dve.tensor_tensor(dif[:, :, c], lo[:, :, c], hi[:, :, c], ALU.subtract))
                    step(dve.reciprocal(rec[:, c], dif[:, 1, c]))
                    step(dve.scalar_tensor_tensor(rec[:, c], lo[:, 1, c], AIM, rec[:, c], ALU.subtract, ALU.mult))
                    step(dve.tensor_tensor(rec[:, c], rec[:, c], dif[:, 0, c], ALU.mult))
                    ins = dve.tensor_tensor(tc[:, 0, c], lo[:, 0, c], rec[:, c], ALU.subtract)
                    if k == 1:
                        ins.then_inc(s["t_ready1"], 1)
                    else:
                        step(ins)

                def count(gr, rnd):
                    before = NT * ((COUNTS - ACT_COUNTS) * gr + rnd)
                    for n in range(gr * NT, (gr + 1) * NT):
                        dve.wait_ge(s["s_ready"], n + 1)
                        if before + n % NT >= 2:
                            dve.wait_ge(s["dve_count"], before + n % NT - 1)
                        yield n, dve.tensor_scalar(above[:, n % 2, :], S_(n), tc[:, 0, n:n + 1], 0.0, ALU.is_gt, ALU.add,
                                                   accum_out=tc[:, 1, n:n + 1]).then_inc(s["dve_count"], 1)

                def take(gr):
                    c = gs(gr)
                    if gr >= 2:
                        dve.wait_ge(s["p_ready"], NT * (gr - 1))
                    for n, _ in count(gr, COUNTS - ACT_COUNTS - 1):
                        i = n % NT
                        dve.wait_ge(s["dve_count"], NT * (COUNTS - ACT_COUNTS) * gr + NT * (COUNTS - ACT_COUNTS - 1) + i + 1)
                        dve.scalar_tensor_tensor(W_(n), above[:, n % 2, :], TAKEN, S_(n), ALU.mult, ALU.add)\
                           .then_inc(s["rest_left"], 1)
                        if i:
                            dve.wait_ge(s["rest_left"], n)
                            dve.max(m8[:, i - 1, :], W_(n - 1)).then_inc(s["max8"], 1)
                    dve.wait_ge(s["rest_left"], (gr + 1) * NT)
                    dve.max(m8[:, NT - 1, :], W_(gr * NT + NT - 1)).then_inc(s["max8"], 1)
                    step(dve.tensor_scalar(rec[:, c], tc[:, 1, c], TOPK - 4.5, None, ALU.subtract))
                    step(dve.tensor_tensor(rec[:, c], rec[:, c], rec[:, c], ALU.mult))
                    dve.tensor_scalar(bad[:, gr % 2, :], rec[:, c], 16.0, None, ALU.is_gt).then_inc(s["bad_ready"], 1)
                    dve.wait_ge(s["bad_ready"], gr + 1)
                    step(dve.tensor_scalar(rec[:, c], tc[:, 1, c], -1.0, float(TOPK), ALU.mult, ALU.add))
                    step(dve.tensor_tensor(keep[:, :, :], rec[:, c].rearrange("p (c a) -> p c a", a=1).broadcast_to([P, NT, 8]),
                                           rank[:, :].rearrange("p (a r) -> p a r", a=1).broadcast_to([P, NT, 8]), ALU.is_gt))
                    dve.wait_ge(s["max8"], (gr + 1) * NT)
                    step(dve.tensor_tensor(m8[:, :, :], m8[:, :, :], keep[:, :, :], ALU.mult))
                    step(dve.tensor_scalar(keep[:, :, :], keep[:, :, :], 1.0, -TAKEN, ALU.subtract, ALU.mult))
                    step(dve.tensor_tensor(m8[:, :, :], m8[:, :, :], keep[:, :, :], ALU.add))
                    for i in range(NT):
                        n = gr * NT + i
                        dve.match_replace(W_(n), m8[:, i, :], W_(n), TAKEN).then_inc(s["matched"], 1)

                def check(gr):
                    dve.wait_ge(s["mm_bad"], gr + 1)
                    dve.wait_ge(s["matched"], (gr + 1) * NT)
                    src = PS[0:1, 6 + gr % 2, 128:128 + NT]
                    step(dve.tensor_copy(nbad[:, 0:NT], src))
                    step(dve.tensor_reduce(nbad_sum[:, :], src, AX, ALU.add))
                    step(dve.tensor_copy(nbad[:, NT:NT + 1], nbad_sum[:, :]))
                    with dve.If(dve.value_load(nbad[0:1, NT:NT + 1]) > 0):
                        for i in range(NT):
                            n = gr * NT + i
                            with dve.If(dve.value_load(nbad[0:1, i:i + 1]) > 0):
                                dve.tensor_copy(W_(n), S_(n)).then_inc(s["slow"], 1)
                                dve.wait_ge(s["slow"], 1)
                                dve.sem_clear(s["slow"])
                                with dve.Fori(0, TOPK // 8):
                                    dve.max(m8[:, 0, :], W_(n)).then_inc(s["slow"], 1)
                                    dve.wait_ge(s["slow"], 1)
                                    dve.match_replace(W_(n), m8[:, 0, :], W_(n), TAKEN).then_inc(s["slow"], 1)
                                    dve.wait_ge(s["slow"], 2)
                                    dve.sem_clear(s["slow"])
                    step(dve.tensor_copy(nbad[:, 0:1], nbad[:, 0:1]))
                    dve.sem_inc(s["w_ready"], 1)

                def out(gr):
                    dve.wait_ge(s["mm_pv"], (gr + 1) * NT)
                    pv = PS[:, 6 + gr % 2, 0:NT * (D1 + 1)].rearrange("p (h t c) -> p h t c", t=4, c=D1 + 1)
                    if gr:
                        dve.wait_ge(s["out_ready"], gr)
                    rp = prec[:, :].rearrange("p (h t c) -> p h t c", t=4, c=1)
                    step(dve.reciprocal(rp, pv[:, :, :, D1:]))
                    dve.tensor_tensor(OUT[:, :, gr * GH:(gr + 1) * GH, :].rearrange("p t h c -> p h t c"),
                                      pv[:, :, :, 0:D1], rp.broadcast_to([P, GH, 4, D1]), ALU.mult)\
                       .then_inc(s["out_ready"], 1)

                update(0, 1)
                update(0, 2)
                for gr in range(NG):
                    if gr + 1 < NG:
                        update(gr + 1, 1)
                    for _ in count(gr, 0):
                        pass
                    if gr >= 1:
                        check(gr - 1)
                    update(gr, 3)
                    for _ in count(gr, 1):
                        pass
                    if gr + 1 < NG:
                        update(gr + 1, 2)
                    if gr >= 2:
                        out(gr - 2)
                    update(gr, 4)
                    take(gr)
                check(NG - 1)
                out(NG - 2)
                out(NG - 1)

        def finish(block, b, s):
            xb = X[:, ds(b, 1), :].rearrange("p a t -> p (a t)")

            @block.tensor
            def _(pe):
                for t in range(4):
                    mm = pe.transpose(PS[:, 0, t * P:(t + 1) * P], OUT[:, t, :, :].rearrange("p h c -> p (h c)"), ident[:, :])
                mm.then_inc(s["mm_oT"], 1)
                pe.wait_ge(s["oT_ready"], 1)
                pe.matmul(PS[:, 1, :], w["Wo"][:, :], OT[:, :], start=True, stop=True).then_inc(s["mm_o"], 1)

            @block.scalar
            def _(act):
                act.wait_ge(s["mm_oT"], 1)
                act.activation(OT[:, :], PS[:, 0, :], ACT.Copy).then_inc(s["oT_ready"], 1)

            @block.vector
            def _(dve):
                step = Chain(dve, s["dve_step"])
                dve.wait_ge(s["mm_o"], 1)
                step(dve.scalar_tensor_tensor(xc[:, :], PS[:, 1, :], col["bo"][:, 0:1], hn[:, :], ALU.add, ALU.subtract))
                step(dve.tensor_tensor(xc[:, :], xc[:, :], gate[:, :], ALU.mult))
                step(dve.tensor_tensor(xc[:, :], xc[:, :], hn[:, :], ALU.add))
                step(dve.scalar_tensor_tensor(xb, xc[:, :], mod[:, 2:3], xb, ALU.mult, ALU.add))

        with nc.Fori(0, NB) as b:
            nested(nc, LN_SEMS + "mm_proj mm_v mm_ss mm_temp mean_ready qk_ready qk_sq gate_ready temp_sig norm_ready "
                   "qk_norm mm_kT kT_ready mm_C C_ready mm_CQ qcq_ready mm_mom var_ready sd_ready dve_step", b, project)
            nested(nc, "q_ready mm_score s_ready exp_ready act_count0 act_count1 t_ready1 dve_count rest_left max8 matched "
                   "bad_ready mm_bad slow w_ready u_ready p_ready mm_pT pT_ready mm_pv out_ready dve_step", b, search)
            nested(nc, "mm_oT oT_ready mm_o dve_step", b, finish)


DEPTH = 6
H2, D2 = 16, 64
WIN = 32
INNER = H2 * D2
NPAIR = H2 // 2
F_IN = P * 4 * 2 // 3
FC = -(-F_IN // P)
QK_SCALE = 8.0


def tower_stage(nc, dram, g, PS):
    X, XF, MOD, eps, mean_w, ident = g.X, g.XF, g.MOD1, g.eps, g.mean_w, g.ident
    with ExitStack() as ctx:
        def sb(n, shape):
            return ctx.enter_context(nc.sbuf_tensor("tower_" + n, shape, F32))
        wqkv, wrot = sb("wqkv", [P, 3 * INNER]), sb("wrot", [P, 2 * INNER])
        wo, w1, w2 = sb("wo", [P, NPAIR, P]), sb("w1", [P, 2 * FC, P]), sb("w2", [P, FC, P])
        b1, cols = sb("b1", [P, DEPTH, 2 * FC]), sb("cols", [P, DEPTH, 7])
        lb1, lcol = sb("lb1", [P, 2 * FC]), sb("lcol", [P, 7])
        tab = sb("tab", [P, 4, T])
        sel2, hsel = sb("sel2", [P, 2]), sb("hsel", [H2, NPAIR, P])
        bias = sb("bias", [P, 2, 2 * WIN])
        xs, xc, sq, rstd, xn = (sb(n, [P, T]) for n in ("xs", "xc", "sq", "rstd", "xn"))
        V, VP = sb("V", [P, 4, INNER]), sb("VP", [P, 4, INNER])
        QT, KT = sb("QT", [P, NPAIR, T]), sb("KT", [P, NPAIR, WIN + T])
        qc, qsq, t1, t2 = (sb(n, [P, 2, T]) for n in ("qc", "qsq", "t1", "t2"))
        rn, rkT = sb("rn", [P, 4, 2, H2]), sb("rkT", [H2, T])
        SC, PT, AO = sb("SC", [P, 2, INNER]), sb("PT", [P, 2, INNER]), sb("AO", [P, INNER])
        OT = sb("OT", [P, NPAIR, T])
        mx, ssum, rsum = sb("mx", [P, 2, H2]), sb("ssum", [P, 2, H2]), sb("rsum", [P, 2, H2])
        mod = sb("mod", [P, 6])
        flat = V[:, :, :].rearrange("p a c -> p (a c)")
        hg = [flat[:, j * T:(j + 1) * T] for j in range(2 * FC)]

        def setup(block, i, s):
            loads = [(b1[:, :, :], dram["f_b1"]), (cols[:, :, :], dram["f_cols"]), (sel2[:, :], dram["sel2"]),
                     (hsel[:, :, :], dram["hsel"]), (bias[:, :, :], dram["winmask"])]

            @block.sync
            def _(sp):
                for tile, src in loads:
                    sp.dma_start(tile, src).then_inc(s["w_in"], 16)
                sp.wait_ge(s["w_in"], 16 * len(loads))

            @block.gpsimd
            def _(pool):
                pool.memset(xs[64:128, 0:1], 0.0).then_inc(s["pool_done"], 1)
                pool.wait_ge(s["pool_done"], 1)
                pool.memset(VP[0:WIN, 0, :], 0.0).then_inc(s["pool_done"], 1)
                pool.wait_ge(s["pool_done"], 2)
                pool.memset(KT[:, :, 0:WIN], 0.0).then_inc(s["pool_done"], 1)
                pool.wait_ge(s["pool_done"], 3)
        stage(nc, "w_in pool_done", 1, setup)

        def enter(block, b, s):
            xb = X[:, ds(b, 1), :].rearrange("p a t -> p (a t)")
            xf = XF[:, ds(b, 1), :].rearrange("p a t -> p (a t)")

            @block.tensor
            def _(pe):
                ln_tensor(pe, s, xb, mean_w[:, :], sq[:, :], PS[:, 0, :], PS[:, 1, :])

            @block.scalar
            def _(act):
                ln_scalar(act, s, xc[:, :], sq[:, :], PS[:, 1, :], rstd[:, :], eps[:, 0:1])

            @block.vector
            def _(dve):
                step = Chain(dve, s["dve_step"])
                step(dve.tensor_copy(mod[:, :], MOD[:, ds(b, 1), :].rearrange("p a j -> p (a j)")))
                ln_vector(dve, s, xb, xc[:, :], PS[:, 0, :], rstd[:, :], mod[:, 4:5], mod[:, 3:4], xf)
        stage(nc, LN_SEMS + "dve_step", NB, enter)

        def load_layer(block, l, s):
            @block.sync
            def _(sp):
                def from_layer(name, tile):
                    src = dram[name][ds(l, 1)]
                    sp.dma_start(tile, src.rearrange("a p c -> p (a c)")).then_inc(s["layer_in"], 16)
                from_layer("f_Wqkv", wqkv[:, :])
                src = dram["f_Wqkv"][ds(l, 1), :, 0:2 * INNER].rearrange("a p (g z c) -> p (a g) z c", z=2, c=D2 // 2)
                dst = wrot[:, :].rearrange("p (g z c) -> p g z c", z=2, c=D2 // 2)
                for z in range(2):
                    sp.dma_start(dst[:, :, z, :], src[:, :, 1 - z, :]).then_inc(s["layer_in"], 16)
                from_layer("f_Wo", wo[:, :, :].rearrange("p a c -> p (a c)"))
                from_layer("f_W1", w1[:, :, :].rearrange("p a c -> p (a c)"))
                from_layer("f_W2", w2[:, :, :].rearrange("p a c -> p (a c)"))
                sp.dma_start(tab[:, :, :], dram["rotary"]).then_inc(s["tab_in"], 16)
                sp.wait_ge(s["layer_in"], 16 * 6)

            @block.vector
            def _(dve):
                dve.tensor_copy(lb1[:, :], b1[:, ds(l, 1), :].rearrange("p a j -> p (a j)")).then_inc(s["col_ready"], 1)
                dve.tensor_copy(lcol[:, :], cols[:, ds(l, 1), :].rearrange("p a j -> p (a j)")).then_inc(s["col_ready"], 1)
                dve.wait_ge(s["col_ready"], 2)
                dve.wait_ge(s["tab_in"], 16)
                for j in range(4):
                    dve.tensor_scalar(tab[:, j, :], tab[:, j, :], lcol[:, 3 + j:4 + j], None, ALU.mult)\
                       .then_inc(s["col_ready"], 1)

        def layer(block, b, s):
            xf = XF[:, ds(b, 1), :].rearrange("p a t -> p (a t)")
            xf_lo = XF[0:64, ds(b, 1), :].rearrange("p a t -> p (a t)")
            xf_hi = XF[64:128, ds(b, 1), 0:T - 1].rearrange("p a t -> p (a t)")

            @block.tensor
            def _(pe):
                pe.wait_ge(s["xs_ready"], 2)
                for t in range(4):
                    for j in range(2):
                        n = 2 * t + j
                        if n >= 2:
                            pe.wait_ge(s["v_ready"], n - 1)
                        pe.matmul(PS[:, n % 2, :], xs[:, t * P:(t + 1) * P],
                                  wqkv[:, 2 * INNER + j * 512:2 * INNER + (j + 1) * 512], start=True, stop=True)\
                          .then_inc(s["mm_v"], 1)
                for p in range(NPAIR):
                    for j in range(2):
                        c = slice(j * INNER + p * P, j * INNER + (p + 1) * P)
                        if p:
                            pe.wait_ge(s["qc_ready"], 2 * (p - 1) + j + 1)
                        pe.matmul(PS[:, 2 + j, :], wqkv[:, c], xs[:, :], start=True, stop=True).then_inc(s["mm_q"], 1)
                        if p:
                            pe.wait_ge(s["t2_ready"], 2 * (p - 1) + j + 1)
                        pe.matmul(PS[:, 4 + j, :], wrot[:, c], xs[:, :], start=True, stop=True).then_inc(s["mm_qr"], 1)
                    if p:
                        norms_of(pe, s, p - 1)
                norms_of(pe, s, NPAIR - 1)
                pe.wait_ge(s["rn_ready"], 1)
                for t in range(4):
                    mm = pe.transpose(PS[0:H2, 7, t * P:(t + 1) * P], rn[:, t, 1, :], ident[:, :])
                mm.then_inc(s["mm_rkT"], 1)
                pe.wait_ge(s["rkT_ready"], 1)
                for p in range(NPAIR):
                    if p >= 2:
                        pe.wait_ge(s["kt_ready"], p - 1)
                    pe.matmul(PS[:, p % 2, :], hsel[:, p, :], rkT[:, :], start=True, stop=True).then_inc(s["mm_rk"], 1)
                pe.wait_ge(s["kt_ready"], NPAIR)
                pe.wait_ge(s["qt_ready"], 2 * NPAIR)

                def scores(t):
                    if t:
                        pe.wait_ge(s["sc_scaled"], 2 * t)
                    for h in range(H2):
                        r = slice(64 * (h % 2), 64 * (h % 2) + 64)
                        for w in range(4):
                            c0 = t * P + w * WIN
                            mm = pe.matmul(PS[32 * w:32 * w + 32, h % 2, (h // 2) * 64:(h // 2) * 64 + 64],
                                           QT[r, h // 2, c0:c0 + WIN], KT[r, h // 2, c0:c0 + 2 * WIN],
                                           start=True, stop=True, tile_position=(64 * (h % 2), 32 * w))
                    mm.then_inc(s["mm_sc"], 1)

                def values(t):
                    pe.wait_ge(s["pt_ready"], t + 1)
                    if t == 0:
                        pe.wait_ge(s["vp_in"], 16 * 4)
                    else:
                        pe.wait_ge(s["ao_ready"], 2 * t)
                    for h in range(H2):
                        hc = (h % 2) * 512 + (h // 2) * 64
                        for w in range(4):
                            r = slice(32 * w, 32 * w + 32)
                            for kb, v in enumerate((VP, V)):
                                mm = pe.matmul(PS[r, 2 + h // 8, (h % 8) * 64:(h % 8) * 64 + 64],
                                               PT[r, t % 2, hc + 32 * kb:hc + 32 * kb + 32],
                                               v[r, t, h * D2:(h + 1) * D2], start=(kb == 0), stop=(kb == 1),
                                               tile_position=(32 * w, 32 * w))
                    mm.then_inc(s["mm_pv"], 1)

                def turn(t):
                    pe.wait_ge(s["ao_ready"], 2 * t + 2)
                    if t:
                        pe.wait_ge(s["ot_ready"], 2 * t)
                    for p in range(NPAIR):
                        mm = pe.transpose(PS[:, 4 + p // 4, (p % 4) * P:(p % 4 + 1) * P], AO[:, p * P:(p + 1) * P],
                                          ident[:, :])
                        if p % 4 == 3:
                            mm.then_inc(s["mm_ot"], 1)
                scores(0)
                for t in range(4):
                    if t < 3:
                        scores(t + 1)
                    values(t)
                    if t:
                        turn(t - 1)
                turn(3)
                pe.wait_ge(s["ot_ready"], 8)
                for p in range(NPAIR):
                    mm = pe.matmul(PS[:, 6, :], wo[:, p, :], OT[:, p, :], start=(p == 0), stop=(p == NPAIR - 1))
                mm.then_inc(s["mm_o"], 1)
                pe.wait_ge(s["xs_ready"], 4)
                ln_tensor(pe, s, xs[:, :], mean_w[:, :], sq[:, :], PS[:, 0, :], PS[:, 1, :])
                pe.wait_ge(s["ln_out"], 1)
                for j in range(FC):
                    pe.matmul(PS[:, 2 + j, :], w1[:, FC + j, :], xn[:, :], start=True, stop=True).then_inc(s["mm_gate"], 1)
                for j in range(FC):
                    if j == 2:
                        pe.wait_ge(s["x_mid"], 1)
                    pe.matmul(PS[:, (5, 7, 6)[j], :], w1[:, j, :], xn[:, :], start=True, stop=True).then_inc(s["mm_val"], 1)
                for j in range(FC):
                    pe.wait_ge(s["h_ready"], j + 1)
                    mm = pe.matmul(PS[:, 0, :], w2[:, j, :], hg[FC + j], start=(j == 0), stop=(j == FC - 1))
                mm.then_inc(s["mm_mlp"], 1)

            @block.scalar
            def _(act):
                for n in range(8):
                    act.wait_ge(s["mm_v"], n + 1)
                    act.activation(V[:, n // 2, (n % 2) * 512:(n % 2 + 1) * 512], PS[:, n % 2, :], ACT.Copy)\
                       .then_inc(s["v_ready"], 1)
                for p in range(NPAIR):
                    for j in range(2):
                        n = 2 * p + j
                        act.wait_ge(s["mm_q"], n + 1)
                        if p:
                            act.wait_ge(s["t1_ready"], n - 1)
                        act.activation(qc[:, j, :], PS[:, 2 + j, :], ACT.Copy).then_inc(s["qc_ready"], 1)
                        act.wait_ge(s["qc_ready"], n + 1)
                        if p:
                            act.wait_ge(s["mm_ss"], n - 1)
                        act.activation(qsq[:, j, :], qc[:, j, :], ACT.Square).then_inc(s["qsq_ready"], 1)
                act.wait_ge(s["mm_ss"], 2 * NPAIR)
                act.activation(rn[:, :, :, :].rearrange("p t z h -> p (t z h)"), PS[:, 6, 0:128], ACT.Sqrt)\
                   .then_inc(s["norm_ready"], 1)
                act.wait_ge(s["mm_rkT"], 1)
                act.activation(rkT[:, :], PS[0:H2, 7, :], ACT.Copy).then_inc(s["rkT_ready"], 1)

                def turned(t):
                    for j in range(2):
                        act.wait_ge(s["mm_ot"], 2 * t + j + 1)
                        act.activation(OT[:, 4 * j:4 * j + 4, t * P:(t + 1) * P],
                                       PS[:, 4 + j, :].rearrange("p (a c) -> p a c", a=4), ACT.Copy).then_inc(s["ot_ready"], 1)
                for t in range(4):
                    act.wait_ge(s["sc_ready"], t + 1)
                    act.activation(SC[:, t % 2, :], SC[:, t % 2, :], ACT.Exp).then_inc(s["exp_ready"], 1)
                    if t >= 2:
                        turned(t - 2)
                turned(2)
                turned(3)
                ln_scalar(act, s, xc[:, :], sq[:, :], PS[:, 1, :], rstd[:, :], eps[:, 0:1])
                for j in range(FC):
                    act.wait_ge(s["mm_gate"], j + 1)
                    act.activation(hg[j], PS[:, 2 + j, :], ACT.Gelu, bias=lb1[:, FC + j:FC + j + 1]).then_inc(s["gelu_ready"], 1)

            @block.gpsimd
            def _(pool):
                for p in range(NPAIR):
                    for j in range(2):
                        n = 2 * p + j
                        pool.wait_ge(s["t1_ready"], n + 1)
                        pool.wait_ge(s["t2_ready"], n + 1)
                        dst = QT[:, p, :] if j == 0 else KT[:, p, WIN:]
                        pool.tensor_tensor(dst, t1[:, j, :], t2[:, j, :], ALU.add).then_inc(s["qt_ready"], 1)

            @block.sync
            def _(sp):
                sp.wait_ge(s["v_ready"], 8)
                sp.dma_start(VP[WIN:P, :, :], V[0:P - WIN, :, :]).then_inc(s["vp_in"], 16)
                for t in range(3):
                    sp.dma_start(VP[0:WIN, t + 1, :], V[P - WIN:P, t, :]).then_inc(s["vp_in"], 16)
                sp.wait_ge(s["vp_in"], 16 * 4)

            @block.vector
            def _(dve):
                step = Chain(dve, s["dve_step"])
                dve.tensor_copy(xs[0:64, :], xf_lo).then_inc(s["xs_ready"], 1)
                dve.tensor_copy(xs[64:128, 1:T], xf_hi).then_inc(s["xs_ready"], 1)
                for p in range(NPAIR):
                    for j in range(2):
                        n = 2 * p + j
                        dve.wait_ge(s["qc_ready"], n + 1)
                        if p:
                            dve.wait_ge(s["qt_ready"], n - 1)
                        dve.tensor_tensor(t1[:, j, :], qc[:, j, :], tab[:, 2 * j, :], ALU.mult).then_inc(s["t1_ready"], 1)
                        dve.wait_ge(s["mm_qr"], n + 1)
                        dve.tensor_tensor(t2[:, j, :], PS[:, 4 + j, :], tab[:, 2 * j + 1, :], ALU.mult)\
                           .then_inc(s["t2_ready"], 1)
                dve.wait_ge(s["norm_ready"], 1)
                flat_rn = rn[:, :, :, :].rearrange("p t z h -> p (t z h)")
                step(dve.tensor_scalar(flat_rn, flat_rn, 1e-12, None, ALU.max))
                dve.reciprocal(flat_rn, flat_rn).then_inc(s["rn_ready"], 1)
                for p in range(NPAIR):
                    dve.wait_ge(s["mm_rk"], p + 1)
                    dve.wait_ge(s["qt_ready"], 2 * p + 2)
                    dve.tensor_tensor(KT[:, p, WIN:], KT[:, p, WIN:], PS[:, p % 2, :], ALU.mult).then_inc(s["kt_ready"], 1)

                def heads(a):
                    return a.rearrange("p (g k) -> p g k", k=2 * WIN)

                def spread(a):
                    return a.rearrange("p (g k) -> p g k", k=1)

                def front(t):
                    dve.wait_ge(s["mm_sc"], t + 1)
                    if t >= 2:
                        dve.wait_ge(s["pt_ready"], t - 1)
                    for j in range(2):
                        dve.tensor_tensor(heads(SC[:, t % 2, 512 * j:512 * j + 512]), heads(PS[:, j, :]),
                                          spread(rn[:, t, 0, 8 * j:8 * j + 8]).broadcast_to([P, 8, 2 * WIN]),
                                          ALU.mult).then_inc(s["sc_scaled"], 1)
                    dve.wait_ge(s["sc_scaled"], 2 * t + 2)
                    sc = heads(SC[:, t % 2, :])
                    mk = bias[:, min(t, 1):min(t, 1) + 1, :].broadcast_to([P, H2, 2 * WIN])
                    step(dve.scalar_tensor_tensor(sc, sc, QK_SCALE, mk, ALU.mult, ALU.add))
                    step(dve.tensor_reduce(mx[:, t % 2, :], sc, AX, ALU.max))
                    dve.tensor_tensor(sc, sc, spread(mx[:, t % 2, :]).broadcast_to([P, H2, 2 * WIN]), ALU.subtract)\
                       .then_inc(s["sc_ready"], 1)

                def back(t):
                    dve.wait_ge(s["exp_ready"], t + 1)
                    if t >= 2:
                        dve.wait_ge(s["mm_pv"], t - 1)
                    dve.transpose(PT[:, t % 2, :], SC[:, t % 2, :]).then_inc(s["pt_ready"], 1)
                    step(dve.tensor_reduce(ssum[:, t % 2, :].rearrange("p (g z) -> p z g", z=2),
                                           SC[:, t % 2, :].rearrange("p (z g k) -> p z g k", z=2, k=2 * WIN), AX, ALU.add))
                    step(dve.reciprocal(rsum[:, t % 2, :], ssum[:, t % 2, :]))

                def outs(t):
                    dve.wait_ge(s["mm_pv"], t + 1)
                    if t:
                        dve.wait_ge(s["mm_ot"], 2 * t)
                    for j in range(2):
                        dve.tensor_tensor(AO[:, 512 * j:512 * j + 512].rearrange("p (g k) -> p g k", k=D2),
                                          PS[:, 2 + j, :].rearrange("p (g k) -> p g k", k=D2),
                                          spread(rsum[:, t % 2, 8 * j:8 * j + 8]).broadcast_to([P, 8, D2]),
                                          ALU.mult).then_inc(s["ao_ready"], 1)
                front(0)
                for t in range(4):
                    if t < 3:
                        front(t + 1)
                    back(t)
                    outs(t)
                dve.wait_ge(s["mm_o"], 1)
                dve.tensor_tensor(xf, xf, PS[:, 6, :], ALU.add).then_inc(s["x_mid"], 1)
                dve.wait_ge(s["x_mid"], 1)
                dve.tensor_copy(xs[0:64, :], xf_lo).then_inc(s["xs_ready"], 1)
                dve.tensor_copy(xs[64:128, 1:T], xf_hi).then_inc(s["xs_ready"], 1)
                dve.wait_ge(s["xs_ready"], 4)
                ln_vector(dve, s, xs[:, :], xc[:, :], PS[:, 0, :], rstd[:, :], lcol[:, 0:1], lcol[:, 1:2], xn[:, :])
                for j in range(FC):
                    dve.wait_ge(s["gelu_ready"], j + 1)
                    dve.wait_ge(s["mm_val"], j + 1)
                    dve.scalar_tensor_tensor(hg[FC + j], PS[:, (5, 7, 6)[j], :], lb1[:, j:j + 1], hg[j], ALU.add, ALU.mult)\
                       .then_inc(s["h_ready"], 1)
                dve.wait_ge(s["mm_mlp"], 1)
                dve.scalar_tensor_tensor(xf, PS[:, 0, :], lcol[:, 2:3], xf, ALU.add, ALU.add).then_inc(s["dve_step"], 1)

        def norms_of(pe, s, p):
            cols6 = PS[:, 6, 0:128].rearrange("p (t z y g) -> p t z y g", t=4, z=2, y=2)
            for j in range(2):
                pe.wait_ge(s["qsq_ready"], 2 * p + j + 1)
                for t in range(4):
                    mm = pe.matmul(cols6[:, t, j, :, p], qsq[:, j, t * P:(t + 1) * P], sel2[:, :], start=True, stop=True)
                mm.then_inc(s["mm_ss"], 1)

        names = LN_SEMS + ("xs_ready mm_v v_ready mm_q mm_qr qc_ready qsq_ready mm_ss t1_ready t2_ready qt_ready "
                           "norm_ready rn_ready mm_rkT rkT_ready mm_rk kt_ready mm_sc sc_scaled sc_ready exp_ready "
                           "pt_ready vp_in mm_pv ao_ready mm_ot ot_ready mm_o x_mid mm_gate mm_val gelu_ready h_ready "
                           "mm_mlp dve_step")
        with nc.Fori(0, DEPTH) as l:
            nested(nc, "layer_in tab_in col_ready", l, load_layer)
            stage(nc, names, NB, layer)

        def leave(block, b, s):
            xb = X[:, ds(b, 1), :].rearrange("p a t -> p (a t)")
            xf = XF[:, ds(b, 1), :].rearrange("p a t -> p (a t)")

            @block.vector
            def _(dve):
                step = Chain(dve, s["dve_step"])
                step(dve.tensor_copy(mod[:, :], MOD[:, ds(b, 1), :].rearrange("p a j -> p (a j)")))
                step(dve.scalar_tensor_tensor(xb, xf, mod[:, 5:6], xb, ALU.mult, ALU.add))
        stage(nc, "dve_step", NB, leave)


class Globals:
    pass


def build(nc, dram, out):
    with ExitStack() as ctx:
        def sb(n, shape):
            return ctx.enter_context(nc.sbuf_tensor(n, shape, F32))
        g = Globals()
        g.X = sb("X", [P, NB, T])
        g.MOD0, g.MOD1 = sb("MOD0", [P, NB, 6]), sb("MOD1", [P, NB, 6])
        g.eps = sb("eps", [P, 4])
        g.mean_w, g.ident = sb("mean_w", [P, P]), sb("ident", [P, P])
        PS = ctx.enter_context(nc.psum_tensor("PS", [P, 8, 512], F32))
        consts = [(g.X[:, :, :], dram["x"]), (g.eps[:, :], dram["eps"]), (g.mean_w[:, :], dram["mean_w"]),
                  (g.ident[:, :], dram["ident"])]
        modulation_stage(nc, dram, consts, PS, (g.MOD0, g.MOD1))
        delta_attention_stage(nc, dram, g, PS)
        experts_stage(nc, dram, g, PS)
        topk_attention_stage(nc, dram, g, PS)
        g.XF = sb("XF", [P, NB, T])
        tower_stage(nc, dram, g, PS)

        def store(block, i, s):
            @block.sync
            def _(sp):
                sp.dma_start(out, g.X[:, :, :]).then_inc(s["out_done"], 16)
                sp.wait_ge(s["out_done"], 16)
        stage(nc, "out_done", 1, store)


def shape_constants(np):
    f = np.float32
    c = {"ident": np.eye(P, dtype=f), "mean_w": np.full((P, P), 1.0 / P, f)}
    c["eps"] = np.tile(np.array([LN_EPS, 1e-6, 0, 0], f), (P, 1))
    i = np.arange(P)
    c["blk32"] = (i[:, None] // D0 == i[None, :] // D0).astype(f)
    r, q = np.arange(CH)[:, None], np.arange(CH)[None, :]
    m = [q < r, r <= q, r == q, (r // 2 == q // 2) & (r % 2 == 1) & (q % 2 == 0)]
    for z in (2, 4, 8, 16):
        m.append((r // (2 * z) == q // (2 * z)) & (q // z % 2 == 1) & (r // z % 2 == 0))
    c["masks"] = np.tile(np.stack(m, 1), (H0, 1, 1)).astype(f)
    sel = np.zeros((P, 4, 3, P), f)
    for h in range(H0):
        ch = slice(32 * h, 32 * h + 32)
        for k in range(4):
            row = 32 * h + 4 * k
            sel[ch, k, 0, row] = sel[ch, k, 0, row + 1] = 1.0 / D0
            sel[ch, k, 1, row + 2] = 1.0 / D0
            sel[ch, k, 2, row + 1] = 1.0 / D0
            sel[ch, k, 2, row + 3] = 1.0
    c["sel"] = sel
    used = i % 32 < 16
    c["stm"] = np.stack([used & (i % 2 == 0), used & (i % 4 == 1), used & (i % 4 == 3)], 1).astype(f)
    ps = np.zeros((16, 4, P), f)
    for h in range(H0):
        for k in range(4):
            ps[4 * h + k, k, 32 * h:32 * h + 32] = 1
    c["psel"] = ps
    c["sel2"] = (i[:, None] // D2 == np.arange(2)[None, :]).astype(f)
    hs = np.zeros((H2, NPAIR, P), f)
    for par in range(2):
        for p in range(NPAIR):
            hs[par * NPAIR + p, p, 64 * par:64 * par + 64] = 1
    c["hsel"] = hs
    q, j = i % WIN, np.arange(2 * WIN)
    ok = (q[:, None] <= j[None, :]) & (j[None, :] <= q[:, None] + WIN)
    first = ok & ((i[:, None] >= WIN) | (j[None, :] >= WIN))
    c["winmask"] = np.where(np.stack([first, ok], 1), 0, -1e30).astype(f)
    half = np.arange(0, D2, 2, dtype=f)
    tt = np.arange(T, dtype=f)
    ang = tt[:, None] * (f(1.0) / f(10000.0) ** (half / f(D2)))[None, :]
    scl = ((half + f(0.4 * D2)) / f(1.4 * D2))[None, :] ** ((tt - T // 2) / f(WIN // 2))[:, None]
    ang, scl = (np.concatenate([z, z], -1) for z in (ang, scl))
    sgn = np.where(np.arange(D2) < D2 // 2, -1, 1).astype(f)
    tabs = [np.cos(ang) * scl, np.sin(ang) * sgn * scl, np.cos(ang) / scl, np.sin(ang) * sgn / scl]
    c["rotary"] = np.tile(np.stack([z.T for z in tabs], 1), (2, 1, 1)).astype(f)
    e = np.arange(8)
    c["tri8"] = np.tile((e[None, :] < e[:, None]).astype(f), (P, 1, 1))
    c["esel"] = np.tile(np.eye(8, dtype=f)[:, :, None], (1, 1, P))
    c["t_blk8"] = (i[:, None] // D1 == i[None, :] // D1).astype(f)
    c["rank"] = np.tile(np.arange(8, dtype=f), (P, 1))
    c["hm"] = (i[:, None] // D1 == np.arange(H1)[None, :]).astype(f)
    return c


def kernel(**inputs):
    import numpy as np
    import concourse.bacc as bacc
    from concourse.bass_utils import run_bass_kernel_spmd as run

    def col(a, rep=1):
        return np.repeat(a.reshape(-1), rep).reshape(-1, 1)

    a = {n[8:]: v for n, v in inputs.items() if n.startswith("L0_attn_")}
    h = shape_constants(np)
    h["x"] = a["hidden_states"].transpose(2, 0, 1)
    for l in range(2):
        h[f"cT{l}"], h[f"wmod{l}"] = inputs[f"L{l}_c"].T, inputs[f"L{l}_wmod"]
    h["qwT"], h["kwT"], h["vwT"], h["owT"] = a["q_w"].T, a["k_w"].T, a["v_w"].T, a["o_w"].T
    h["bwT"] = np.repeat(a["b_w"].T, D0, axis=1)
    h["cw"] = np.stack([a["q_cw"], a["k_cw"], a["v_cw"]], 1)
    h["firs"], h["firl"] = a["fir_short_w"].reshape(P, FIR_S), a["fir_long_w"].reshape(P, FIR_L)
    h["mlp1h"] = a["mlp1_w"].T[:P]
    h["mlp1s"] = np.tile(np.concatenate([a["mlp1_w"].T[P:], np.zeros((16, P), np.float32)]), (4, 1))
    h["mlp1b"], h["mlp2T"] = col(a["mlp1_b"]), a["mlp2_w"].T
    h["mlp2b"] = np.tile(a["mlp2_b"], (P, 1))
    h["ltemp"], h["cres"] = col(a["logit_temp"], P), col(a["conv_res_logit"], D0)
    h["normw"] = np.tile(a["norm_w"], H0).reshape(P, 1)
    m = {n[7:]: v for n, v in inputs.items() if n.startswith("L0_ffn_")}
    h["w1"] = np.concatenate([m["w1"], m["cfc"][None]]).transpose(2, 0, 1)
    h["w2"] = np.concatenate([m["w2"], m["cproj"][None]]).transpose(2, 0, 1)
    h["gate_wT"], h["lb_bias"] = m["gate_w"].T, np.tile(m["lb_bias"], (P, 1))
    t = {n[8:]: v for n, v in inputs.items() if n.startswith("L1_attn_")}
    for n in ("Wq", "Wk", "Wv", "Wo", "Wg", "Wt"):
        h["t_" + n] = t[n]
    for n in ("bq", "bk", "bo", "bg"):
        h["t_" + n] = col(t[n])
    h["t_bt"], h["t_bv"] = col(t["bt"], P), np.tile(t["bv"], (P, 1))
    u = {n[7:]: v for n, v in inputs.items() if n.startswith("L1_ffn_")}
    h["f_Wqkv"] = u["Wqkv"]
    h["f_Wo"] = u["Wo"].reshape(DEPTH, NPAIR, P, P).transpose(0, 2, 1, 3).reshape(DEPTH, P, NPAIR * P)

    def chunked(v, axis):
        fill = [(0, 0)] * v.ndim
        fill[axis] = (0, FC * P - F_IN)
        return np.pad(v, fill)
    h["f_W1"] = np.concatenate([chunked(z, 2) for z in np.split(u["W1"], 2, 2)], 2)
    h["f_W2"] = chunked(u["W2"], 1).reshape(DEPTH, FC, P, P).transpose(0, 2, 1, 3).reshape(DEPTH, P, FC * P)
    h["f_b1"] = np.concatenate([chunked(z, 1) for z in np.split(u["b1"], 2, 1)], 1)\
        .reshape(DEPTH, 2 * FC, P).transpose(2, 0, 1)
    qs, ks = u["q_scale"], u["k_scale"]
    swap = (np.arange(D2) + D2 // 2) % D2
    h["f_cols"] = np.stack([u["ln_g"], u["ln_b"], u["b2"]] + [np.tile(z, (1, 2)) for z in
                           (qs, qs[:, swap], ks, ks[:, swap])], 1).transpose(2, 0, 1)

    nc = bacc.Bacc("TRN2", target_bir_lowering=False, num_devices=1)
    arrays, dram = {}, {}
    for n, v in h.items():
        arrays["in_" + n] = np.ascontiguousarray(v)
        dram[n] = nc.dram_tensor("in_" + n, v.shape, F32, kind="ExternalInput").ap()
    out = nc.dram_tensor("out", (P, NB, T), F32, kind="ExternalOutput").ap()
    build(nc, dram, out)
    r = run(nc, [arrays], core_ids=[0])
    return np.ascontiguousarray(r.results[0]["out"].transpose(1, 2, 0))
```

```python
from contextlib import ExitStack

import concourse.bass as bass
from concourse import mybir
from concourse.alu_op_type import AluOpType as ALU

F32 = mybir.dt.float32
ACT = mybir.ActivationFunctionType
AX = mybir.AxisListType.X
ds = bass.ds

P = 128
NB = 8
T = 512
LN_EPS = 1e-5
H0, D0 = 4, 32
CH = 32
NCH = T // CH
FIR_S, FIR_L = 5, 64
PROB_FLOOR = 0.02


def semaphores(nc, ctx, names):
    return {n: ctx.enter_context(nc.semaphore(n)) for n in names.split()}


def end_of_body(nc, s):
    for h in s.values():
        nc.gpsimd.sem_clear(h)
    nc.all_engine_barrier()


def stage(nc, names, count, body):
    with ExitStack() as ctx:
        s = semaphores(nc, ctx, names)

        def once(i):
            with nc.Block() as block:
                body(block, i, s)
            end_of_body(nc, s)

        if count == 1:
            once(0)
        else:
            with nc.Fori(0, count) as i:
                once(i)


LN_SEMS = "ln_mean ln_xc ln_sq ln_var ln_log ln_rstd ln_norm ln_out "


def ln_tensor(pe, s, x, mean_w, sq, ps_mean, ps_var):
    pe.matmul(ps_mean, mean_w, x, start=True, stop=True).then_inc(s["ln_mean"], 1)
    pe.wait_ge(s["ln_sq"], 1)
    pe.matmul(ps_var, mean_w, sq, start=True, stop=True).then_inc(s["ln_var"], 1)


def ln_scalar(act, s, xc, sq, ps_var, rstd, eps):
    act.wait_ge(s["ln_xc"], 1)
    act.activation(sq, xc, ACT.Square).then_inc(s["ln_sq"], 1)
    act.wait_ge(s["ln_var"], 1)
    act.activation(rstd, ps_var, ACT.Ln, bias=eps).then_inc(s["ln_log"], 1)
    act.wait_ge(s["ln_log"], 1)
    act.activation(rstd, rstd, ACT.Exp, scale=-0.5).then_inc(s["ln_rstd"], 1)


def ln_vector(dve, s, x, xc, ps_mean, rstd, gain, shift, out):
    dve.wait_ge(s["ln_mean"], 1)
    dve.tensor_tensor(xc, x, ps_mean, ALU.subtract).then_inc(s["ln_xc"], 1)
    dve.wait_ge(s["ln_rstd"], 1)
    dve.wait_ge(s["ln_xc"], 1)
    dve.tensor_tensor(xc, xc, rstd, ALU.mult).then_inc(s["ln_norm"], 1)
    dve.wait_ge(s["ln_norm"], 1)
    dve.tensor_scalar(out, xc, gain, shift, ALU.mult, ALU.add).then_inc(s["ln_out"], 1)


def nested(nc, names, i, body):
    with ExitStack() as ctx:
        s = semaphores(nc, ctx, names)
        with nc.Block() as block:
            body(block, i, s)
        end_of_body(nc, s)


class Chain:

    def __init__(self, eng, sem):
        self.eng, self.sem, self.n = eng, sem, 0

    def __call__(self, ins):
        self.n += 1
        ins.then_inc(self.sem, 1)
        self.eng.wait_ge(self.sem, self.n)


def modulation_stage(nc, dram, consts, PS, MOD):
    with ExitStack() as ctx:
        def sb(n, shape):
            return ctx.enter_context(nc.sbuf_tensor("mod_" + n, shape, F32))
        cT = [sb(f"cT{l}", [P, NB]) for l in range(2)]
        wm = [sb(f"wm{l}", [P, 6 * P]) for l in range(2)]
        sgn = sb("sgn", [P, NB])

        def body(block, i, s):
            @block.sync
            def _(sp):
                for l in range(2):
                    sp.dma_start(cT[l][:, :], dram[f"cT{l}"]).then_inc(s["c_in"], 16)
                    sp.dma_start(wm[l][:, :], dram[f"wmod{l}"]).then_inc(s["c_in"], 16)
                for tile, src in consts:
                    sp.dma_start(tile, src).then_inc(s["const_in"], 16)
                sp.wait_ge(s["const_in"], 16 * len(consts))

            @block.scalar
            def _(act):
                act.wait_ge(s["c_in"], 64)
                for l in range(2):
                    act.activation(cT[l][:, :], cT[l][:, :], ACT.Silu).then_inc(s["c_silu"], 1)

            @block.tensor
            def _(pe):
                pe.wait_ge(s["c_silu"], 2)
                for l in range(2):
                    for j in range(6):
                        mm = pe.matmul(PS[:, l, j * NB:(j + 1) * NB], wm[l][:, j * P:(j + 1) * P],
                                       cT[l][:, :], start=True, stop=True)
                    mm.then_inc(s["mod_ps"], 1)

            @block.vector
            def _(dve):
                step = Chain(dve, s["dve_step"])
                for l in range(2):
                    dve.wait_ge(s["mod_ps"], l + 1)
                    m = MOD[l]
                    step(dve.tensor_copy(m[:, :, :].rearrange("p b j -> p j b"),
                                         PS[:, l, 0:6 * NB].rearrange("p (j b) -> p j b", j=6)))
                    for j in (1, 4):
                        step(dve.tensor_scalar(m[:, :, j], m[:, :, j], 1.0, None, ALU.add))
                    for j in (2, 5):
                        step(dve.tensor_scalar(sgn[:, :], m[:, :, j], 0.0, 2.0, ALU.is_ge, ALU.mult))
                        step(dve.tensor_scalar(sgn[:, :], sgn[:, :], 1.0, None, ALU.subtract))
                        step(dve.tensor_tensor(m[:, :, j], m[:, :, j], sgn[:, :], ALU.mult))
                        step(dve.scalar_tensor_tensor(m[:, :, j], m[:, :, j], 0.25, sgn[:, :], ALU.max, ALU.mult))

        stage(nc, "c_in const_in c_silu mod_ps dve_step", 1, body)


def delta_attention_stage(nc, dram, g, PS):
    X, MOD, eps, mean_w, ident = g.X, g.MOD0, g.eps, g.mean_w, g.ident
    with ExitStack() as ctx:
        def sb(n, shape):
            return ctx.enter_context(nc.sbuf_tensor("delta_" + n, shape, F32))
        w = {n: sb("a_" + n, [P, P]) for n in ("qwT", "kwT", "vwT", "bwT", "mlp1h", "mlp1s", "owT")}
        cw = sb("a_cw", [P, 3, 4])
        firs, firl = sb("a_firs", [P, FIR_S]), sb("a_firl", [P, FIR_L])
        mlp1b, mlp2T, mlp2b = sb("a_mlp1b", [P, 1]), sb("a_mlp2T", [P, 4]), sb("a_mlp2b", [P, 4])
        ltemp, cres, normw = sb("a_ltemp", [P, 1]), sb("a_cres", [P, 1]), sb("a_normw", [P, 1])
        itemp, tscr = sb("a_itemp", [P, 1]), sb("a_tscr", [P, 2])
        blk = sb("a_blk", [P, P])
        masks = sb("a_masks", [P, 8, CH])
        sel = sb("a_sel", [P, 4, 3, P])
        stm = sb("a_stm", [P, 3])
        psel = sb("a_psel", [16, 4, P])
        loads = [(w[n][:, :], dram[n]) for n in w] + [
            (cw[:, :, :], dram["cw"]), (firs[:, :], dram["firs"]), (firl[:, :], dram["firl"]),
            (mlp1b[:, :], dram["mlp1b"]), (mlp2T[:, :], dram["mlp2T"]), (mlp2b[:, :], dram["mlp2b"]),
            (ltemp[:, :], dram["ltemp"]), (cres[:, :], dram["cres"]), (normw[:, :], dram["normw"]),
            (blk[:, :], dram["blk32"]), (masks[:, :, :], dram["masks"]), (sel[:, :, :, :], dram["sel"]),
            (stm[:, :], dram["stm"]), (psel[:, :, :], dram["psel"])]
        xc, sq, rstd, hn = sb("xc", [P, T]), sb("sq", [P, T]), sb("rstd", [P, T]), sb("hn", [P, T])
        pad = [sb(f"pad{j}", [P, 3 + T]) for j in range(3)]
        acc = [sb(f"acc{j}", [P, T]) for j in range(3)]
        vpad = sb("vpad", [P, FIR_L - 1 + T])
        V = vpad[:, FIR_L - 1:]
        qn, kn, beta, kb, vb = (sb(n, [P, T]) for n in ("qn", "kn", "beta", "kb", "vb"))
        kR, kbR, vbR = (sb(n, [P, T]) for n in ("kR", "kbR", "vbR"))
        M, MT, LT, AT, Xi, Zi, Y = (sb(n, [P, T]) for n in ("M", "MT", "LT", "AT", "Xi", "Zi", "Y"))
        U, WT, UA, S = sb("U", [P, T]), sb("WT", [P, T]), sb("UA", [P, CH]), sb("S", [P, D0])
        SH, LO, DE = sb("SH", [P, T]), sb("LO", [P, T]), sb("DE", [P, T])
        ab, sqr = sb("ab", [P, 4, T]), sb("sqr", [P, 4, T])
        st, h1 = sb("st", [P, T]), sb("h1", [P, 4, T])
        lg, pr, r16, m16 = sb("lg", [P, 64]), sb("pr", [P, 64]), sb("r16", [P, 16]), sb("m16", [P, 16])
        pT = sb("pT", [16, T])
        o = sb("o", [P, T])
        mod = sb("mod", [P, 6])

        def c3(a):
            return a.rearrange("p (n c) -> p n c", c=CH)

        def mask(j):
            return masks[:, j:j + 1, :].broadcast_to([P, NCH, CH])

        def setup(block, i, s):
            @block.sync
            def _(sp):
                for tile, src in loads:
                    sp.dma_start(tile, src).then_inc(s["w_in"], 16)

            @block.gpsimd
            def _(pool):
                pool.memset(vpad[:, 0:FIR_L - 1], 0.0).then_inc(s["pool_done"], 1)
                for j in range(3):
                    pool.memset(pad[j][:, 0:3], 0.0).then_inc(s["pool_done"], 1)
                pool.wait_ge(s["pool_done"], 4)

            @block.scalar
            def _(act):
                act.wait_ge(s["w_in"], 16 * len(loads))
                step = Chain(act, s["act_step"])
                step(act.activation(cres[:, :], cres[:, :], ACT.Sigmoid))
                step(act.activation(tscr[:, 0:1], ltemp[:, :], ACT.Abs))
                step(act.activation(tscr[:, 0:1], tscr[:, 0:1], ACT.Exp, scale=-1.0))
                step(act.activation(tscr[:, 0:1], tscr[:, 0:1], ACT.Ln, bias=1.0))

            @block.vector
            def _(dve):
                dve.wait_ge(s["act_step"], 4)
                step = Chain(dve, s["dve_step"])
                step(dve.scalar_tensor_tensor(tscr[:, 1:2], ltemp[:, :], 0.0, tscr[:, 0:1], ALU.max, ALU.add))
                step(dve.reciprocal(itemp[:, :], tscr[:, 1:2]))

        stage(nc, "w_in pool_done act_step dve_step", 1, setup)

        def body(block, b, s):
            xb = X[:, ds(b, 1), :].rearrange("p a t -> p (a t)")

            @block.tensor
            def _(pe):
                ln_tensor(pe, s, xb, mean_w[:, :], sq[:, :], PS[:, 0, :], PS[:, 1, :])
                pe.wait_ge(s["ln_out"], 1)
                for j, n in enumerate(("qwT", "kwT", "vwT", "bwT")):
                    pe.matmul(PS[:, 2 + j, :], w[n][:, :], hn[:, :], start=True, stop=True).then_inc(s["proj"], 1)
                for j in range(2):
                    pe.wait_ge(s["qk_sq"], j + 1)
                    pe.matmul(PS[:, j, :], blk[:, :], sqr[:, j, :], start=True, stop=True).then_inc(s["qk_ss"], 1)

                def blocks(bank, a, c, done):
                    for n in range(NCH):
                        for h in range(H0):
                            r, f = slice(32 * h, 32 * h + 32), slice(CH * n, CH * n + CH)
                            mm = pe.matmul(PS[r, bank, f], a[r, f], c[r, f], start=True, stop=True,
                                           tile_position=(32 * h, 32 * h))
                    mm.then_inc(done, 1)

                pe.wait_ge(s["kb_ready"], 3)
                blocks(2, kb, kn, s["mm_M"])
                blocks(3, kn, qn, s["mm_AT"])
                for lev in range(4):
                    pe.wait_ge(s["inv_in"], lev + 1)
                    blocks(4, LT, Xi, s["mm_Y"])
                    pe.wait_ge(s["y_ready"], lev + 1)
                    if lev < 3:
                        blocks(5, Zi, Y, s["mm_XY"])
                    else:
                        blocks(5, Y, Zi, s["mm_XY"])
                pe.wait_ge(s["inv_out"], 1)
                blocks(6, Zi, vbR, s["mm_u"])
                blocks(7, kbR, Zi, s["mm_w"])
                pe.wait_ge(s["uw_ready"], 2)
                for n in range(NCH):
                    f = slice(CH * n, CH * n + CH)
                    pe.wait_ge(s["state"], n + 1)
                    for h in range(H0):
                        r = slice(32 * h, 32 * h + 32)
                        mm = pe.matmul(PS[r, 2, 0:D0], WT[r, f], S[r, :], start=True, stop=True,
                                       tile_position=(32 * h, 32 * h))
                    mm.then_inc(s["mm_ws"], 1)
                    for h in range(H0):
                        r = slice(32 * h, 32 * h + 32)
                        mm = pe.matmul(PS[r, 3, f], qn[r, f], S[r, :], start=True, stop=False,
                                       tile_position=(32 * h, 32 * h))
                    pe.wait_ge(s["ua_ready"], n + 1)
                    for h in range(H0):
                        r = slice(32 * h, 32 * h + 32)
                        mm = pe.matmul(PS[r, 4, 0:D0], kR[r, f], UA[r, :], start=True, stop=True,
                                       tile_position=(32 * h, 32 * h))
                    mm.then_inc(s["mm_ds"], 1)
                    for h in range(H0):
                        r = slice(32 * h, 32 * h + 32)
                        mm = pe.matmul(PS[r, 3, f], AT[r, f], UA[r, :], start=False, stop=True,
                                       tile_position=(32 * h, 32 * h))
                    mm.then_inc(s["mm_out"], 1)
                pe.wait_ge(s["src_ready"], 4)
                src = (SH, LO, DE, V)
                for k in range(4):
                    pe.wait_ge(s["src_abs"], k + 1)
                    pe.matmul(PS[:, 0, :], sel[:, k, 0, :], src[k][:, :], start=(k == 0), stop=False)
                    mm = pe.matmul(PS[:, 0, :], sel[:, k, 1, :], ab[:, k, :], start=False, stop=(k == 3))
                mm.then_inc(s["mm_stat"], 1)
                for k in range(4):
                    pe.wait_ge(s["src_sq"], k + 1)
                    mm = pe.matmul(PS[:, 1, :], sel[:, k, 2, :], sqr[:, k, :], start=(k == 0), stop=(k == 3))
                mm.then_inc(s["mm_stat"], 1)
                pe.wait_ge(s["stat_ready"], 1)
                for h in range(H0):
                    r = slice(32 * h, 32 * h + 32)
                    pe.matmul(PS[:, 4 + h, :], w["mlp1h"][:, :], hn[:, :], start=True, stop=False)
                    pe.matmul(PS[:, 4 + h, :], w["mlp1s"][r, :], st[r, :], start=False, stop=True,
                              tile_position=(32 * h, 0)).then_inc(s["mm_h1"], 1)
                for h in range(H0):
                    pe.wait_ge(s["h1_ready"], h + 1)
                    for t in range(4):
                        mm = pe.matmul(PS[:, 2, t * 16 + h * 4:t * 16 + h * 4 + 4],
                                       h1[:, h, t * P:(t + 1) * P], mlp2T[:, :], start=True, stop=True)
                mm.then_inc(s["mm_lg"], 1)
                pe.wait_ge(s["p_ready"], 1)
                for t in range(4):
                    mm = pe.transpose(PS[0:16, 3, t * P:(t + 1) * P], pr[:, t * 16:(t + 1) * 16], ident[:, :])
                mm.then_inc(s["mm_pT"], 1)
                pe.wait_ge(s["pT_ready"], 1)
                for k in range(4):
                    pe.matmul(PS[:, 4 + k, :], psel[:, k, :], pT[:, :], start=True, stop=True).then_inc(s["mm_P"], 1)
                pe.wait_ge(s["o_sq"], 1)
                pe.matmul(PS[:, 0, :], blk[:, :], sq[:, :], start=True, stop=True).then_inc(s["mm_oss"], 1)
                pe.wait_ge(s["o_ready"], 1)
                pe.matmul(PS[:, 1, :], w["owT"][:, :], o[:, :], start=True, stop=True).then_inc(s["mm_fin"], 1)

            @block.scalar
            def _(act):
                ln_scalar(act, s, xc[:, :], sq[:, :], PS[:, 1, :], rstd[:, :], eps[:, 0:1])
                for j in range(3):
                    act.wait_ge(s["proj"], j + 1)
                    act.activation(pad[j][:, 3:], PS[:, 2 + j, :], ACT.Copy).then_inc(s["pad_ready"], 1)
                act.wait_ge(s["proj"], 4)
                act.activation(beta[:, :], PS[:, 5, :], ACT.Sigmoid).then_inc(s["beta_raw"], 1)
                for j in range(3):
                    act.wait_ge(s["conv"], j + 1)
                    act.activation((qn[:, :], kn[:, :], V)[j], acc[j][:, :], ACT.Silu).then_inc(s["silu"], 1)
                for j in range(2):
                    act.wait_ge(s["silu"], j + 1)
                    act.activation(sqr[:, j, :], (qn, kn)[j][:, :], ACT.Square).then_inc(s["qk_sq"], 1)
                for j in range(2):
                    act.wait_ge(s["qk_ss"], j + 1)
                    act.activation(ab[:, j, :], PS[:, j, :], ACT.Ln, bias=eps[:, 1:2]).then_inc(s["rn_log"], 1)
                for j in range(2):
                    act.wait_ge(s["rn_log"], j + 1)
                    act.activation(ab[:, j, :], ab[:, j, :], ACT.Exp, scale=-0.5).then_inc(s["rn"], 1)
                act.wait_ge(s["mm_u"], 1)
                act.activation(U[:, :], PS[:, 6, :], ACT.Copy).then_inc(s["uw_ready"], 1)
                act.wait_ge(s["mm_w"], 1)
                act.activation(WT[:, :], PS[:, 7, :], ACT.Copy).then_inc(s["uw_ready"], 1)
                act.wait_ge(s["src_ready"], 4)
                for k, a in enumerate((SH[:, :], LO[:, :], DE[:, :], V)):
                    act.activation(ab[:, k, :], a, ACT.Abs).then_inc(s["src_abs"], 1)
                for k, a in enumerate((SH[:, :], LO[:, :], DE[:, :], V)):
                    act.activation(sqr[:, k, :], a, ACT.Square).then_inc(s["src_sq"], 1)
                act.wait_ge(s["mm_stat"], 2)
                act.activation(st[:, :], PS[:, 1, :], ACT.Sqrt, scale=stm[:, 2:3]).then_inc(s["stat_sqrt"], 1)
                for h in range(H0):
                    act.wait_ge(s["mm_h1"], h + 1)
                    act.activation(h1[:, h, :], PS[:, 4 + h, :], ACT.Gelu_apprx_tanh, bias=mlp1b[:, 0:1])\
                       .then_inc(s["h1_ready"], 1)
                act.wait_ge(s["lg_ready"], 1)
                act.activation(pr[:, :], lg[:, :], ACT.Exp, scale=itemp[:, 0:1]).then_inc(s["lg_exp"], 1)
                act.wait_ge(s["mm_pT"], 1)
                act.activation(pT[:, :], PS[0:16, 3, :], ACT.Copy).then_inc(s["pT_ready"], 1)
                act.wait_ge(s["o_mix"], 1)
                act.activation(sq[:, :], o[:, :], ACT.Square).then_inc(s["o_sq"], 1)
                act.wait_ge(s["mm_oss"], 1)
                act.activation(rstd[:, :], PS[:, 0, :], ACT.Ln, bias=eps[:, 0:1], scale=1.0 / D0).then_inc(s["o_log"], 1)
                act.wait_ge(s["o_log"], 1)
                act.activation(rstd[:, :], rstd[:, :], ACT.Exp, scale=-0.5).then_inc(s["o_rstd"], 1)

            @block.vector
            def _(dve):
                step = Chain(dve, s["dve_step"])
                step(dve.tensor_copy(mod[:, :], MOD[:, ds(b, 1), :].rearrange("p a j -> p (a j)")))
                ln_vector(dve, s, xb, xc[:, :], PS[:, 0, :], rstd[:, :], mod[:, 1:2], mod[:, 0:1], hn[:, :])
                for j in range(3):
                    dve.wait_ge(s["pad_ready"], j + 1)
                    step(dve.tensor_scalar(acc[j][:, :], pad[j][:, 3:3 + T], cw[:, j, 3:4], None, ALU.mult))
                    for k in range(3):
                        ins = dve.scalar_tensor_tensor(acc[j][:, :], pad[j][:, k:k + T], cw[:, j, k:k + 1],
                                                       acc[j][:, :], ALU.mult, ALU.add)
                        if k < 2:
                            step(ins)
                    ins.then_inc(s["conv"], 1)
                dve.wait_ge(s["beta_raw"], 1)
                step(dve.tensor_scalar(beta[:, :], beta[:, :], 1e-6, None, ALU.max))
                dve.wait_ge(s["silu"], 3)
                step(dve.tensor_tensor(vb[:, :], V, beta[:, :], ALU.mult))
                dve.wait_ge(s["rn"], 2)
                step(dve.tensor_tensor(kn[:, :], kn[:, :], ab[:, 1, :], ALU.mult))
                dve.tensor_tensor(qn[:, :], qn[:, :], ab[:, 0, :], ALU.mult).then_inc(s["kb_ready"], 1)
                dve.tensor_tensor(kb[:, :], kn[:, :], beta[:, :], ALU.mult).then_inc(s["kb_ready"], 1)
                dve.wait_ge(s["kb_ready"], 2)
                dve.transpose(kR[:, :], kn[:, :]).then_inc(s["kb_ready"], 1)
                step(dve.transpose(vbR[:, :], vb[:, :]))
                step(dve.transpose(kbR[:, :], kb[:, :]))
                dve.wait_ge(s["mm_M"], 1)
                step(dve.tensor_tensor(c3(M[:, :]), c3(PS[:, 2, :]), mask(0), ALU.mult))
                step(dve.transpose(MT[:, :], M[:, :]))
                dve.wait_ge(s["mm_AT"], 1)
                step(dve.tensor_tensor(c3(AT[:, :]), c3(PS[:, 3, :]), mask(1), ALU.mult))
                step(dve.tensor_tensor(c3(M[:, :]), c3(M[:, :]), mask(3), ALU.mult))
                step(dve.tensor_tensor(c3(Xi[:, :]), mask(2), c3(M[:, :]), ALU.subtract))
                for lev in range(4):
                    step(dve.transpose(Zi[:, :], Xi[:, :]))
                    dve.tensor_tensor(c3(LT[:, :]), c3(MT[:, :]), mask(4 + lev), ALU.mult).then_inc(s["inv_in"], 1)
                    dve.wait_ge(s["mm_Y"], lev + 1)
                    dve.tensor_copy(Y[:, :], PS[:, 4, :]).then_inc(s["y_ready"], 1)
                    dve.wait_ge(s["mm_XY"], lev + 1)
                    if lev < 3:
                        step(dve.tensor_tensor(Xi[:, :], Xi[:, :], PS[:, 5, :], ALU.subtract))
                    else:
                        dve.tensor_tensor(Zi[:, :], Zi[:, :], PS[:, 5, :], ALU.subtract).then_inc(s["inv_out"], 1)
                dve.memset(S[:, :], 0.0).then_inc(s["state"], 1)
                taps = [(SH, firs, FIR_S, k) for k in range(FIR_S)] + [(LO, firl, FIR_L, k) for k in range(FIR_L)]

                def tap():
                    if taps:
                        dst, f, K, k = taps.pop(0)
                        src = vpad[:, FIR_L - K + k:FIR_L - K + k + T]
                        if k == 0:
                            step(dve.tensor_scalar(dst[:, :], src, f[:, 0:1], None, ALU.mult))
                        else:
                            step(dve.scalar_tensor_tensor(dst[:, :], src, f[:, k:k + 1], dst[:, :],
                                                          ALU.mult, ALU.add))
                dve.wait_ge(s["uw_ready"], 2)
                for n in range(NCH):
                    f = slice(CH * n, CH * n + CH)
                    tap()
                    dve.wait_ge(s["mm_ws"], n + 1)
                    if n:
                        dve.wait_ge(s["mm_out"], n)
                    dve.tensor_tensor(UA[:, :], U[:, f], PS[:, 2, 0:D0], ALU.subtract).then_inc(s["ua_ready"], 1)
                    tap()
                    tap()
                    dve.wait_ge(s["mm_ds"], n + 1)
                    dve.wait_ge(s["state"], n + 1)
                    dve.tensor_tensor(S[:, :], S[:, :], PS[:, 4, 0:D0], ALU.add).then_inc(s["state"], 1)
                    tap()
                    tap()
                while taps:
                    tap()
                dve.wait_ge(s["mm_out"], NCH)
                dve.transpose(DE[:, :], PS[:, 3, :]).then_inc(s["src_ready"], 4)
                dve.wait_ge(s["mm_stat"], 2)
                step(dve.tensor_copy(o[:, :], PS[:, 0, :]))
                step(dve.scalar_tensor_tensor(sq[:, :], o[:, :], stm[:, 1:2], o[:, :], ALU.mult, ALU.mult))
                dve.wait_ge(s["stat_sqrt"], 1)
                step(dve.scalar_tensor_tensor(sq[:, :], PS[:, 1, :], stm[:, 1:2], sq[:, :], ALU.mult, ALU.subtract))
                step(dve.scalar_tensor_tensor(sq[:, :], o[:, :], stm[:, 0:1], sq[:, :], ALU.mult, ALU.add))
                dve.tensor_tensor(st[:, :], st[:, :], sq[:, :], ALU.add).then_inc(s["stat_ready"], 1)
                dve.wait_ge(s["mm_lg"], 1)

                def g4(a):
                    return a.rearrange("p (g k) -> p g k", k=4)

                def bc(a):
                    return a.rearrange("p (g k) -> p g k", k=1).broadcast_to([P, 16, 4])
                step(dve.tensor_tensor(g4(lg[:, :]), g4(PS[:, 2, 0:64]),
                                       mlp2b[:, :].rearrange("p (g k) -> p g k", g=1).broadcast_to([P, 16, 4]), ALU.add))
                step(dve.tensor_reduce(m16[:, :], g4(lg[:, :]), AX, ALU.max))
                dve.tensor_tensor(g4(lg[:, :]), g4(lg[:, :]), bc(m16[:, :]), ALU.subtract).then_inc(s["lg_ready"], 1)
                dve.wait_ge(s["lg_exp"], 1)
                step(dve.tensor_reduce(m16[:, :], g4(pr[:, :]), AX, ALU.add))
                step(dve.reciprocal(r16[:, :], m16[:, :]))
                step(dve.tensor_tensor(g4(pr[:, :]), g4(pr[:, :]), bc(r16[:, :]), ALU.mult))
                step(dve.tensor_scalar(pr[:, :], pr[:, :], PROB_FLOOR, None, ALU.max))
                step(dve.tensor_reduce(m16[:, :], g4(pr[:, :]), AX, ALU.add))
                step(dve.reciprocal(r16[:, :], m16[:, :]))
                dve.tensor_tensor(g4(pr[:, :]), g4(pr[:, :]), bc(r16[:, :]), ALU.mult).then_inc(s["p_ready"], 1)
                dve.wait_ge(s["mm_P"], 1)
                step(dve.scalar_tensor_tensor(o[:, :], PS[:, 4, :], cres[:, 0:1], SH[:, :], ALU.add, ALU.mult))
                for k, a in ((1, LO[:, :]), (2, DE[:, :]), (3, V)):
                    dve.wait_ge(s["mm_P"], k + 1)
                    step(dve.tensor_tensor(xc[:, :], a, PS[:, 4 + k, :], ALU.mult))
                    ins = dve.tensor_tensor(o[:, :], o[:, :], xc[:, :], ALU.add)
                    if k < 3:
                        step(ins)
                ins.then_inc(s["o_mix"], 1)
                dve.wait_ge(s["o_rstd"], 1)
                dve.scalar_tensor_tensor(o[:, :], o[:, :], normw[:, 0:1], rstd[:, :], ALU.mult, ALU.mult)\
                   .then_inc(s["o_ready"], 1)
                dve.wait_ge(s["mm_fin"], 1)
                dve.scalar_tensor_tensor(xb, PS[:, 1, :], mod[:, 2:3], xb, ALU.mult, ALU.add).then_inc(s["dve_step"], 1)

        stage(nc, LN_SEMS + "proj pad_ready beta_raw conv silu qk_sq qk_ss rn_log rn kb_ready mm_M mm_AT inv_in "
              "mm_Y y_ready mm_XY inv_out mm_u mm_w uw_ready state mm_ws ua_ready mm_ds mm_out src_ready src_abs "
              "src_sq mm_stat stat_sqrt stat_ready mm_h1 h1_ready mm_lg lg_ready lg_exp p_ready mm_pT pT_ready mm_P "
              "o_mix o_sq mm_oss o_log o_rstd o_ready mm_fin dve_step", NB, body)


def experts_stage(nc, dram, g, PS):
    X, MOD, eps, mean_w, ident = g.X, g.MOD0, g.eps, g.mean_w, g.ident
    NE = 8
    with ExitStack() as ctx:
        def sb(n, shape):
            return ctx.enter_context(nc.sbuf_tensor("moe_" + n, shape, F32))
        w1, w2 = sb("m_w1", [P, NE + 1, P]), sb("m_w2", [P, NE + 1, P])
        gw, lb, tri, esel = sb("m_gw", [P, NE]), sb("m_lb", [P, NE]), sb("m_tri", [P, NE, NE]), sb("m_esel", [NE, NE, P])
        xc, sq, rstd, hn = sb("xc", [P, T]), sb("sq", [P, T]), sb("rstd", [P, T]), sb("hn", [P, T])
        lgt, lgb, sg = sb("lgt", [P, 4, NE]), sb("lgb", [P, 4, NE]), sb("sg", [P, 4, NE])
        gt, eq = sb("gt", [P, 4, NE, NE]), sb("eq", [P, 4, NE, NE])
        cnt, ws, wr = sb("cnt", [P, 4, NE]), sb("ws", [P, 4]), sb("wr", [P, 4])
        weT = sb("weT", [NE, T])
        relu, act2, hid = sb("relu", [P, 2, T]), sb("act2", [P, 2, T]), sb("hid", [P, 2, T])
        mod = sb("mod", [P, 6])
        loads = [(w1[:, :, :], dram["w1"]), (w2[:, :, :], dram["w2"]), (gw[:, :], dram["gate_wT"]),
                 (lb[:, :], dram["lb_bias"]), (tri[:, :, :], dram["tri8"]), (esel[:, :, :], dram["esel"])]

        def setup(block, i, s):
            @block.sync
            def _(sp):
                for tile, src in loads:
                    sp.dma_start(tile, src).then_inc(s["w_in"], 16)
                sp.wait_ge(s["w_in"], 16 * len(loads))
        stage(nc, "w_in", 1, setup)

        def body(block, b, s):
            xb = X[:, ds(b, 1), :].rearrange("p a t -> p (a t)")

            @block.tensor
            def _(pe):
                ln_tensor(pe, s, xb, mean_w[:, :], sq[:, :], PS[:, 0, :], PS[:, 1, :])
                pe.wait_ge(s["ln_out"], 1)
                for t in range(4):
                    mm = pe.matmul(PS[:, 2, t * NE:(t + 1) * NE], hn[:, t * P:(t + 1) * P], gw[:, :],
                                   start=True, stop=True)
                mm.then_inc(s["mm_lg"], 1)

                def up(e):
                    if e >= 2:
                        pe.wait_ge(s["act_relu"], e - 1)
                    pe.matmul(PS[:, 4 + e % 2, :], w1[:, e, :], hn[:, :], start=True, stop=True).then_inc(s["mm_up"], 1)

                def spread(e):
                    if e >= 2:
                        pe.wait_ge(s["hid_ready"], e - 1)
                    pe.matmul(PS[:, 6 + e % 2, :], esel[:, e, :], weT[:, :], start=True, stop=True).then_inc(s["mm_we"], 1)

                def down(e):
                    if e < NE:
                        pe.wait_ge(s["hid_ready"], e + 1)
                    else:
                        pe.wait_ge(s["act_sq"], e + 1)
                    rhs = hid[:, e % 2, :] if e < NE else act2[:, e % 2, :]
                    pe.matmul(PS[:, 1, :], w2[:, e, :], rhs, start=(e == 0), stop=(e == NE)).then_inc(s["mm_down"], 1)
                up(0)
                up(1)
                pe.wait_ge(s["we_ready"], 1)
                for t in range(4):
                    mm = pe.transpose(PS[0:NE, 3, t * P:(t + 1) * P], cnt[:, t, :], ident[:, :])
                mm.then_inc(s["mm_weT"], 1)
                pe.wait_ge(s["weT_ready"], 1)
                spread(0)
                for e in range(NE + 1):
                    if e + 2 <= NE:
                        up(e + 2)
                    if e + 1 < NE:
                        spread(e + 1)
                    down(e)

            @block.scalar
            def _(act):
                ln_scalar(act, s, xc[:, :], sq[:, :], PS[:, 1, :], rstd[:, :], eps[:, 0:1])
                act.wait_ge(s["lg_ready"], 1)
                act.activation(sg[:, :, :], lgt[:, :, :], ACT.Sigmoid).then_inc(s["sig_ready"], 1)
                act.wait_ge(s["mm_weT"], 1)
                act.activation(weT[:, :], PS[0:NE, 3, :], ACT.Copy).then_inc(s["weT_ready"], 1)
                for e in range(NE + 1):
                    act.wait_ge(s["mm_up"], e + 1)
                    act.activation(relu[:, e % 2, :], PS[:, 4 + e % 2, :], ACT.Relu).then_inc(s["act_relu"], 1)
                    act.wait_ge(s["act_relu"], e + 1)
                    if e >= 2:
                        act.wait_ge(s["hid_ready"], e - 1)
                    act.activation(act2[:, e % 2, :], relu[:, e % 2, :], ACT.Square).then_inc(s["act_sq"], 1)

            @block.vector
            def _(dve):
                step = Chain(dve, s["dve_step"])
                step(dve.tensor_copy(mod[:, :], MOD[:, ds(b, 1), :].rearrange("p a j -> p (a j)")))
                ln_vector(dve, s, xb, xc[:, :], PS[:, 0, :], rstd[:, :], mod[:, 4:5], mod[:, 3:4], hn[:, :])
                dve.wait_ge(s["mm_lg"], 1)
                dve.tensor_copy(lgt[:, :, :], PS[:, 2, 0:4 * NE].rearrange("p (t e) -> p t e", e=NE)).then_inc(s["lg_ready"], 1)
                dve.wait_ge(s["lg_ready"], 1)
                bias = lb[:, :].rearrange("p (t e) -> p t e", t=1).broadcast_to([P, 4, NE])
                step(dve.tensor_tensor(lgb[:, :, :], lgt[:, :, :], bias, ALU.add))
                other = lgb[:, :, :].rearrange("p t (a e) -> p t a e", a=1).broadcast_to([P, 4, NE, NE])
                own = lgb[:, :, :].rearrange("p t (e a) -> p t e a", a=1).broadcast_to([P, 4, NE, NE])
                below = tri[:, :, :].rearrange("p (a e) f -> p a e f", a=1).broadcast_to([P, 4, NE, NE])
                step(dve.tensor_tensor(gt[:, :, :, :], other, own, ALU.is_gt))
                step(dve.tensor_tensor(eq[:, :, :, :], other, own, ALU.is_equal))
                step(dve.tensor_tensor(eq[:, :, :, :], eq[:, :, :, :], below, ALU.mult))
                step(dve.tensor_tensor(gt[:, :, :, :], gt[:, :, :, :], eq[:, :, :, :], ALU.add))
                step(dve.tensor_reduce(cnt[:, :, :], gt[:, :, :, :], AX, ALU.add))
                dve.wait_ge(s["sig_ready"], 1)
                step(dve.scalar_tensor_tensor(cnt[:, :, :], cnt[:, :, :], 1.5, sg[:, :, :], ALU.is_lt, ALU.mult))
                step(dve.tensor_reduce(ws[:, :], cnt[:, :, :], AX, ALU.add))
                step(dve.tensor_scalar(ws[:, :], ws[:, :], 1e-6, None, ALU.add))
                step(dve.reciprocal(wr[:, :], ws[:, :]))
                wrb = wr[:, :].rearrange("p (t a) -> p t a", a=1).broadcast_to([P, 4, NE])
                dve.tensor_tensor(cnt[:, :, :], cnt[:, :, :], wrb, ALU.mult).then_inc(s["we_ready"], 1)
                for e in range(NE):
                    dve.wait_ge(s["act_sq"], e + 1)
                    dve.wait_ge(s["mm_we"], e + 1)
                    if e >= 2:
                        dve.wait_ge(s["mm_down"], e - 1)
                    dve.tensor_tensor(hid[:, e % 2, :], act2[:, e % 2, :], PS[:, 6 + e % 2, :], ALU.mult)\
                       .then_inc(s["hid_ready"], 1)
                dve.wait_ge(s["mm_down"], NE + 1)
                dve.scalar_tensor_tensor(xb, PS[:, 1, :], mod[:, 5:6], xb, ALU.mult, ALU.add).then_inc(s["dve_step"], 1)

        stage(nc, LN_SEMS + "mm_lg mm_up mm_we mm_down mm_weT weT_ready we_ready act_relu act_sq hid_ready "
              "lg_ready sig_ready dve_step", NB, body)


H1, D1 = 16, 8
TOPK = T // 4
TAKEN = -1e30
GH = 2
NT = 4 * GH
NG = H1 // GH
COUNTS = 5
ACT_COUNTS = 2
AIM = TOPK - 4.3
Z0, SLOPE, REACH = 0.697, 0.313 * T, 0.8


def topk_attention_stage(nc, dram, g, PS):
    X, MOD, eps, mean_w, ident = g.X, g.MOD1, g.eps, g.mean_w, g.ident
    with ExitStack() as ctx:
        def sb(n, shape, dt=F32):
            return ctx.enter_context(nc.sbuf_tensor("topk_" + n, shape, dt))
        w = {n: sb("t_" + n, [P, P]) for n in ("Wq", "Wk", "Wv", "Wo", "Wg", "blk8", "bv")}
        col = {n: sb("t_" + n, [P, 1]) for n in ("bq", "bk", "bo", "bg", "bt", "Wt")}
        hm, rank, ones = sb("hm", [P, H1]), sb("rank", [P, 8]), sb("ones", [P, 1])
        loads = [(w[n][:, :], dram["t_" + n]) for n in w] + [(col[n][:, :], dram["t_" + n]) for n in col]
        loads += [(hm[:, :], dram["hm"]), (rank[:, :], dram["rank"])]
        xc, sq, rstd, hn = sb("xc", [P, T]), sb("sq", [P, T]), sb("rstd", [P, T]), sb("hn", [P, T])
        qk, qks, gate = sb("qk", [P, 2, T]), sb("qks", [P, 2, T]), sb("gate", [P, T])
        Vt, OUT, OT = sb("Vt", [P, 4, H1, D1 + 1]), sb("OUT", [P, 4, H1, D1]), sb("OT", [P, T])
        hsum, itemp, kbm = sb("hsum", [P, 2]), sb("itemp", [P, 2]), sb("kbm", [P, H1])
        qm = sb("qm", [P, 2, T])
        NC_ = H1 * 4
        tc, lo, hi, dif = (sb(n, [P, 2, NC_]) for n in ("tc", "lo", "hi", "dif"))
        mean, sd, signs, rec = (sb(n, [P, NC_]) for n in ("mean", "sd", "signs", "rec"))
        up, dn = sb("up", [P, NC_], mybir.dt.int32), sb("dn", [P, NC_], mybir.dt.int32)
        S, E, W = sb("S", [P, 3 * NT, T]), sb("E", [P, 3 * NT, T]), sb("W", [P, 2 * NT, T])
        above, junk = sb("above", [P, 2, T], mybir.dt.bfloat16), sb("junk", [P, 2 * ACT_COUNTS, T], mybir.dt.bfloat16)
        m8, keep, bad = sb("m8", [P, NT, 8]), sb("keep", [P, NT, 8]), sb("bad", [P, 2, NT])
        nbad = sb("nbad", [1, NT + 1], mybir.dt.int32)
        nbad_sum = sb("nbad_sum", [1, 1])
        prec = sb("prec", [P, NT])
        PT = sb("PT", [P, 2, T])
        mod = sb("mod", [P, 6])

        def setup(block, i, s):
            @block.sync
            def _(sp):
                for tile, src in loads:
                    sp.dma_start(tile, src).then_inc(s["w_in"], 16)
                sp.wait_ge(s["w_in"], 16 * len(loads))

            @block.gpsimd
            def _(pool):
                pool.memset(Vt[:, :, :, D1:], 1.0).then_inc(s["ones"], 1)
                pool.wait_ge(s["ones"], 1)
                pool.memset(ones[:, :], 1.0).then_inc(s["ones"], 1)
                pool.wait_ge(s["ones"], 2)
        stage(nc, "w_in ones", 1, setup)

        def project(block, b, s):
            xb = X[:, ds(b, 1), :].rearrange("p a t -> p (a t)")

            @block.tensor
            def _(pe):
                ln_tensor(pe, s, xb, mean_w[:, :], sq[:, :], PS[:, 0, :], PS[:, 1, :])
                pe.wait_ge(s["ln_out"], 1)
                for j, n in enumerate(("Wq", "Wk", "Wg")):
                    pe.matmul(PS[:, 2 + j, :], w[n][:, :], hn[:, :], start=True, stop=True).then_inc(s["mm_proj"], 1)
                for t in range(4):
                    mm = pe.matmul(PS[:, 5, t * P:(t + 1) * P], hn[:, t * P:(t + 1) * P], w["Wv"][:, :],
                                   start=True, stop=True)
                mm.then_inc(s["mm_v"], 1)
                for j in range(2):
                    pe.wait_ge(s["qk_sq"], j + 1)
                    pe.matmul(PS[:, j, :], w["blk8"][:, :], qks[:, j, :], start=True, stop=True).then_inc(s["mm_ss"], 1)
                pe.wait_ge(s["mean_ready"], 1)
                pe.matmul(PS[:, 6, 0:1], hsum[:, 0:1].broadcast_to([P, P]), col["Wt"][:, :], start=True, stop=True)\
                  .then_inc(s["mm_temp"], 1)
                pe.wait_ge(s["qk_norm"], 2)
                for t in range(4):
                    mm = pe.transpose(PS[:, 2, t * P:(t + 1) * P], qk[:, 1, t * P:(t + 1) * P], ident[:, :])
                mm.then_inc(s["mm_kT"], 1)
                pe.wait_ge(s["kT_ready"], 1)
                for t in range(4):
                    mm = pe.matmul(PS[:, 3, 0:P], sq[:, t * P:(t + 1) * P], sq[:, t * P:(t + 1) * P],
                                   start=(t == 0), stop=(t == 3))
                mm.then_inc(s["mm_C"], 1)
                pe.wait_ge(s["C_ready"], 1)
                pe.matmul(PS[:, 4, :], rstd[:, 0:P], qk[:, 0, :], start=True, stop=True).then_inc(s["mm_CQ"], 1)
                pe.wait_ge(s["qcq_ready"], 1)
                for t in range(4):
                    tt = slice(t * P, (t + 1) * P)
                    pe.matmul(PS[:, 7, t * H1:(t + 1) * H1], qk[:, 0, tt], kbm[:, :], start=True, stop=True)
                    mm = pe.matmul(PS[:, 7, (4 + t) * H1:(5 + t) * H1], xc[:, tt], hm[:, :], start=True, stop=True)
                mm.then_inc(s["mm_mom"], 1)

            @block.scalar
            def _(act):
                ln_scalar(act, s, xc[:, :], sq[:, :], PS[:, 1, :], rstd[:, :], eps[:, 0:1])
                for j, n in enumerate(("bq", "bk")):
                    act.wait_ge(s["mm_proj"], j + 1)
                    act.activation(qk[:, j, :], PS[:, 2 + j, :], ACT.Identity, bias=col[n][:, 0:1]).then_inc(s["qk_ready"], 1)
                for j in range(2):
                    act.wait_ge(s["qk_ready"], j + 1)
                    act.activation(qks[:, j, :], qk[:, j, :], ACT.Square).then_inc(s["qk_sq"], 1)
                act.wait_ge(s["mm_proj"], 3)
                act.activation(gate[:, :], PS[:, 4, :], ACT.Sigmoid, bias=col["bg"][:, 0:1]).then_inc(s["gate_ready"], 1)
                act.wait_ge(s["mm_temp"], 1)
                act.activation(itemp[:, 0:1], PS[:, 6, 0:1], ACT.Sigmoid, bias=col["bt"][:, 0:1], scale=1.0 / T)\
                   .then_inc(s["temp_sig"], 1)
                for j in range(2):
                    act.wait_ge(s["mm_ss"], j + 1)
                    act.activation(qks[:, j, :], PS[:, j, :], ACT.Sqrt).then_inc(s["norm_ready"], 1)
                act.wait_ge(s["mm_kT"], 1)
                act.activation(sq[:, :], PS[:, 2, :], ACT.Copy).then_inc(s["kT_ready"], 1)
                act.wait_ge(s["var_ready"], 1)
                act.activation(sd[:, :], sd[:, :], ACT.Sqrt).then_inc(s["sd_ready"], 1)

            @block.vector
            def _(dve):
                step = Chain(dve, s["dve_step"])
                step(dve.tensor_copy(mod[:, :], MOD[:, ds(b, 1), :].rearrange("p a j -> p (a j)")))
                ln_vector(dve, s, xb, xc[:, :], PS[:, 0, :], rstd[:, :], mod[:, 1:2], mod[:, 0:1], hn[:, :])
                dve.wait_ge(s["ln_out"], 1)
                dve.tensor_reduce(hsum[:, 0:1], hn[:, :], AX, ALU.add).then_inc(s["mean_ready"], 1)
                dve.wait_ge(s["mm_v"], 1)
                bv = w["bv"][:, :].rearrange("p (a h c) -> p a h c", a=1, c=D1).broadcast_to([P, 4, H1, D1])
                step(dve.tensor_tensor(Vt[:, :, :, 0:D1],
                                       PS[:, 5, :].rearrange("p (t h c) -> p t h c", t=4, c=D1), bv, ALU.add))
                dve.wait_ge(s["temp_sig"], 1)
                step(dve.tensor_scalar(itemp[:, 0:1], itemp[:, 0:1], 0.5, None, ALU.add))
                step(dve.reciprocal(itemp[:, 1:2], itemp[:, 0:1]))
                for j in range(2):
                    dve.wait_ge(s["norm_ready"], j + 1)
                    step(dve.tensor_scalar(qks[:, j, :], qks[:, j, :], 1e-12, None, ALU.max))
                    step(dve.reciprocal(qks[:, j, :], qks[:, j, :]))
                    sc = itemp[:, 1:2] if j == 0 else 1.0
                    dve.scalar_tensor_tensor(qk[:, j, :], qk[:, j, :], sc, qks[:, j, :], ALU.mult, ALU.mult)\
                       .then_inc(s["qk_norm"], 1)
                dve.wait_ge(s["qk_norm"], 2)
                step(dve.tensor_reduce(hsum[:, 1:2], qk[:, 1, :], AX, ALU.add))
                step(dve.tensor_scalar(kbm[:, :], hm[:, :], hsum[:, 1:2], 1.0 / T, ALU.mult, ALU.mult))
                dve.wait_ge(s["mm_C"], 1)
                dve.scalar_tensor_tensor(rstd[:, 0:P], PS[:, 3, 0:P], 1.0 / T, w["blk8"][:, :], ALU.mult, ALU.mult)\
                   .then_inc(s["C_ready"], 1)
                dve.wait_ge(s["mm_CQ"], 1)
                dve.tensor_tensor(xc[:, :], qk[:, 0, :], PS[:, 4, :], ALU.mult).then_inc(s["qcq_ready"], 1)
                dve.wait_ge(s["mm_mom"], 1)

                def by_head(bank_cols):
                    return bank_cols.rearrange("p (t h) -> p h t", t=4)
                h4 = "p (h t) -> p h t"
                step(dve.tensor_copy(mean[:, :].rearrange(h4, t=4), by_head(PS[:, 7, 0:4 * H1])))
                step(dve.tensor_tensor(rec[:, :], mean[:, :], mean[:, :], ALU.mult))
                step(dve.tensor_tensor(sd[:, :].rearrange(h4, t=4), by_head(PS[:, 7, 4 * H1:8 * H1]),
                                       rec[:, :].rearrange(h4, t=4), ALU.subtract))
                dve.tensor_scalar(sd[:, :], sd[:, :], 1e-12, None, ALU.max).then_inc(s["var_ready"], 1)
                dve.wait_ge(s["sd_ready"], 1)
                for tile, z, c in ((tc, Z0, 0.0), (lo, Z0 - REACH, AIM + REACH * SLOPE), (hi, Z0 + REACH, AIM - REACH * SLOPE)):
                    step(dve.scalar_tensor_tensor(tile[:, 0, :], sd[:, :], z, mean[:, :], ALU.mult, ALU.add))
                    step(dve.memset(tile[:, 1, :], c))

        def search(block, b, s):
            def S_(n):
                return S[:, n % (3 * NT), :]

            def E_(n):
                return E[:, n % (3 * NT), :]

            def W_(n):
                return W[:, n % (2 * NT), :]

            @block.tensor
            def _(pe):
                def score(n):
                    h, t = n // 4, n % 4
                    pe.wait_ge(s["q_ready"], h + 1)
                    if n >= 4:
                        pe.wait_ge(s["exp_ready"], n - 3)
                    pe.matmul(PS[:, n % 4, :], qm[:, h % 2, t * P:(t + 1) * P], qk[:, 1, :], start=True, stop=True)\
                      .then_inc(s["mm_score"], 1)

                def turn(n):
                    pe.wait_ge(s["p_ready"], n + 1)
                    if n >= 2:
                        pe.wait_ge(s["pT_ready"], n - 1)
                    for k in range(4):
                        mm = pe.transpose(PS[:, 4 + n % 2, k * P:(k + 1) * P], E_(n)[:, k * P:(k + 1) * P], ident[:, :])
                    mm.then_inc(s["mm_pT"], 1)

                def values(n):
                    gr, i = n // NT, n % NT
                    pe.wait_ge(s["pT_ready"], n + 1)
                    if i == 0 and gr >= 2:
                        pe.wait_ge(s["out_ready"], gr - 1)
                    for k in range(4):
                        mm = pe.matmul(PS[:, 6 + gr % 2, i * (D1 + 1):(i + 1) * (D1 + 1)],
                                       PT[:, n % 2, k * P:(k + 1) * P], Vt[:, k, n // 4, :],
                                       start=(k == 0), stop=(k == 3))
                    mm.then_inc(s["mm_pv"], 1)

                for n in range(2 * NT):
                    score(n)
                for gr in range(NG + 1):
                    if gr >= 1:
                        if gr >= 3:
                            pe.wait_ge(s["out_ready"], gr - 2)
                        pe.wait_ge(s["bad_ready"], gr)
                        pe.matmul(PS[0:1, 6 + (gr - 1) % 2, 128:128 + NT], ones[:, :],
                                  bad[:, (gr - 1) % 2, :],
                                  start=True, stop=True).then_inc(s["mm_bad"], 1)
                    for i in range(NT + 1):
                        if gr + 2 < NG and i < NT:
                            score((gr + 2) * NT + i)
                        if gr >= 1 and i < NT:
                            turn((gr - 1) * NT + i)
                        if gr >= 1 and i >= 1:
                            values((gr - 1) * NT + i - 1)

            @block.scalar
            def _(act):
                def load(n):
                    act.wait_ge(s["mm_score"], n + 1)
                    if n >= 3 * NT:
                        act.wait_ge(s["w_ready"], n // NT - 2)
                        act.wait_ge(s["mm_pT"], n - 3 * NT + 1)
                    act.activation(S_(n), PS[:, n % 4, :], ACT.Copy).then_inc(s["s_ready"], 1)
                    act.activation(E_(n), PS[:, n % 4, :], ACT.Exp).then_inc(s["exp_ready"], 1)

                def count(n, k):
                    if n % NT == 0 and k:
                        act.wait_ge(s["t_ready%d" % k], n // NT)
                    act.wait_ge(s["s_ready"], n + 1)
                    if n - NT >= 2:
                        act.wait_ge(s["act_count%d" % k], n - NT - 1)
                    act.activation(junk[:, 2 * k + n % 2, :], S_(n), ACT.Sign, bias=tc[:, 0, n:n + 1], scale=-1.0,
                                   accum_out=signs[:, n:n + 1]).then_inc(s["act_count%d" % k], 1)

                def rest(n):
                    act.wait_ge(s["w_ready"], n // NT + 1)
                    act.activation(W_(n), W_(n), ACT.Exp).then_inc(s["u_ready"], 1)

                def turned(n):
                    act.wait_ge(s["mm_pT"], n + 1)
                    if n >= 2:
                        act.wait_ge(s["mm_pv"], n - 1)
                    act.activation(PT[:, n % 2, :], PS[:, 4 + n % 2, :], ACT.Copy).then_inc(s["pT_ready"], 1)

                for n in range(2 * NT):
                    load(n)
                    if n >= NT:
                        count(n, 0)
                for gr in range(NG + 1):
                    if gr + 1 < NG:
                        for n in range((gr + 1) * NT, (gr + 2) * NT):
                            count(n, 1)
                    for i in range(NT + 3):
                        if gr >= 1 and i < NT:
                            rest((gr - 1) * NT + i)
                        if gr >= 1 and 2 <= i < NT + 2:
                            turned((gr - 1) * NT + i - 2)
                        if gr + 2 < NG and i >= 3:
                            load((gr + 2) * NT + i - 3)
                            count((gr + 2) * NT + i - 3, 0)

            @block.gpsimd
            def _(pool):
                def mask_q(h):
                    if h >= 2:
                        pool.wait_ge(s["mm_score"], 4 * (h - 1))
                    pool.tensor_scalar(qm[:, h % 2, :], qk[:, 0, :], hm[:, h:h + 1], 1.0, ALU.mult, ALU.mult)\
                        .then_inc(s["q_ready"], 1)
                for h in range(3 * GH):
                    mask_q(h)
                for gr in range(1, NG + 1):
                    for h in range((gr + 2) * GH, min(H1, (gr + 3) * GH)):
                        mask_q(h)
                    for i in range(NT):
                        n = (gr - 1) * NT + i
                        pool.wait_ge(s["u_ready"], n + 1)
                        pool.tensor_tensor(E_(n), E_(n), W_(n), ALU.subtract).then_inc(s["p_ready"], 1)

            @block.vector
            def _(dve):
                step = Chain(dve, s["dve_step"])

                def gs(gr):
                    return slice(gr * NT, (gr + 1) * NT)

                def counted(gr, rnd):
                    return NT * (rnd if gr == 0 else COUNTS + (COUNTS - ACT_COUNTS) * (gr - 1) + rnd)

                def update(gr, k):
                    c = gs(gr)
                    if gr and k <= ACT_COUNTS:
                        dve.wait_ge(s["act_count%d" % (k - 1)], NT * gr)
                        step(dve.tensor_scalar(tc[:, 1, c], signs[:, c], -0.5, T / 2.0, ALU.mult, ALU.add))
                    else:
                        dve.wait_ge(s["dve_count"], counted(gr, k - (ACT_COUNTS if gr else 0)))
                    step(dve.tensor_scalar(up[:, c], tc[:, 1, c], AIM, None, ALU.is_ge))
                    step(dve.tensor_scalar(dn[:, c], tc[:, 1, c], AIM, None, ALU.is_lt))

                    def both(m):
                        return m[:, c].rearrange("p (a c) -> p a c", a=1).broadcast_to([P, 2, NT])
                    step(dve.copy_predicated(lo[:, :, c], both(up), tc[:, :, c]))
                    step(dve.copy_predicated(hi[:, :, c], both(dn), tc[:, :, c]))
                    step(dve.tensor_tensor(dif[:, :, c], lo[:, :, c], hi[:, :, c], ALU.subtract))
                    step(dve.reciprocal(rec[:, c], dif[:, 1, c]))
                    step(dve.scalar_tensor_tensor(rec[:, c], lo[:, 1, c], AIM, rec[:, c], ALU.subtract, ALU.mult))
                    step(dve.tensor_tensor(rec[:, c], rec[:, c], dif[:, 0, c], ALU.mult))
                    ins = dve.tensor_tensor(tc[:, 0, c], lo[:, 0, c], rec[:, c], ALU.subtract)
                    if gr and k < ACT_COUNTS:
                        ins.then_inc(s["t_ready%d" % k], 1)
                    else:
                        step(ins)

                def count(gr, rnd):
                    before = counted(gr, rnd)
                    for n in range(gr * NT, (gr + 1) * NT):
                        dve.wait_ge(s["s_ready"], n + 1)
                        if before + n % NT >= 2:
                            dve.wait_ge(s["dve_count"], before + n % NT - 1)
                        yield n, dve.tensor_scalar(above[:, n % 2, :], S_(n), tc[:, 0, n:n + 1], 0.0, ALU.is_gt, ALU.add,
                                                   accum_out=tc[:, 1, n:n + 1]).then_inc(s["dve_count"], 1)

                def take(gr):
                    c = gs(gr)
                    if gr >= 2:
                        dve.wait_ge(s["p_ready"], NT * (gr - 1))
                    last = COUNTS - 1 - (ACT_COUNTS if gr else 0)
                    for n, _ in count(gr, last):
                        i = n % NT
                        dve.wait_ge(s["dve_count"], counted(gr, last) + i + 1)
                        dve.scalar_tensor_tensor(W_(n), above[:, n % 2, :], TAKEN, S_(n), ALU.mult, ALU.add)\
                           .then_inc(s["rest_left"], 1)
                        if i:
                            dve.wait_ge(s["rest_left"], n)
                            dve.max(m8[:, i - 1, :], W_(n - 1)).then_inc(s["max8"], 1)
                    dve.wait_ge(s["rest_left"], (gr + 1) * NT)
                    dve.max(m8[:, NT - 1, :], W_(gr * NT + NT - 1)).then_inc(s["max8"], 1)
                    step(dve.tensor_scalar(rec[:, c], tc[:, 1, c], TOPK - 4.5, None, ALU.subtract))
                    step(dve.tensor_tensor(rec[:, c], rec[:, c], rec[:, c], ALU.mult))
                    dve.tensor_scalar(bad[:, gr % 2, :], rec[:, c], 16.0, None, ALU.is_gt).then_inc(s["bad_ready"], 1)
                    dve.wait_ge(s["bad_ready"], gr + 1)
                    step(dve.tensor_scalar(rec[:, c], tc[:, 1, c], -1.0, float(TOPK), ALU.mult, ALU.add))
                    step(dve.tensor_tensor(keep[:, :, :], rec[:, c].rearrange("p (c a) -> p c a", a=1).broadcast_to([P, NT, 8]),
                                           rank[:, :].rearrange("p (a r) -> p a r", a=1).broadcast_to([P, NT, 8]), ALU.is_gt))
                    dve.wait_ge(s["max8"], (gr + 1) * NT)
                    step(dve.tensor_tensor(m8[:, :, :], m8[:, :, :], keep[:, :, :], ALU.mult))
                    step(dve.tensor_scalar(keep[:, :, :], keep[:, :, :], 1.0, -TAKEN, ALU.subtract, ALU.mult))
                    step(dve.tensor_tensor(m8[:, :, :], m8[:, :, :], keep[:, :, :], ALU.add))
                    for i in range(NT):
                        n = gr * NT + i
                        dve.match_replace(W_(n), m8[:, i, :], W_(n), TAKEN).then_inc(s["matched"], 1)

                def check(gr):
                    dve.wait_ge(s["mm_bad"], gr + 1)
                    dve.wait_ge(s["matched"], (gr + 1) * NT)
                    src = PS[0:1, 6 + gr % 2, 128:128 + NT]
                    step(dve.tensor_copy(nbad[:, 0:NT], src))
                    step(dve.tensor_reduce(nbad_sum[:, :], src, AX, ALU.add))
                    step(dve.tensor_copy(nbad[:, NT:NT + 1], nbad_sum[:, :]))
                    with dve.If(dve.value_load(nbad[0:1, NT:NT + 1]) > 0):
                        for i in range(NT):
                            n = gr * NT + i
                            with dve.If(dve.value_load(nbad[0:1, i:i + 1]) > 0):
                                dve.tensor_copy(W_(n), S_(n)).then_inc(s["slow"], 1)
                                dve.wait_ge(s["slow"], 1)
                                dve.sem_clear(s["slow"])
                                with dve.Fori(0, TOPK // 8):
                                    dve.max(m8[:, 0, :], W_(n)).then_inc(s["slow"], 1)
                                    dve.wait_ge(s["slow"], 1)
                                    dve.match_replace(W_(n), m8[:, 0, :], W_(n), TAKEN).then_inc(s["slow"], 1)
                                    dve.wait_ge(s["slow"], 2)
                                    dve.sem_clear(s["slow"])
                    step(dve.tensor_copy(nbad[:, 0:1], nbad[:, 0:1]))
                    dve.sem_inc(s["w_ready"], 1)

                def out(gr):
                    dve.wait_ge(s["mm_pv"], (gr + 1) * NT)
                    pv = PS[:, 6 + gr % 2, 0:NT * (D1 + 1)].rearrange("p (h t c) -> p h t c", t=4, c=D1 + 1)
                    if gr:
                        dve.wait_ge(s["out_ready"], gr)
                    rp = prec[:, :].rearrange("p (h t c) -> p h t c", t=4, c=1)
                    step(dve.reciprocal(rp, pv[:, :, :, D1:]))
                    dve.tensor_tensor(OUT[:, :, gr * GH:(gr + 1) * GH, :].rearrange("p t h c -> p h t c"),
                                      pv[:, :, :, 0:D1], rp.broadcast_to([P, GH, 4, D1]), ALU.mult)\
                       .then_inc(s["out_ready"], 1)

                for rnd in range(ACT_COUNTS):
                    for _ in count(0, rnd):
                        pass
                    update(0, rnd + 1)
                for _ in count(0, 2):
                    pass
                update(0, 3)
                for gr in range(NG):
                    if gr + 1 < NG:
                        update(gr + 1, 1)
                    if gr:
                        for _ in count(gr, 0):
                            pass
                        check(gr - 1)
                        update(gr, 3)
                    for _ in count(gr, 1 if gr else 3):
                        pass
                    if gr + 1 < NG:
                        update(gr + 1, 2)
                    if gr >= 2:
                        out(gr - 2)
                    update(gr, 4)
                    take(gr)
                check(NG - 1)
                out(NG - 2)
                out(NG - 1)

        def finish(block, b, s):
            xb = X[:, ds(b, 1), :].rearrange("p a t -> p (a t)")

            @block.tensor
            def _(pe):
                for t in range(4):
                    mm = pe.transpose(PS[:, 0, t * P:(t + 1) * P], OUT[:, t, :, :].rearrange("p h c -> p (h c)"), ident[:, :])
                mm.then_inc(s["mm_oT"], 1)
                pe.wait_ge(s["oT_ready"], 1)
                pe.matmul(PS[:, 1, :], w["Wo"][:, :], OT[:, :], start=True, stop=True).then_inc(s["mm_o"], 1)

            @block.scalar
            def _(act):
                act.wait_ge(s["mm_oT"], 1)
                act.activation(OT[:, :], PS[:, 0, :], ACT.Copy).then_inc(s["oT_ready"], 1)

            @block.vector
            def _(dve):
                step = Chain(dve, s["dve_step"])
                dve.wait_ge(s["mm_o"], 1)
                step(dve.scalar_tensor_tensor(xc[:, :], PS[:, 1, :], col["bo"][:, 0:1], hn[:, :], ALU.add, ALU.subtract))
                step(dve.tensor_tensor(xc[:, :], xc[:, :], gate[:, :], ALU.mult))
                step(dve.tensor_tensor(xc[:, :], xc[:, :], hn[:, :], ALU.add))
                step(dve.scalar_tensor_tensor(xb, xc[:, :], mod[:, 2:3], xb, ALU.mult, ALU.add))

        with nc.Fori(0, NB) as b:
            nested(nc, LN_SEMS + "mm_proj mm_v mm_ss mm_temp mean_ready qk_ready qk_sq gate_ready temp_sig norm_ready "
                   "qk_norm mm_kT kT_ready mm_C C_ready mm_CQ qcq_ready mm_mom var_ready sd_ready dve_step", b, project)
            nested(nc, "q_ready mm_score s_ready exp_ready act_count0 act_count1 t_ready1 dve_count rest_left max8 matched "
                   "bad_ready mm_bad slow w_ready u_ready p_ready mm_pT pT_ready mm_pv out_ready dve_step", b, search)
            nested(nc, "mm_oT oT_ready mm_o dve_step", b, finish)


DEPTH = 6
H2, D2 = 16, 64
WIN = 32
INNER = H2 * D2
NPAIR = H2 // 2
F_IN = P * 4 * 2 // 3
FC = -(-F_IN // P)
QK_SCALE = 8.0
V_BANK = (0, 0, 6, 4)
S_BANK = (0, 0, 6, 0)


def tower_stage(nc, dram, g, PS):
    X, XF, MOD, eps, mean_w, ident = g.X, g.XF, g.MOD1, g.eps, g.mean_w, g.ident
    with ExitStack() as ctx:
        def sb(n, shape):
            return ctx.enter_context(nc.sbuf_tensor("tower_" + n, shape, F32))
        wqkv, wrot = sb("wqkv", [P, 3 * INNER]), sb("wrot", [P, 2 * INNER])
        wo, w1, w2 = sb("wo", [P, NPAIR, P]), sb("w1", [P, 2 * FC, P]), sb("w2", [P, FC, P])
        b1, cols = sb("b1", [P, DEPTH, 2 * FC]), sb("cols", [P, DEPTH, 7])
        lb1, lcol = sb("lb1", [P, 2 * FC]), sb("lcol", [P, 7])
        tab = sb("tab", [P, 4, T])
        sel2, hsel = sb("sel2", [P, 2]), sb("hsel", [H2, NPAIR, P])
        bias = sb("bias", [P, 2, 2 * WIN])
        xs, xm, xc, sq, rstd = (sb(n, [P, T]) for n in ("xs", "xm", "xc", "sq", "rstd"))
        V = sb("V", [P, 4, INNER])
        QT, KT = sb("QT", [P, NPAIR, T]), sb("KT", [P, NPAIR, WIN + T])
        qc, qsq, t1, t2 = (sb(n, [P, 2, T]) for n in ("qc", "qsq", "t1", "t2"))
        rn, rkT = sb("rn", [P, 4, 2, H2]), sb("rkT", [H2, T])
        SC = sb("SC", [P, 2, INNER])
        PB = sb("PB", [P, 2, H2, WIN + P])
        OT = sb("OT", [P, NPAIR, T])
        mx, ssum, rsum = sb("mx", [P, 2, H2]), sb("ssum", [P, 2, H2]), sb("rsum", [P, 2, H2])
        mod = sb("mod", [P, 6])
        hg = [sb("hg%d" % j, [P, T])[:, :] for j in range(FC - 2)] + [SC[:, 0, 0:T], SC[:, 0, T:2 * T]]

        def setup(block, i, s):
            loads = [(b1[:, :, :], dram["f_b1"]), (cols[:, :, :], dram["f_cols"]), (sel2[:, :], dram["sel2"]),
                     (hsel[:, :, :], dram["hsel"]), (bias[:, :, :], dram["winmask"])]

            @block.sync
            def _(sp):
                for tile, src in loads:
                    sp.dma_start(tile, src).then_inc(s["w_in"], 16)
                sp.wait_ge(s["w_in"], 16 * len(loads))

            @block.gpsimd
            def _(pool):
                zero = (xs[64:128, 0:1], xm[64:128, 0:1], PB[:, :, :, :], KT[:, :, 0:WIN])
                for n, tile in enumerate(zero):
                    pool.memset(tile, 0.0).then_inc(s["pool_done"], 1)
                    pool.wait_ge(s["pool_done"], n + 1)
        stage(nc, "w_in pool_done", 1, setup)

        def enter(block, b, s):
            xb = X[:, ds(b, 1), :].rearrange("p a t -> p (a t)")
            xf = XF[:, ds(b, 1), :].rearrange("p a t -> p (a t)")

            @block.tensor
            def _(pe):
                ln_tensor(pe, s, xb, mean_w[:, :], sq[:, :], PS[:, 0, :], PS[:, 1, :])

            @block.scalar
            def _(act):
                ln_scalar(act, s, xc[:, :], sq[:, :], PS[:, 1, :], rstd[:, :], eps[:, 0:1])

            @block.vector
            def _(dve):
                step = Chain(dve, s["dve_step"])
                step(dve.tensor_copy(mod[:, :], MOD[:, ds(b, 1), :].rearrange("p a j -> p (a j)")))
                ln_vector(dve, s, xb, xc[:, :], PS[:, 0, :], rstd[:, :], mod[:, 4:5], mod[:, 3:4], xf)
        stage(nc, LN_SEMS + "dve_step", NB, enter)

        def load_layer(block, l, s):
            @block.sync
            def _(sp):
                def from_layer(name, tile):
                    src = dram[name][ds(l, 1)]
                    sp.dma_start(tile, src.rearrange("a p c -> p (a c)")).then_inc(s["layer_in"], 16)
                from_layer("f_Wqkv", wqkv[:, :])
                src = dram["f_Wqkv"][ds(l, 1), :, 0:2 * INNER].rearrange("a p (g z c) -> p (a g) z c", z=2, c=D2 // 2)
                dst = wrot[:, :].rearrange("p (g z c) -> p g z c", z=2, c=D2 // 2)
                for z in range(2):
                    sp.dma_start(dst[:, :, z, :], src[:, :, 1 - z, :]).then_inc(s["layer_in"], 16)
                from_layer("f_Wo", wo[:, :, :].rearrange("p a c -> p (a c)"))
                from_layer("f_W1", w1[:, :, :].rearrange("p a c -> p (a c)"))
                from_layer("f_W2", w2[:, :, :].rearrange("p a c -> p (a c)"))
                sp.dma_start(tab[:, :, :], dram["rotary"]).then_inc(s["tab_in"], 16)
                sp.wait_ge(s["layer_in"], 16 * 6)

            @block.vector
            def _(dve):
                dve.tensor_copy(lb1[:, :], b1[:, ds(l, 1), :].rearrange("p a j -> p (a j)")).then_inc(s["col_ready"], 1)
                dve.tensor_copy(lcol[:, :], cols[:, ds(l, 1), :].rearrange("p a j -> p (a j)")).then_inc(s["col_ready"], 1)
                dve.wait_ge(s["col_ready"], 2)
                dve.wait_ge(s["tab_in"], 16)
                for j in range(4):
                    dve.tensor_scalar(tab[:, j, :], tab[:, j, :], lcol[:, 3 + j:4 + j], None, ALU.mult)\
                       .then_inc(s["col_ready"], 1)

        def layer(block, s, xf, mlp_xf):
            if xf is not None:
                xf_lo, xf_hi = xf[0:64, :], xf[64:128, 0:T - 1]

            def mlp_mean(pe):
                pe.matmul(PS[:, 7, :], mean_w[:, :], xm[:, :], start=True, stop=True).then_inc(s["ln_mean"], 1)

            def mlp_var(pe):
                pe.wait_ge(s["ln_sq"], 1)
                pe.matmul(PS[:, 7, :], mean_w[:, :], sq[:, :], start=True, stop=True).then_inc(s["ln_var"], 1)

            def mlp_in(pe, j):
                pe.wait_ge(s["ln_out"], 1)
                if j:
                    pe.wait_ge(s["gelu_ready"], j)
                pe.matmul(PS[:, 0, :], w1[:, FC + j, :], xc[:, :], start=True, stop=True).then_inc(s["mm_gate"], 1)
                if j:
                    pe.wait_ge(s["h_ready"], j)
                pe.matmul(PS[:, 1, :], w1[:, j, :], xc[:, :], start=True, stop=True).then_inc(s["mm_val"], 1)

            def mlp_out(pe, j):
                pe.wait_ge(s["h_ready"], j + 1)
                mm = pe.matmul(PS[:, 7, :], w2[:, j, :], hg[j], start=(j == 0), stop=(j == FC - 1))
                if j == FC - 1:
                    mm.then_inc(s["mm_mlp"], 1)

            @block.tensor
            def _(pe):
                if xf is None:
                    mlp_mean(pe)
                    mlp_var(pe)
                    for j in range(FC):
                        mlp_in(pe, j)
                        mlp_out(pe, j)
                    return
                if mlp_xf is not None:
                    mlp_mean(pe)
                pe.wait_ge(s["xs_ready"], 2)

                def v_half(n):
                    if n in (2, 3):
                        pe.wait_ge(s["v_ready"], n - 1)
                    t, c = n // 2, 2 * INNER + n % 2 * 512
                    pe.matmul(PS[:, V_BANK[n // 2] + n % 2, :], xs[:, t * P:(t + 1) * P], wqkv[:, c:c + 512],
                              start=True, stop=True).then_inc(s["mm_v"], 1)

                for p in range(NPAIR):
                    for j in range(2):
                        c = slice(j * INNER + p * P, j * INNER + (p + 1) * P)
                        if p:
                            pe.wait_ge(s["qc_ready"], 2 * (p - 1) + j + 1)
                        pe.matmul(PS[:, 2 + j, :], wqkv[:, c], xs[:, :], start=True, stop=True).then_inc(s["mm_q"], 1)
                        if p:
                            pe.wait_ge(s["t2_ready"], 2 * (p - 1) + j + 1)
                        pe.matmul(PS[:, 4 + j, :], wrot[:, c], xs[:, :], start=True, stop=True).then_inc(s["mm_qr"], 1)
                    if p:
                        norms_of(pe, s, p - 1)
                    if mlp_xf is not None:
                        if p == 0:
                            mlp_var(pe)
                        if 2 <= p <= FC + 1:
                            mlp_in(pe, p - 2)
                        if 4 <= p <= FC + 3:
                            mlp_out(pe, p - 4)
                norms_of(pe, s, NPAIR - 1)
                v_half(0)
                v_half(1)
                pe.wait_ge(s["rn_ready"], 1)
                if mlp_xf is not None:
                    pe.wait_ge(s["x_out"], 1)
                for t in range(4):
                    mm = pe.transpose(PS[0:H2, 7, t * P:(t + 1) * P], rn[:, t, 1, :], ident[:, :])
                mm.then_inc(s["mm_rkT"], 1)
                v_half(2)
                v_half(3)
                pe.wait_ge(s["rkT_ready"], 1)
                for p in range(NPAIR):
                    if p >= 2:
                        pe.wait_ge(s["kt_ready"], p - 1)
                    pe.matmul(PS[:, 2 + p % 2, :], hsel[:, p, :], rkT[:, :], start=True, stop=True).then_inc(s["mm_rk"], 1)
                pe.wait_ge(s["kt_ready"], NPAIR)
                pe.wait_ge(s["qt_ready"], 2 * NPAIR)

                def scores(t):
                    if t % 2:
                        pe.wait_ge(s["sc_scaled"], 2 if t == 1 else 4)
                    else:
                        pe.wait_ge(s["v_ready"], 6 if t else 4)
                    for g, w in [(g, w) for g in range(NPAIR) for w in range(4)]:
                        for h in (2 * g, 2 * g + 1):
                            r = slice(64 * (h % 2), 64 * (h % 2) + 64)
                            c0 = t * P + w * WIN
                            mm = pe.matmul(PS[32 * w:32 * w + 32, S_BANK[t] + h % 2, (h // 2) * 64:(h // 2) * 64 + 64],
                                           QT[r, h // 2, c0:c0 + WIN], KT[r, h // 2, c0:c0 + 2 * WIN],
                                           start=True, stop=True, tile_position=(64 * (h % 2), 32 * w))
                    mm.then_inc(s["mm_sc"], 1)

                def values(t):
                    pe.wait_ge(s["pt_ready"], 8 * (t + 1))
                    pe.wait_ge(s["v_ready"], 2 if t == 0 else 8)
                    if t >= 2:
                        pe.wait_ge(s["ot_ready"], 2 * (t - 1))
                    for h in range(H2):
                        x, hc = (h % 2) * 8 + h // 2, slice(h * D2, (h + 1) * D2)
                        out = PS[64 * (h % 2):64 * (h % 2) + 64, 2 + 2 * (t % 2) + h // 8, (h // 2 % 4) * P:(h // 2 % 4 + 1) * P]
                        mm = pe.matmul(out, V[:, t, hc], PB[:, t % 2, x, WIN:], start=True, stop=(t == 0),
                                       tile_position=(0, 64 * (h % 2)))
                        if t:
                            mm = pe.matmul(out, V[P - WIN:P, t - 1, hc], PB[P - WIN:P, t % 2, x, 0:P],
                                           start=False, stop=True, tile_position=(P - WIN, 64 * (h % 2)))
                        if h % 8 == 7:
                            mm.then_inc(s["mm_pv"], 1)

                scores(0)
                for n in range(4, 8):
                    v_half(n)
                scores(1)
                scores(2)
                values(0)
                scores(3)
                for t in range(1, 4):
                    values(t)
                pe.wait_ge(s["ot_ready"], 8)
                for p in range(NPAIR):
                    mm = pe.matmul(PS[:, 6, :], wo[:, p, :], OT[:, p, :], start=(p == 0), stop=(p == NPAIR - 1))
                mm.then_inc(s["mm_o"], 1)

            def mlp_rstd(act):
                act.wait_ge(s["ln_var"], 1)
                act.activation(rstd[:, :], PS[:, 7, :], ACT.Ln, bias=eps[:, 0:1]).then_inc(s["ln_log"], 1)
                act.wait_ge(s["ln_log"], 1)
                act.activation(rstd[:, :], rstd[:, :], ACT.Exp, scale=-0.5).then_inc(s["ln_rstd"], 1)

            def mlp_square(act):
                act.wait_ge(s["ln_xc"], 1)
                act.activation(sq[:, :], xc[:, :], ACT.Square).then_inc(s["ln_sq"], 1)

            def mlp_gelu(act, j):
                act.wait_ge(s["mm_gate"], j + 1)
                act.activation(hg[j], PS[:, 0, :], ACT.Gelu, bias=lb1[:, FC + j:FC + j + 1])\
                   .then_inc(s["gelu_ready"], 1)

            @block.scalar
            def _(act):
                if xf is None:
                    mlp_square(act)
                    mlp_rstd(act)
                    for j in range(FC):
                        mlp_gelu(act, j)
                    return
                def v_copy(n):
                    act.wait_ge(s["mm_v"], n + 1)
                    act.activation(V[:, n // 2, (n % 2) * 512:(n % 2 + 1) * 512], PS[:, V_BANK[n // 2] + n % 2, :],
                                   ACT.Copy).then_inc(s["v_ready"], 1)

                if mlp_xf is not None:
                    mlp_square(act)
                for p in range(NPAIR):
                    for j in range(2):
                        n = 2 * p + j
                        act.wait_ge(s["mm_q"], n + 1)
                        if p:
                            act.wait_ge(s["t1_ready"], n - 1)
                        act.activation(qc[:, j, :], PS[:, 2 + j, :], ACT.Copy).then_inc(s["qc_ready"], 1)
                        act.wait_ge(s["qc_ready"], n + 1)
                        if p:
                            act.wait_ge(s["mm_ss"], n - 1)
                        act.activation(qsq[:, j, :], qc[:, j, :], ACT.Square).then_inc(s["qsq_ready"], 1)
                    if mlp_xf is not None and p == 0:
                        mlp_rstd(act)
                    if mlp_xf is not None and 2 <= p <= FC + 1:
                        mlp_gelu(act, p - 2)
                act.wait_ge(s["mm_ss"], 2 * NPAIR)
                act.activation(rn[:, :, :, :].rearrange("p t z h -> p (t z h)"), PS[:, 6, 0:128], ACT.Sqrt)\
                   .then_inc(s["norm_ready"], 1)
                v_copy(0)
                v_copy(1)
                act.wait_ge(s["mm_rkT"], 1)
                act.activation(rkT[:, :], PS[0:H2, 7, :], ACT.Copy).then_inc(s["rkT_ready"], 1)
                v_copy(2)
                v_copy(3)

                def turned(t):
                    for j in range(2):
                        act.wait_ge(s["mm_pv"], 2 * t + j + 1)
                        act.activation(OT[:, 4 * j:4 * j + 4, t * P:(t + 1) * P],
                                       PS[:, 2 + 2 * (t % 2) + j, :].rearrange("p (a c) -> p a c", a=4), ACT.Copy)\
                           .then_inc(s["ot_ready"], 1)
                def exp(t):
                    act.wait_ge(s["sc_ready"], t + 1)
                    act.activation(SC[:, t % 2, :], SC[:, t % 2, :], ACT.Exp).then_inc(s["exp_ready"], 1)
                for n in range(4, 8):
                    v_copy(n)
                exp(0)
                exp(1)
                exp(2)
                turned(0)
                exp(3)
                turned(1)
                turned(2)
                turned(3)

            def heads(a):
                return a.rearrange("p (g k) -> p g k", k=2 * WIN)

            def spread(a):
                return a.rearrange("p (g k) -> p g k", k=1)

            @block.gpsimd
            def _(pool):
                if xf is None:
                    return
                for p in range(NPAIR):
                    for j in range(2):
                        n = 2 * p + j
                        pool.wait_ge(s["t1_ready"], n + 1)
                        pool.wait_ge(s["t2_ready"], n + 1)
                        dst = QT[:, p, :] if j == 0 else KT[:, p, WIN:]
                        pool.tensor_tensor(dst, t1[:, j, :], t2[:, j, :], ALU.add).then_inc(s["qt_ready"], 1)

                def less_max(t):
                    pool.wait_ge(s["mx_ready"], t + 1)
                    sc = heads(SC[:, t % 2, :])
                    pool.tensor_tensor(sc, sc, spread(mx[:, t % 2, :]).broadcast_to([P, H2, 2 * WIN]), ALU.subtract)\
                        .then_inc(s["sc_ready"], 1)

                def over_sum(t):
                    pool.wait_ge(s["sum_ready"], t + 1)
                    sc = heads(SC[:, t % 2, :])
                    pool.tensor_tensor(sc, sc, spread(rsum[:, t % 2, :]).broadcast_to([P, H2, 2 * WIN]), ALU.mult)\
                        .then_inc(s["prob_ready"], 1)
                less_max(0)
                over_sum(0)
                less_max(1)
                less_max(2)
                over_sum(1)
                over_sum(2)
                less_max(3)
                over_sum(3)

            def mlp_center(dve):
                dve.wait_ge(s["ln_mean"], 1)
                dve.tensor_tensor(xc[:, :], xm[:, :], PS[:, 7, :], ALU.subtract).then_inc(s["ln_xc"], 1)

            def mlp_norm(dve):
                dve.wait_ge(s["ln_rstd"], 1)
                dve.wait_ge(s["ln_xc"], 1)
                dve.tensor_tensor(xc[:, :], xc[:, :], rstd[:, :], ALU.mult).then_inc(s["ln_norm"], 1)
                dve.wait_ge(s["ln_norm"], 1)
                dve.tensor_scalar(xc[:, :], xc[:, :], lcol[:, 0:1], lcol[:, 1:2], ALU.mult, ALU.add).then_inc(s["ln_out"], 1)

            def mlp_product(dve, j):
                dve.wait_ge(s["gelu_ready"], j + 1)
                dve.wait_ge(s["mm_val"], j + 1)
                dve.scalar_tensor_tensor(hg[j], PS[:, 1, :], lb1[:, j:j + 1], hg[j], ALU.add, ALU.mult)\
                   .then_inc(s["h_ready"], 1)

            def mlp_add(dve):
                dve.wait_ge(s["mm_mlp"], 1)
                dve.scalar_tensor_tensor(mlp_xf, PS[:, 7, :], lcol[:, 2:3], mlp_xf, ALU.add, ALU.add).then_inc(s["x_out"], 1)

            @block.vector
            def _(dve):
                step = Chain(dve, s["dve_step"])
                if xf is None:
                    mlp_center(dve)
                    mlp_norm(dve)
                    for j in range(FC):
                        mlp_product(dve, j)
                    mlp_add(dve)
                    return
                dve.tensor_copy(xs[0:64, :], xf_lo).then_inc(s["xs_ready"], 1)
                dve.tensor_copy(xs[64:128, 1:T], xf_hi).then_inc(s["xs_ready"], 1)
                if mlp_xf is not None:
                    mlp_center(dve)
                for p in range(NPAIR):
                    for j in range(2):
                        n = 2 * p + j
                        dve.wait_ge(s["qc_ready"], n + 1)
                        if p:
                            dve.wait_ge(s["qt_ready"], n - 1)
                        dve.tensor_tensor(t1[:, j, :], qc[:, j, :], tab[:, 2 * j, :], ALU.mult).then_inc(s["t1_ready"], 1)
                        dve.wait_ge(s["mm_qr"], n + 1)
                        dve.tensor_tensor(t2[:, j, :], PS[:, 4 + j, :], tab[:, 2 * j + 1, :], ALU.mult)\
                           .then_inc(s["t2_ready"], 1)
                    if mlp_xf is not None:
                        if p == 1:
                            mlp_norm(dve)
                        elif 2 <= p <= FC + 1:
                            mlp_product(dve, p - 2)
                        elif p == FC + 3:
                            mlp_add(dve)
                dve.wait_ge(s["norm_ready"], 1)
                flat_rn = rn[:, :, :, :].rearrange("p t z h -> p (t z h)")
                step(dve.tensor_scalar(flat_rn, flat_rn, 1e-12, None, ALU.max))
                dve.reciprocal(flat_rn, flat_rn).then_inc(s["rn_ready"], 1)
                for p in range(NPAIR):
                    dve.wait_ge(s["mm_rk"], p + 1)
                    dve.wait_ge(s["qt_ready"], 2 * p + 2)
                    dve.tensor_tensor(KT[:, p, WIN:], KT[:, p, WIN:], PS[:, 2 + p % 2, :], ALU.mult).then_inc(s["kt_ready"], 1)

                def front(t):
                    dve.wait_ge(s["mm_sc"], t + 1)
                    if t >= 2:
                        dve.wait_ge(s["pt_ready"], 8 * (t - 1))
                    for j in range(2):
                        dve.tensor_tensor(heads(SC[:, t % 2, 512 * j:512 * j + 512]), heads(PS[:, S_BANK[t] + j, :]),
                                          spread(rn[:, t, 0, 8 * j:8 * j + 8]).broadcast_to([P, 8, 2 * WIN]),
                                          ALU.mult).then_inc(s["sc_scaled"], 1)
                    dve.wait_ge(s["sc_scaled"], 2 * t + 2)
                    sc = heads(SC[:, t % 2, :])
                    mk = bias[:, min(t, 1):min(t, 1) + 1, :].broadcast_to([P, H2, 2 * WIN])
                    step(dve.scalar_tensor_tensor(sc, sc, QK_SCALE, mk, ALU.mult, ALU.add))
                    dve.tensor_reduce(mx[:, t % 2, :], sc, AX, ALU.max).then_inc(s["mx_ready"], 1)

                def sums(t):
                    dve.wait_ge(s["exp_ready"], t + 1)
                    step(dve.tensor_reduce(ssum[:, t % 2, :], heads(SC[:, t % 2, :]), AX, ALU.add))
                    dve.reciprocal(rsum[:, t % 2, :], ssum[:, t % 2, :]).then_inc(s["sum_ready"], 1)

                def turned(t):
                    dve.wait_ge(s["prob_ready"], t + 1)
                    if t >= 2:
                        dve.wait_ge(s["mm_pv"], 2 * (t - 1))
                    for w in range(4):
                        rows, cols_w = slice(WIN * w, WIN * w + WIN), slice(WIN * w + WIN, WIN * w + 2 * WIN)
                        sc = SC[rows, t % 2, :].rearrange("p (x k) -> p x k", k=2 * WIN)
                        dve.transpose(PB[rows, t % 2, :, cols_w], sc[:, :, WIN:]).then_inc(s["pt_ready"], 1)
                        before = slice((WIN * w - WIN) % P, (WIN * w - WIN) % P + WIN)
                        dst = PB[before, t % 2, :, cols_w if w else slice(0, WIN)]
                        dve.transpose(dst, sc[:, :, 0:WIN]).then_inc(s["pt_ready"], 1)
                front(0)
                sums(0)
                front(1)
                turned(0)
                front(2)
                sums(1)
                turned(1)
                sums(2)
                front(3)
                turned(2)
                sums(3)
                turned(3)
                dve.wait_ge(s["mm_o"], 1)
                dve.tensor_tensor(xf, xf, PS[:, 6, :], ALU.add).then_inc(s["x_mid"], 1)
                dve.wait_ge(s["x_mid"], 1)
                dve.tensor_copy(xm[0:64, :], xf_lo).then_inc(s["xm_ready"], 1)
                dve.tensor_copy(xm[64:128, 1:T], xf_hi).then_inc(s["xm_ready"], 1)

        def norms_of(pe, s, p):
            cols6 = PS[:, 6, 0:128].rearrange("p (t z y g) -> p t z y g", t=4, z=2, y=2)
            for j in range(2):
                pe.wait_ge(s["qsq_ready"], 2 * p + j + 1)
                for t in range(4):
                    mm = pe.matmul(cols6[:, t, j, :, p], qsq[:, j, t * P:(t + 1) * P], sel2[:, :], start=True, stop=True)
                mm.then_inc(s["mm_ss"], 1)

        names = LN_SEMS + ("xs_ready mm_v v_ready mm_q mm_qr qc_ready qsq_ready mm_ss t1_ready t2_ready qt_ready "
                           "norm_ready rn_ready mm_rkT rkT_ready mm_rk kt_ready mm_sc sc_scaled mx_ready sc_ready exp_ready sum_ready prob_ready "
                           "pt_ready mm_pv ot_ready mm_o x_mid mm_gate mm_val gelu_ready h_ready "
                           "mm_mlp xm_ready x_out dve_step")
        later = XF[:, 1:, :]

        def first(block, b, s):
            layer(block, s, XF[:, 0, :], None)

        def middle(block, b, s):
            layer(block, s, later[:, ds(b, 1), :].rearrange("p a t -> p (a t)"),
                  XF[:, ds(b, 1), :].rearrange("p a t -> p (a t)"))

        def last(block, b, s):
            layer(block, s, None, XF[:, NB - 1, :])

        with nc.Fori(0, DEPTH) as l:
            nested(nc, "layer_in tab_in col_ready", l, load_layer)
            stage(nc, names, 1, first)
            stage(nc, names, NB - 1, middle)
            stage(nc, names, 1, last)

        def leave(block, b, s):
            xb = X[:, ds(b, 1), :].rearrange("p a t -> p (a t)")
            xf = XF[:, ds(b, 1), :].rearrange("p a t -> p (a t)")

            @block.vector
            def _(dve):
                step = Chain(dve, s["dve_step"])
                step(dve.tensor_copy(mod[:, :], MOD[:, ds(b, 1), :].rearrange("p a j -> p (a j)")))
                step(dve.scalar_tensor_tensor(xb, xf, mod[:, 5:6], xb, ALU.mult, ALU.add))
        stage(nc, "dve_step", NB, leave)


class Globals:
    pass


def build(nc, dram, out):
    with ExitStack() as ctx:
        def sb(n, shape):
            return ctx.enter_context(nc.sbuf_tensor(n, shape, F32))
        g = Globals()
        g.X = sb("X", [P, NB, T])
        g.MOD0, g.MOD1 = sb("MOD0", [P, NB, 6]), sb("MOD1", [P, NB, 6])
        g.eps = sb("eps", [P, 4])
        g.mean_w, g.ident = sb("mean_w", [P, P]), sb("ident", [P, P])
        PS = ctx.enter_context(nc.psum_tensor("PS", [P, 8, 512], F32))
        consts = [(g.X[:, :, :], dram["x"]), (g.eps[:, :], dram["eps"]), (g.mean_w[:, :], dram["mean_w"]),
                  (g.ident[:, :], dram["ident"])]
        modulation_stage(nc, dram, consts, PS, (g.MOD0, g.MOD1))
        delta_attention_stage(nc, dram, g, PS)
        experts_stage(nc, dram, g, PS)
        topk_attention_stage(nc, dram, g, PS)
        g.XF = sb("XF", [P, NB, T])
        tower_stage(nc, dram, g, PS)

        def store(block, i, s):
            @block.sync
            def _(sp):
                sp.dma_start(out, g.X[:, :, :]).then_inc(s["out_done"], 16)
                sp.wait_ge(s["out_done"], 16)
        stage(nc, "out_done", 1, store)


def shape_constants(np):
    f = np.float32
    c = {"ident": np.eye(P, dtype=f), "mean_w": np.full((P, P), 1.0 / P, f)}
    c["eps"] = np.tile(np.array([LN_EPS, 1e-6, 0, 0], f), (P, 1))
    i = np.arange(P)
    c["blk32"] = (i[:, None] // D0 == i[None, :] // D0).astype(f)
    r, q = np.arange(CH)[:, None], np.arange(CH)[None, :]
    m = [q < r, r <= q, r == q, (r // 2 == q // 2) & (r % 2 == 1) & (q % 2 == 0)]
    for z in (2, 4, 8, 16):
        m.append((r // (2 * z) == q // (2 * z)) & (q // z % 2 == 1) & (r // z % 2 == 0))
    c["masks"] = np.tile(np.stack(m, 1), (H0, 1, 1)).astype(f)
    sel = np.zeros((P, 4, 3, P), f)
    for h in range(H0):
        ch = slice(32 * h, 32 * h + 32)
        for k in range(4):
            row = 32 * h + 4 * k
            sel[ch, k, 0, row] = sel[ch, k, 0, row + 1] = 1.0 / D0
            sel[ch, k, 1, row + 2] = 1.0 / D0
            sel[ch, k, 2, row + 1] = 1.0 / D0
            sel[ch, k, 2, row + 3] = 1.0
    c["sel"] = sel
    used = i % 32 < 16
    c["stm"] = np.stack([used & (i % 2 == 0), used & (i % 4 == 1), used & (i % 4 == 3)], 1).astype(f)
    ps = np.zeros((16, 4, P), f)
    for h in range(H0):
        for k in range(4):
            ps[4 * h + k, k, 32 * h:32 * h + 32] = 1
    c["psel"] = ps
    c["sel2"] = (i[:, None] // D2 == np.arange(2)[None, :]).astype(f)
    hs = np.zeros((H2, NPAIR, P), f)
    for par in range(2):
        for p in range(NPAIR):
            hs[par * NPAIR + p, p, 64 * par:64 * par + 64] = 1
    c["hsel"] = hs
    q, j = i % WIN, np.arange(2 * WIN)
    ok = (q[:, None] <= j[None, :]) & (j[None, :] <= q[:, None] + WIN)
    first = ok & ((i[:, None] >= WIN) | (j[None, :] >= WIN))
    c["winmask"] = np.where(np.stack([first, ok], 1), 0, -1e30).astype(f)
    half = np.arange(0, D2, 2, dtype=f)
    tt = np.arange(T, dtype=f)
    ang = tt[:, None] * (f(1.0) / f(10000.0) ** (half / f(D2)))[None, :]
    scl = ((half + f(0.4 * D2)) / f(1.4 * D2))[None, :] ** ((tt - T // 2) / f(WIN // 2))[:, None]
    ang, scl = (np.concatenate([z, z], -1) for z in (ang, scl))
    sgn = np.where(np.arange(D2) < D2 // 2, -1, 1).astype(f)
    tabs = [np.cos(ang) * scl, np.sin(ang) * sgn * scl, np.cos(ang) / scl, np.sin(ang) * sgn / scl]
    c["rotary"] = np.tile(np.stack([z.T for z in tabs], 1), (2, 1, 1)).astype(f)
    e = np.arange(8)
    c["tri8"] = np.tile((e[None, :] < e[:, None]).astype(f), (P, 1, 1))
    c["esel"] = np.tile(np.eye(8, dtype=f)[:, :, None], (1, 1, P))
    c["t_blk8"] = (i[:, None] // D1 == i[None, :] // D1).astype(f)
    c["rank"] = np.tile(np.arange(8, dtype=f), (P, 1))
    c["hm"] = (i[:, None] // D1 == np.arange(H1)[None, :]).astype(f)
    return c


def kernel(**inputs):
    import numpy as np
    import concourse.bacc as bacc
    from concourse.bass_utils import run_bass_kernel_spmd as run

    def col(a, rep=1):
        return np.repeat(a.reshape(-1), rep).reshape(-1, 1)

    a = {n[8:]: v for n, v in inputs.items() if n.startswith("L0_attn_")}
    h = shape_constants(np)
    h["x"] = a["hidden_states"].transpose(2, 0, 1)
    for l in range(2):
        h[f"cT{l}"], h[f"wmod{l}"] = inputs[f"L{l}_c"].T, inputs[f"L{l}_wmod"]
    h["qwT"], h["kwT"], h["vwT"], h["owT"] = a["q_w"].T, a["k_w"].T, a["v_w"].T, a["o_w"].T
    h["bwT"] = np.repeat(a["b_w"].T, D0, axis=1)
    h["cw"] = np.stack([a["q_cw"], a["k_cw"], a["v_cw"]], 1)
    h["firs"], h["firl"] = a["fir_short_w"].reshape(P, FIR_S), a["fir_long_w"].reshape(P, FIR_L)
    h["mlp1h"] = a["mlp1_w"].T[:P]
    h["mlp1s"] = np.tile(np.concatenate([a["mlp1_w"].T[P:], np.zeros((16, P), np.float32)]), (4, 1))
    h["mlp1b"], h["mlp2T"] = col(a["mlp1_b"]), a["mlp2_w"].T
    h["mlp2b"] = np.tile(a["mlp2_b"], (P, 1))
    h["ltemp"], h["cres"] = col(a["logit_temp"], P), col(a["conv_res_logit"], D0)
    h["normw"] = np.tile(a["norm_w"], H0).reshape(P, 1)
    m = {n[7:]: v for n, v in inputs.items() if n.startswith("L0_ffn_")}
    h["w1"] = np.concatenate([m["w1"], m["cfc"][None]]).transpose(2, 0, 1)
    h["w2"] = np.concatenate([m["w2"], m["cproj"][None]]).transpose(2, 0, 1)
    h["gate_wT"], h["lb_bias"] = m["gate_w"].T, np.tile(m["lb_bias"], (P, 1))
    t = {n[8:]: v for n, v in inputs.items() if n.startswith("L1_attn_")}
    for n in ("Wq", "Wk", "Wv", "Wo", "Wg", "Wt"):
        h["t_" + n] = t[n]
    for n in ("bq", "bk", "bo", "bg"):
        h["t_" + n] = col(t[n])
    h["t_bt"], h["t_bv"] = col(t["bt"], P), np.tile(t["bv"], (P, 1))
    u = {n[7:]: v for n, v in inputs.items() if n.startswith("L1_ffn_")}
    h["f_Wqkv"] = u["Wqkv"]
    h["f_Wo"] = u["Wo"].reshape(DEPTH, NPAIR, P, P).transpose(0, 2, 1, 3).reshape(DEPTH, P, NPAIR * P)

    def chunked(v, axis):
        fill = [(0, 0)] * v.ndim
        fill[axis] = (0, FC * P - F_IN)
        return np.pad(v, fill)
    h["f_W1"] = np.concatenate([chunked(z, 2) for z in np.split(u["W1"], 2, 2)], 2)
    h["f_W2"] = chunked(u["W2"], 1).reshape(DEPTH, FC, P, P).transpose(0, 2, 1, 3).reshape(DEPTH, P, FC * P)
    h["f_b1"] = np.concatenate([chunked(z, 1) for z in np.split(u["b1"], 2, 1)], 1)\
        .reshape(DEPTH, 2 * FC, P).transpose(2, 0, 1)
    qs, ks = u["q_scale"], u["k_scale"]
    swap = (np.arange(D2) + D2 // 2) % D2
    h["f_cols"] = np.stack([u["ln_g"], u["ln_b"], u["b2"]] + [np.tile(z, (1, 2)) for z in
                           (qs, qs[:, swap], ks, ks[:, swap])], 1).transpose(2, 0, 1)

    nc = bacc.Bacc("TRN2", target_bir_lowering=False, num_devices=1)
    arrays, dram = {}, {}
    for n, v in h.items():
        arrays["in_" + n] = np.ascontiguousarray(v)
        dram[n] = nc.dram_tensor("in_" + n, v.shape, F32, kind="ExternalInput").ap()
    out = nc.dram_tensor("out", (P, NB, T), F32, kind="ExternalOutput").ap()
    build(nc, dram, out)
    r = run(nc, [arrays], core_ids=[0])
    return np.ascontiguousarray(r.results[0]["out"].transpose(1, 2, 0))
```
